# Optimizing a Trainium2 kernel written in Bass

```python
import numpy as np
import jax
import jax.numpy as jnp

def _softmax(x, axis=-1):
    return jax.nn.softmax(x, axis=axis)

def _gelu(x):
    return jax.nn.gelu(x, approximate=True)

def _silu(x):
    return jax.nn.silu(x)

def _sigmoid(x):
    return jax.nn.sigmoid(x)

def _layernorm(x, axis=-1, eps=1e-05):
    m = jnp.mean(x, axis=axis, keepdims=True)
    v = jnp.var(x, axis=axis, keepdims=True)
    return (x - m) / jnp.sqrt(v + eps)

def _scatter_add(tgt, idx, src, axis=0):
    return tgt.at[idx].add(src)

def _segment_sum(src, seg, n):
    return jax.ops.segment_sum(src, seg, n)
kernel_name = 'mk_recurrent_d2_jaxref_r8_8caf19'

def setup_inputs(seed: int=0):
    np.random.seed(seed)
    _w = jnp.asarray

    def _L0_attn_setup():
        import jax, jax.numpy as jnp
        import numpy as np
        D = 128
        H = 16
        S = 256
        B = 2
        LN_EPS = 1e-05
        key = jax.random.key(seed)
        ks = jax.random.split(key, 8)
        x = jax.random.normal(ks[0], (B, S, D), dtype=jnp.float32)
        W_w = jax.random.normal(ks[1], (3 * D, D), dtype=jnp.float32) * 0.02
        W_b = jnp.zeros((3 * D,), dtype=jnp.float32)
        proj_w = jax.random.normal(ks[2], (D, D), dtype=jnp.float32) * 0.02
        proj_b = jnp.zeros((D,), dtype=jnp.float32)
        ln_g = jnp.ones((D,), dtype=jnp.float32)
        ln_b = jnp.zeros((D,), dtype=jnp.float32)
        rpb = jax.random.normal(ks[3], (2 * S - 1, H), dtype=jnp.float32)
        return {'x': x, 'W_w': W_w, 'W_b': W_b, 'proj_w': proj_w, 'proj_b': proj_b, 'ln_g': ln_g, 'ln_b': ln_b, 'rpb': rpb}
    _L0_attn_in = _L0_attn_setup()

    def _L0_ffn_setup():
        import jax, jax.numpy as jnp
        import numpy as np
        B, T, D, DFF, E = (4, 256, 128, 512, 8)
        key = jax.random.key(seed)
        ks = jax.random.split(key, 4)
        s_in = 1.0 / np.sqrt(D)
        s_ff = 1.0 / np.sqrt(DFF)
        return {'x': jax.random.normal(ks[0], (B, T, D), dtype=jnp.float32), 'gate_W': jax.random.normal(ks[1], (D, E), dtype=jnp.float32) * s_in, 'gate_b': jnp.zeros((E,), dtype=jnp.float32), 'W1': jax.random.normal(ks[2], (E, D, DFF), dtype=jnp.float32) * s_in, 'b1': jnp.zeros((E, DFF), dtype=jnp.float32), 'W2': jax.random.normal(ks[3], (E, DFF, D), dtype=jnp.float32) * s_ff, 'b2': jnp.zeros((E, D), dtype=jnp.float32)}
    _L0_ffn_in = _L0_ffn_setup()

    def _L1_attn_setup():
        import jax, jax.numpy as jnp
        import numpy as np
        GAMMA = 0.9
        SCALE_BASE = 512.0

        def _xpos(x, downscale=False):
            B, L, D = x.shape
            half = D // 2
            scale_vec = (jnp.arange(0, D, 2, dtype=jnp.float32) + 0.4 * D) / (1.4 * D)
            power = jnp.arange(L, dtype=jnp.float32) / SCALE_BASE
            scale = scale_vec[None, :] ** power[:, None]
            if downscale:
                scale = 1.0 / scale
            inv_freq = 1.0 / 10000.0 ** (jnp.arange(half, dtype=jnp.float32) / half)
            sinusoid = jnp.arange(L, dtype=jnp.float32)[:, None] * inv_freq[None, :]
            sin = jnp.repeat(jnp.sin(sinusoid) * scale, 2, axis=-1)
            cos = jnp.repeat(jnp.cos(sinusoid) * scale, 2, axis=-1)
            x_even = x[..., 0::2]
            x_odd = x[..., 1::2]
            rot = jnp.stack((-x_odd, x_even), axis=-1).reshape(x.shape)
            return x * cos + rot * sin

        def _get_D(seq_len):
            n = jnp.arange(seq_len, dtype=jnp.float32)[:, None]
            m = jnp.arange(seq_len, dtype=jnp.float32)[None, :]
            D = GAMMA ** jnp.abs(n - m)
            return D
        key = jax.random.key(seed)
        k1, k2, k3, k4 = jax.random.split(key, 4)
        B, L, H, Dh = (8, 256, 128, 128)
        X = jax.random.normal(k1, (B, L, H), dtype=jnp.float32)
        W_Q = jax.random.normal(k2, (H, Dh), dtype=jnp.float32) / H
        W_K = jax.random.normal(k3, (H, Dh), dtype=jnp.float32) / H
        W_V = jax.random.normal(k4, (H, Dh), dtype=jnp.float32) / H
        return {'X': X, 'W_Q': W_Q, 'W_K': W_K, 'W_V': W_V}
    _L1_attn_in = _L1_attn_setup()

    def _L1_ffn_setup():
        import jax, jax.numpy as jnp
        import numpy as np
        B, S, D = (2, 256, 128)
        H = 256
        E = 8
        K = 2
        HS = 256 * 1
        SCALE = 1.0 / float(np.sqrt(D))
        key = jax.random.key(seed)
        ks = jax.random.split(key, 9)
        init = 0.02
        return {'x': jax.random.normal(ks[0], (B, S, D), dtype=jnp.float32), 'Wr': jax.random.normal(ks[1], (D, E), dtype=jnp.float32) * init, 'rb': jnp.zeros((E,), dtype=jnp.float32), 'W1': jax.random.normal(ks[2], (E, D, H), dtype=jnp.float32) * init, 'W2': jax.random.normal(ks[3], (E, H, D), dtype=jnp.float32) * init, 'W3': jax.random.normal(ks[4], (E, D, H), dtype=jnp.float32) * init, 'Ws1': jax.random.normal(ks[5], (D, HS), dtype=jnp.float32) * init, 'Ws2': jax.random.normal(ks[6], (HS, D), dtype=jnp.float32) * init, 'Ws3': jax.random.normal(ks[7], (D, HS), dtype=jnp.float32) * init}
    _L1_ffn_in = _L1_ffn_setup()
    _d = {'L0_attn_x': _L0_attn_in['x'], 'L0_attn_W_w': _L0_attn_in['W_w'], 'L0_attn_W_b': _L0_attn_in['W_b'], 'L0_attn_proj_w': _L0_attn_in['proj_w'], 'L0_attn_proj_b': _L0_attn_in['proj_b'], 'L0_attn_ln_g': _L0_attn_in['ln_g'], 'L0_attn_ln_b': _L0_attn_in['ln_b'], 'L0_attn_rpb': _L0_attn_in['rpb'], 'L0_ffn_gate_W': _L0_ffn_in['gate_W'], 'L0_ffn_gate_b': _L0_ffn_in['gate_b'], 'L0_ffn_W1': _L0_ffn_in['W1'], 'L0_ffn_b1': _L0_ffn_in['b1'], 'L0_ffn_W2': _L0_ffn_in['W2'], 'L0_ffn_b2': _L0_ffn_in['b2'], 'L1_attn_W_Q': _L1_attn_in['W_Q'], 'L1_attn_W_K': _L1_attn_in['W_K'], 'L1_attn_W_V': _L1_attn_in['W_V'], 'L1_ffn_Wr': _L1_ffn_in['Wr'], 'L1_ffn_rb': _L1_ffn_in['rb'], 'L1_ffn_W1': _L1_ffn_in['W1'], 'L1_ffn_W2': _L1_ffn_in['W2'], 'L1_ffn_W3': _L1_ffn_in['W3'], 'L1_ffn_Ws1': _L1_ffn_in['Ws1'], 'L1_ffn_Ws2': _L1_ffn_in['Ws2'], 'L1_ffn_Ws3': _L1_ffn_in['Ws3']}
    _x0 = _d['L0_attn_x']
    _d['L0_attn_x'] = jax.random.normal(jax.random.fold_in(jax.random.key(seed), 1), (16, 256, 128), dtype=_x0.dtype)
    del _x0
    return _d

def reference(L0_attn_x, L0_attn_W_w, L0_attn_W_b, L0_attn_proj_w, L0_attn_proj_b, L0_attn_ln_g, L0_attn_ln_b, L0_attn_rpb, L0_ffn_gate_W, L0_ffn_gate_b, L0_ffn_W1, L0_ffn_b1, L0_ffn_W2, L0_ffn_b2, L1_attn_W_Q, L1_attn_W_K, L1_attn_W_V, L1_ffn_Wr, L1_ffn_rb, L1_ffn_W1, L1_ffn_W2, L1_ffn_W3, L1_ffn_Ws1, L1_ffn_Ws2, L1_ffn_Ws3):

    def _L0_attn_ref(x, W_w, W_b, proj_w, proj_b, ln_g, ln_b, rpb):
        import jax, jax.numpy as jnp
        import numpy as np
        D = 128
        H = 16
        S = 256
        B = 2
        LN_EPS = 1e-05
        b, s, d = x.shape
        hd = d // H
        qkv = x @ W_w.T + W_b
        q, k, v = jnp.split(qkv, 3, axis=-1)
        q, k, v = (z.reshape(b, s, H, hd).transpose(0, 2, 1, 3) for z in (q, k, v))
        attn = jnp.einsum('bhqd,bhkd->bhqk', q, k) / jnp.sqrt(jnp.float32(d))
        causal = jnp.triu(jnp.ones((s, s), dtype=bool), k=1)
        attn = jnp.where(causal[None, None], -jnp.inf, attn)
        rel_idx = jnp.arange(s)[None, :] - jnp.arange(s)[:, None] + (s - 1)
        bias = rpb[rel_idx].transpose(2, 0, 1)
        attn = attn + bias[None]
        w = jax.nn.softmax(attn, axis=-1)
        o = jnp.einsum('bhqk,bhkd->bhqd', w, v)
        o = o.transpose(0, 2, 1, 3).reshape(b, s, d)
        out = o @ proj_w.T + proj_b
        y = x + out
        mu = jnp.mean(y, axis=-1, keepdims=True)
        var = jnp.var(y, axis=-1, keepdims=True)
        return (y - mu) / jnp.sqrt(var + LN_EPS) * ln_g + ln_b

    def _L0_ffn_ref(x, gate_W, gate_b, W1, b1, W2, b2):
        import jax, jax.numpy as jnp
        import numpy as np
        B, T, D, DFF, E = (4, 256, 128, 512, 8)
        b, t, d = x.shape
        num_experts = gate_W.shape[-1]
        logits = jnp.einsum('btd,de->bte', x, gate_W) + gate_b
        top1 = jnp.argmax(logits, axis=-1).reshape(-1)
        flat_x = x.reshape(b * t, d)
        out = jnp.zeros_like(flat_x)
        for e in range(num_experts):
            mask = (top1 == e).astype(x.dtype)[:, None]
            h = jax.nn.gelu(flat_x * mask @ W1[e] + b1[e], approximate=False)
            out = out + (h @ W2[e] + b2[e]) * mask
        return out.reshape(b, t, d)

    def _L1_attn_ref(X, W_Q, W_K, W_V):
        import jax, jax.numpy as jnp
        import numpy as np
        GAMMA = 0.9
        SCALE_BASE = 512.0

        def _xpos(x, downscale=False):
            B, L, D = x.shape
            half = D // 2
            scale_vec = (jnp.arange(0, D, 2, dtype=jnp.float32) + 0.4 * D) / (1.4 * D)
            power = jnp.arange(L, dtype=jnp.float32) / SCALE_BASE
            scale = scale_vec[None, :] ** power[:, None]
            if downscale:
                scale = 1.0 / scale
            inv_freq = 1.0 / 10000.0 ** (jnp.arange(half, dtype=jnp.float32) / half)
            sinusoid = jnp.arange(L, dtype=jnp.float32)[:, None] * inv_freq[None, :]
            sin = jnp.repeat(jnp.sin(sinusoid) * scale, 2, axis=-1)
            cos = jnp.repeat(jnp.cos(sinusoid) * scale, 2, axis=-1)
            x_even = x[..., 0::2]
            x_odd = x[..., 1::2]
            rot = jnp.stack((-x_odd, x_even), axis=-1).reshape(x.shape)
            return x * cos + rot * sin

        def _get_D(seq_len):
            n = jnp.arange(seq_len, dtype=jnp.float32)[:, None]
            m = jnp.arange(seq_len, dtype=jnp.float32)[None, :]
            D = GAMMA ** jnp.abs(n - m)
            return D
        B, L, H = X.shape
        D = _get_D(L)
        Q = _xpos(X @ W_Q)
        K = _xpos(X @ W_K, downscale=True)
        V = X @ W_V
        scores = jnp.einsum('bqd,bkd->bqk', Q, K)
        p_attn = jax.nn.softmax(scores, axis=-1)
        p_attn = p_attn * D[None, :, :]
        return jnp.einsum('bqk,bkv->bqv', p_attn, V)

    def _L1_ffn_ref(x, Wr, rb, W1, W2, W3, Ws1, Ws2, Ws3):
        import jax, jax.numpy as jnp
        import numpy as np
        B, S, D = (2, 256, 128)
        H = 256
        E = 8
        K = 2
        HS = 256 * 1
        SCALE = 1.0 / float(np.sqrt(D))
        logits = jnp.einsum('bsd,de->bse', x, Wr) * SCALE
        _, idx = jax.lax.top_k(logits + rb, K)
        gathered = jnp.take_along_axis(logits, idx, axis=-1)
        w = jax.nn.softmax(gathered, axis=-1)
        w_full = jnp.sum(jax.nn.one_hot(idx, E, dtype=x.dtype) * w[..., None], axis=-2)
        h = jnp.einsum('bsd,edh->bseh', x, W1) * jax.nn.silu(jnp.einsum('bsd,edh->bseh', x, W3))
        expert_out = jnp.einsum('bseh,ehd->bsed', h, W2)
        out = jnp.einsum('bsed,bse->bsd', expert_out, w_full)
        hs = jnp.einsum('bsd,dh->bsh', x, Ws1) * jax.nn.silu(jnp.einsum('bsd,dh->bsh', x, Ws3))
        out = out + jnp.einsum('bsh,hd->bsd', hs, Ws2)
        return out
    x = L0_attn_x
    xn = _layernorm(x, axis=-1)
    s = _L0_attn_ref(xn, L0_attn_W_w, L0_attn_W_b, L0_attn_proj_w, L0_attn_proj_b, L0_attn_ln_g, L0_attn_ln_b, L0_attn_rpb)
    g = _silu(_L0_ffn_ref(xn, L0_ffn_gate_W, L0_ffn_gate_b, L0_ffn_W1, L0_ffn_b1, L0_ffn_W2, L0_ffn_b2))
    x = x + s * g
    xn = _layernorm(x, axis=-1)
    s = _L1_attn_ref(xn, L1_attn_W_Q, L1_attn_W_K, L1_attn_W_V)
    g = _silu(_L1_ffn_ref(xn, L1_ffn_Wr, L1_ffn_rb, L1_ffn_W1, L1_ffn_W2, L1_ffn_W3, L1_ffn_Ws1, L1_ffn_Ws2, L1_ffn_Ws3))
    x = x + s * g
    return x

_drawn_inputs = setup_inputs


def setup_inputs(seed=0):
    import zlib

    import numpy as np

    out = dict(_drawn_inputs(seed))
    spreads = {'L0_attn_W_b': (0.0, 0.8),
     'L0_attn_proj_b': (0.0, 0.343),
     'L0_attn_ln_g': (1.0, 0.2),
     'L0_attn_ln_b': (0.0, 0.1),
     'L0_ffn_gate_b': (0.0, 0.1),
     'L0_ffn_b1': (0.0, 0.1),
     'L0_ffn_b2': (0.0, 0.1),
     'L1_ffn_rb': (0.0, 0.8)}
    factors = {'L0_attn_W_w': 8.0,
     'L0_attn_proj_w': 6.719,
     'L0_attn_rpb': 8.0,
     'L1_attn_W_Q': 8.0,
     'L1_attn_W_K': 8.0,
     'L1_attn_W_V': 8.0,
     'L1_ffn_Wr': 8.0,
     'L1_ffn_W1': 8.0,
     'L1_ffn_W2': 8.0,
     'L1_ffn_W3': 8.0,
     'L1_ffn_Ws1': 8.0,
     'L1_ffn_Ws2': 8.0,
     'L1_ffn_Ws3': 8.0}
    for name, (base, spread) in spreads.items():
        noise = np.random.default_rng([zlib.crc32(name.encode()), seed]).standard_normal(out[name].shape)
        drawn = base * np.exp(spread * noise) if base else spread * noise
        out[name] = jnp.asarray(drawn.astype(out[name].dtype))
    for name, factor in factors.items():
        out[name] = (out[name] * factor).astype(out[name].dtype)
    return out
```

```python
from contextlib import ExitStack

import numpy as np

import concourse.bass as bass
from concourse import mybir

F32 = mybir.dt.float32
BF16 = mybir.dt.bfloat16
I32 = mybir.dt.int32
ALU = mybir.AluOpType
ACT = mybir.ActivationFunctionType
X = mybir.AxisListType.X

P = 128
B, S = 16, 256
NT = B * S // P
GT = 4
NG = NT // GT
H, HD = 16, 8
E = 8
F0 = 512
F1 = 256
SLOTS = 256
SHARED = B * S // SLOTS
ROUTED0 = (B * S + E * (SLOTS - 1)) // SLOTS
ROUTED1 = (2 * B * S + E * (SLOTS - 1)) // SLOTS
ROUTED0 += ROUTED0 % 2
ROUTED1 += ROUTED1 % 2
TILES = SHARED + ROUTED1
LN_EPS = 1e-5
BIG = 1e30
PARTS = 3
KROWS = PARTS * PARTS * HD
MROWS = KROWS + PARTS
HALF = H // 2
SCALE0 = float(1.0 / np.sqrt(np.float32(P)))
SCALE1 = 1.0 / float(np.sqrt(P))


class Sems:

    before = None

    def __init__(self, nc, _):
        self.nc, self.stack, self.all = nc, ExitStack(), []
        self.old, Sems.before = Sems.before, self

    def __call__(self, name):
        self.all.append(self.stack.enter_context(self.nc.semaphore(name)))
        return self.all[-1]

    def pair(self, name):
        return [self(f"{name}{u}") for u in range(2)]

    def clear_old(self, sp):
        for one in self.old.all if self.old else ():
            sp.sem_clear(one)

    def done(self):
        if self.old:
            self.old.stack.close()


def build_constants(nc, R, D):
    with ExitStack() as ctx:
        sem = Sems(nc, ctx)
        ctx.callback(sem.done)
        zeros = ctx.enter_context(nc.sbuf_tensor("zeros", [P, 2048], F32))
        loaded, filled, flags, tables = sem("c_loaded"), sem("c_filled"), sem("c_flags"), sem("c_tables")
        slots_zero, bias_loaded = sem("c_slots_zero"), sem("c_bias_loaded")
        block = ctx.enter_context(nc.Block())

        loads = [(R.x[:], D["x"].rearrange("(t p) d -> p t d", p=P)),
                 (R.gate_w[0][:], D["gate_W"]), (R.gate_w[1][:], D["Wr"]),
                 (R.gb[:], bass.AP(tensor=D["gate_b"].tensor, offset=0, ap=[[0, P], [1, E]])),
                 (R.rb[:], bass.AP(tensor=D["rb"].tensor, offset=0, ap=[[0, P], [1, E]])),
                 (R.w_qkv[:], D["w_qkv"]), (R.b_qk[:], D["b_qk"]),
                 (R.b_v[:], bass.AP(tensor=D["b_v"].tensor, offset=0, ap=[[0, P], [1, P]])),
                 (R.w_proj[:], D["w_proj"]),
                 (R.b_proj[:], bass.AP(tensor=D["b_proj"].tensor, offset=0, ap=[[0, P], [1, P]])),
                 (R.ln_g[:], bass.AP(tensor=D["ln_g"].tensor, offset=0, ap=[[0, P], [1, P]])),
                 (R.ln_b[:], bass.AP(tensor=D["ln_b"].tensor, offset=0, ap=[[0, P], [1, P]])),
                 (R.w_x1[:], D["w_x1"])]

        @block.sync
        def _(sp):
            sem.clear_old(sp)
            for dst, src in loads:
                sp.dma_start(dst, src).then_inc(loaded, 16)
            sp.wait_ge(filled, 1)
            zt = zeros[:].rearrange("p (n d) -> p n d", d=P)
            n = 2048 // P
            for r in range(0, TILES * SLOTS, n * P):
                m = min(n, (TILES * SLOTS - r) // P)
                sp.dma_start(D["slots_in"][r:r + m * P, :].rearrange("(n p) d -> p n d", p=P),
                             zt[:, 0:m, :]).then_inc(slots_zero, 16)
            sp.wait_ge(slots_zero, 16 * (-(-TILES * SLOTS // (n * P))))
            sp.wait_ge(loaded, 16 * len(loads))

        @block.gpsimd
        def _(pool):
            pool.memset(zeros[:], 0.0).then_inc(filled, 1)
            pool.memset(R.ident[:], 0.0).then_inc(flags, 1)
            pool.memset(R.ones_bf[:], 1.0).then_inc(flags, 1)
            pool.memset(R.reverse[:], 0.0).then_inc(flags, 1)
            pool.memset(R.neg_half[:], -0.5).then_inc(flags, 1)
            pool.memset(R.eps[:], LN_EPS).then_inc(flags, 1)
            pool.wait_ge(flags, 5)
            pool.affine_select(out=R.ident[:], in_=R.ident[:], compare_op=ALU.not_equal, fill=1.0, base=0,
                               pattern=[[-1, P]], channel_multiplier=1).then_inc(flags, 1)
            pool.affine_select(out=R.reverse[:], in_=R.reverse[:], compare_op=ALU.not_equal, fill=1.0, base=1 - P,
                               pattern=[[1, P]], channel_multiplier=1).then_inc(flags, 1)
            pool.affine_select(out=R.upper_bf[:], in_=R.ones_bf[:], compare_op=ALU.is_gt, fill=0.0, base=0,
                               pattern=[[1, P]], channel_multiplier=-1).then_inc(flags, 1)
            pool.iota(R.expert_m8[:], [[1, E]], base=-E, channel_multiplier=0,
                      allow_small_or_imprecise_dtypes=True).then_inc(tables, 1)
            pool.iota(R.tile_start[:], [[SLOTS, S * B // SLOTS]], base=0, channel_multiplier=0,
                      allow_small_or_imprecise_dtypes=True).then_inc(tables, 1)
            pool.iota(R.tile_no[:], [[1, ROUTED1]], base=0, channel_multiplier=0,
                      allow_small_or_imprecise_dtypes=True).then_inc(tables, 1)

        @block.vector
        def _(dve):
            dve.memset(R.zero32[:], 0.0)
            dve.wait_ge(loaded, 16 * len(loads))
            dve.tensor_scalar(R.bq_neg[:], R.b_qk[:, 0:1], -SCALE0, None, ALU.mult)


def wait_if(eng, sem, value):
    if not isinstance(value, int) or value > 0:
        eng.wait_ge(sem, value)


def pairs_of_groups(eng, pair):
    pair(eng, 0)
    with eng.Fori(1, NG // 2) as j:
        pair(eng, j)


def layer_norm_gate(nc, R, D, layer):
    tag = f"n{layer}_"
    with ExitStack() as ctx:
        sem = Sems(nc, ctx)
        ctx.callback(sem.done)

        def sb(name, shape, dt=F32):
            return ctx.enter_context(nc.sbuf_tensor(tag + name, shape, dt))

        stats = [sb(f"stats{u}", [P, GT, 6]) for u in range(2)]
        mean_var = [sb(f"mean_var{u}", [P, GT, 2]) for u in range(2)]
        var_eps = [sb(f"var_eps{u}", [P, GT]) for u in range(2)]
        rstd = [sb(f"rstd{u}", [P, GT]) for u in range(2)]
        xn = [sb(f"xn{u}", [P, GT, P]) for u in range(2)]
        xt = [sb(f"xt{u}", [P, GT * P]) for u in range(2)]
        pt = [ctx.enter_context(nc.psum_tensor(f"{tag}pt{u}", [P, GT * P], F32)) for u in range(2)]
        pg = [ctx.enter_context(nc.psum_tensor(f"{tag}pg{u}", [P, 512], F32)) for u in range(2)]
        stats_ok, mv_ok, eps_ok = sem(tag + "stats_ok"), sem.pair(tag + "mv_ok"), sem.pair(tag + "eps_ok")
        rstd_ok, xn_ok = sem.pair(tag + "rstd_ok"), sem.pair(tag + "xn_ok")
        turned, xt_ok = sem.pair(tag + "turned"), sem.pair(tag + "xt_ok")
        gated, logits_ok = sem.pair(tag + "gated"), sem.pair(tag + "logits_ok")
        xn_kept, xt_kept, xn_slots = sem.pair(tag + "xn_kept"), sem.pair(tag + "xt_kept"), sem.pair(tag + "xn_slots")
        block = ctx.enter_context(nc.Block())

        @block.sync
        def _(sp):
            sem.clear_old(sp)
            def pair(sp, j):
                for u in range(2):
                    g = 2 * j + u
                    wait_if(sp, xn_ok[u], GT * (j + 1))
                    sp.dma_start(R.xn[:, bass.ds(GT * g, GT), :], xn[u][:]).then_inc(xn_kept[u], 16)
                    if layer == 1:
                        sp.dma_start(D["slots_in"][bass.ds(GT * P * g, GT * P), :].rearrange(
                            "(t p) d -> p t d", p=P), xn[u][:]).then_inc(xn_slots[u], 16)
                    wait_if(sp, xt_ok[u], j + 1)
                    sp.dma_start(R.xt[:, bass.ds(GT * P * g, GT * P)], xt[u][:]).then_inc(xt_kept[u], 16)
            pairs_of_groups(sp, pair)
            for u in range(2):
                sp.wait_ge(xn_kept[u], 16 * (NG // 2))
                sp.wait_ge(xt_kept[u], 16 * (NG // 2))
                if layer == 1:
                    sp.wait_ge(xn_slots[u], 16 * (NG // 2))

        @block.vector
        def _(dve):
            def pair(dve, j):
                for u in range(2):
                    g = 2 * j + u
                    for k in range(GT):
                        if u and k == GT - 1:
                            dve.wait_ge(stats_ok, 2 * GT * j + GT)
                        dve.bn_stats(stats[u][:, k, :], R.x[:, GT * g + k, :]).then_inc(stats_ok, 1)
                for k in range(GT):
                    dve.bn_aggr(mean_var[0][:, k, :], stats[0][:, k, :]).then_inc(mv_ok[0], 1)
                for u in range(2):
                    g = 2 * j + u
                    wait_if(dve, rstd_ok[u], j + 1)
                    wait_if(dve, turned[u], j)
                    wait_if(dve, xn_kept[u], 16 * j)
                    if layer == 1:
                        wait_if(dve, xn_slots[u], 16 * j)
                    if u == 0:
                        dve.wait_ge(stats_ok, 2 * GT * j + 2 * GT)
                    for k in range(GT):
                        dve.tensor_scalar(xn[u][:, k, :], R.x[:, GT * g + k, :], mean_var[u][:, k, 0:1],
                                          rstd[u][:, k:k + 1], ALU.subtract, ALU.mult).then_inc(xn_ok[u], 1)
                        if u == 0:
                            dve.bn_aggr(mean_var[1][:, k, :], stats[1][:, k, :]).then_inc(mv_ok[1], 1)
                for u in range(2):
                    g = 2 * j + u
                    wait_if(dve, gated[u], j + 1)
                    got = pg[u][:, 0:GT * E].rearrange("p (k e) -> p k e", e=E)
                    if layer == 0:
                        dve.tensor_tensor(R.logits[:, bass.ds(GT * g, GT), :], got,
                                          R.gb[:].unsqueeze(1).to_broadcast([P, GT, E]), ALU.add
                                          ).then_inc(logits_ok[u], 1)
                    else:
                        dve.tensor_scalar(R.logits[:, bass.ds(GT * g, GT), :], got, SCALE1, None, ALU.mult
                                          ).then_inc(logits_ok[u], 1)
            pairs_of_groups(dve, pair)

        @block.gpsimd
        def _(pool):
            def pair(pool, j):
                for u in range(2):
                    wait_if(pool, mv_ok[u], GT * (j + 1))
                    pool.tensor_tensor(var_eps[u][:], mean_var[u][:, :, 1], R.eps[:], ALU.add
                                       ).then_inc(eps_ok[u], 1)
                    wait_if(pool, eps_ok[u], j + 1)
                    wait_if(pool, xn_ok[u], GT * j)
                    pool.tensor_tensor(rstd[u][:], var_eps[u][:], R.neg_half[:, 0:GT], ALU.pow
                                       ).then_inc(rstd_ok[u], 1)
            pairs_of_groups(pool, pair)

        @block.tensor
        def _(pe):
            def pair(pe, j):
                for u in range(2):
                    wait_if(pe, xt_ok[u], j)
                    for k in range(GT):
                        wait_if(pe, xn_ok[u], GT * j + k + 1)
                        mm = pe.transpose(pt[u][:, k * P:(k + 1) * P], xn[u][:, k, :], R.ident[:])
                    mm.then_inc(turned[u], 1)
                for u in range(2):
                    wait_if(pe, xt_ok[u], j + 1)
                    wait_if(pe, logits_ok[u], j)
                    for k in range(GT):
                        mm = pe.matmul(pg[u][:, k * E:(k + 1) * E], xt[u][:, k * P:(k + 1) * P],
                                       R.gate_w[layer][:], start=True, stop=True)
                    mm.then_inc(gated[u], 1)
            pairs_of_groups(pe, pair)

        @block.scalar
        def _(act):
            def pair(act, j):
                for u in range(2):
                    wait_if(act, turned[u], j + 1)
                    wait_if(act, gated[u], j)
                    wait_if(act, xt_kept[u], 16 * j)
                    act.activation(xt[u][:], pt[u][:], ACT.Copy).then_inc(xt_ok[u], 1)
            pairs_of_groups(act, pair)


def route(nc, R, D, layer):
    tag = f"r{layer}_"
    tops = 1 + layer
    routed = (ROUTED0, ROUTED1)[layer]
    with ExitStack() as ctx:
        sem = Sems(nc, ctx)
        ctx.callback(sem.done)

        def sb(name, shape, dt=F32):
            return ctx.enter_context(nc.sbuf_tensor(tag + name, shape, dt))

        best, first = sb("best", [P, NT]), sb("first", [P, NT])
        hit = sb("hit", [P, NT, E])
        pick = [sb(f"pick{n}", [P, NT, E]) for n in range(tops)]
        chosen = sb("chosen", [P, NT, E])
        sel = sb("sel", [P, NT, E])
        mask_bf = sb("mask_bf", [P, E, NT], BF16)
        count, upto, slot = sb("count", [P, E, NT]), sb("upto", [P, E, NT]), sb("slot", [P, E, NT])
        over = sb("over", [P, E, B * S // SLOTS])
        tiles, last, start = sb("tiles", [P, E]), sb("last", [P, E]), sb("start", [P, E])
        before = sb("before", [P, ROUTED1, E])
        owner = sb("owner", [P, ROUTED1])
        pos_f = sb("pos_f", [P, NT])
        top_logit = [sb(f"top_logit{n}", [P, NT]) for n in range(tops)]
        prank = ctx.enter_context(nc.psum_tensor(tag + "prank", [P, 512], F32))
        pcount = ctx.enter_context(nc.psum_tensor(tag + "pcount", [P, 512], F32))
        steps, mask_ok, ranked = sem(tag + "steps"), sem(tag + "mask_ok"), sem(tag + "ranked")
        pos_ok, scattered, exps = sem(tag + "pos_ok"), sem(tag + "scattered"), sem(tag + "exps")
        diff_ok = sem(tag + "diff_ok")
        block = ctx.enter_context(nc.Block())
        per_tile = [P, NT, E]

        @block.vector
        def _(dve):
            done = [0]

            def step(ins):
                done[0] += 1
                ins.then_inc(steps, 1)
                dve.wait_ge(steps, done[0])

            em8 = R.expert_m8[:].unsqueeze(1).to_broadcast(per_tile)

            def one_hot(out, logits):
                step(dve.tensor_reduce(best[:], logits, X, ALU.max))
                step(dve.tensor_tensor(hit[:], logits, best[:].unsqueeze(2).to_broadcast(per_tile), ALU.is_equal))
                step(dve.tensor_tensor(hit[:], hit[:], em8, ALU.mult))
                step(dve.tensor_reduce(first[:], hit[:], X, ALU.min))
                step(dve.tensor_tensor(out[:], em8, first[:].unsqueeze(2).to_broadcast(per_tile), ALU.is_equal))

            def logit_of(out, chose):
                step(dve.tensor_tensor(hit[:], R.logits[:], chose[:], ALU.mult))
                step(dve.tensor_reduce(out[:], hit[:], X, ALU.add))

            if layer == 0:
                one_hot(pick[0], R.logits[:])
                marked = pick[0]
            else:
                step(dve.tensor_tensor(sel[:], R.logits[:], R.rb[:].unsqueeze(1).to_broadcast(per_tile), ALU.add))
                one_hot(pick[0], sel[:])
                step(dve.scalar_tensor_tensor(out=sel[:], in0=pick[0][:], scalar=-BIG, in1=sel[:],
                                              op0=ALU.mult, op1=ALU.add))
                one_hot(pick[1], sel[:])
                step(dve.tensor_tensor(chosen[:], pick[0][:], pick[1][:], ALU.add))
                marked = chosen
            dve.tensor_copy(mask_bf[:].rearrange("p e t -> p t e"), marked[:]).then_inc(mask_ok, 1)
            if layer == 1:
                for n in range(2):
                    logit_of(top_logit[n], pick[n])
                step(dve.tensor_tensor(best[:], top_logit[0][:], top_logit[1][:], ALU.max))
                for n in range(2):
                    ins = dve.tensor_tensor(top_logit[n][:], top_logit[n][:], best[:], ALU.subtract)
                    ins.then_inc(diff_ok, 1)
                dve.wait_ge(exps, 2)
                step(dve.tensor_tensor(first[:], R.weight[0][:], R.weight[1][:], ALU.add))
                step(dve.reciprocal(best[:], first[:]))
                for n in range(2):
                    step(dve.tensor_tensor(R.weight[n][:], R.weight[n][:], best[:], ALU.mult))
            dve.wait_ge(ranked, 1)
            step(dve.tensor_copy(count[:].rearrange("p e t -> p (e t)"), pcount[:, 0:E * NT]))
            for e in range(E):
                ins = dve.tensor_tensor_scan(upto[:, e, :], count[:, e, :], R.zero32[:], 0.0, ALU.add, ALU.add)
                step(ins)
            step(dve.tensor_tensor(over[:], upto[:, :, NT - 1:NT].to_broadcast([P, E, B * S // SLOTS]),
                                   R.tile_start[:].unsqueeze(1).to_broadcast([P, E, B * S // SLOTS]), ALU.is_gt))
            step(dve.tensor_reduce(tiles[:], over[:], X, ALU.add))
            step(dve.tensor_tensor_scan(last[:], tiles[:], R.zero32[:, 0:E], 0.0, ALU.add, ALU.add))
            step(dve.tensor_tensor(start[:], last[:], tiles[:], ALU.subtract))
            step(dve.tensor_scalar(start[:], start[:], float(SLOTS), float(SHARED * SLOTS * layer), ALU.mult, ALU.add))
            step(dve.tensor_tensor(slot[:], prank[:, 0:E * NT].rearrange("p (e t) -> p e t", e=E), upto[:], ALU.add))
            step(dve.tensor_tensor(slot[:], slot[:], count[:], ALU.subtract))
            step(dve.tensor_tensor(slot[:], slot[:], start[:].unsqueeze(2).to_broadcast([P, E, NT]), ALU.add))
            for n in range(tops):
                step(dve.tensor_tensor(hit[:], slot[:].rearrange("p e t -> p t e"), pick[n][:], ALU.mult))
                step(dve.tensor_reduce(pos_f[:], hit[:], X, ALU.add))
                step(dve.tensor_copy(R.pos[n][:], pos_f[:]))
            step(dve.tensor_tensor(before[:], R.tile_no[:].unsqueeze(2).to_broadcast([P, ROUTED1, E]),
                                   last[:].unsqueeze(1).to_broadcast([P, ROUTED1, E]), ALU.is_ge))
            step(dve.tensor_reduce(owner[:], before[:], X, ALU.add))
            step(dve.tensor_scalar(owner[:], owner[:], float(E - 1), None, ALU.min))
            at = SHARED if layer else 0
            step(dve.tensor_copy(R.tile_expert[0:1, at:at + routed], owner[0:1, 0:routed]))
            if layer == 1:
                step(dve.memset(R.tile_expert[0:1, 0:SHARED], E))

        @block.sync
        def _(sp):
            sem.clear_old(sp)

        @block.scalar
        def _(act):
            if layer == 1:
                for n in range(2):
                    act.wait_ge(diff_ok, n + 1)
                    act.activation(R.weight[n][:], top_logit[n][:], ACT.Exp).then_inc(exps, 1)

        @block.tensor
        def _(pe):
            pe.wait_ge(mask_ok, 1)
            flat = mask_bf[:].rearrange("p e t -> p (e t)")
            pe.matmul(prank[:, 0:E * NT], R.upper_bf[:], flat, start=True, stop=True)
            pe.matmul(pcount[:, 0:E * NT], R.ones_bf[:], flat, start=True, stop=True).then_inc(ranked, 1)

    with ExitStack() as ctx:
        sem = Sems(nc, ctx)
        ctx.callback(sem.done)
        scattered = R.scattered
        block = ctx.enter_context(nc.Block())

        @block.sync
        def _(sp):
            sem.clear_old(sp)

        @block.gpsimd
        def _(pool):
            for t in range(NT):
                for n in range(tops):
                    pool.indirect_dma_start(D["slots_in"], bass.IndirectOffsetOnAxis(ap=R.pos[n][:, t:t + 1], axis=0),
                                            R.xn[:, t, :], None).then_inc(scattered, 16)
            pool.wait_ge(scattered, 16 * NT * tops + 16 * NT * layer)


def experts(nc, R, D, layer):
    tag = f"e{layer}_"
    tiles = (ROUTED0, TILES)[layer]
    C = (F0, F1)[layer] // P
    with ExitStack() as ctx:
        sem = Sems(nc, ctx)
        ctx.callback(sem.done)

        def sb(name, shape, dt=F32):
            return [ctx.enter_context(nc.sbuf_tensor(f"{tag}{name}{u}", shape, dt)) for u in range(2)]

        w_up, w_down = sb("w_up", [P, 4, P]), sb("w_down", [P, C, P])
        x_in, x_t = sb("x_in", [P, 2, P]), sb("x_t", [P, SLOTS])
        hid = sb("hid", [P, C, SLOTS])
        pre = sb("pre", [P, C, SLOTS])
        y_out = sb("y_out", [P, 2, P])
        b_up = sb("b_up", [P, 4]) if layer == 0 else None
        b_down = sb("b_down", [P, P]) if layer == 0 else None
        loads = 5 if layer == 0 else 4
        pt = ctx.enter_context(nc.psum_tensor(tag + "pt", [P, 512], F32))
        ph = [[ctx.enter_context(nc.psum_tensor(f"{tag}ph{u}{n}", [P, 2, SLOTS], F32)) for n in range(2)]
              for u in range(2)]
        py = [ctx.enter_context(nc.psum_tensor(f"{tag}py{u}", [P, 512], F32)) for u in range(2)]
        in_ok, turned, x_ok = sem.pair(tag + "in_ok"), sem.pair(tag + "turned"), sem.pair(tag + "x_ok")
        up_ok, pre_ok, hid_ok = sem.pair(tag + "up_ok"), sem.pair(tag + "pre_ok"), sem.pair(tag + "hid_ok")
        down_ok, y_ok = sem.pair(tag + "down_ok"), sem.pair(tag + "y_ok")
        stored, stored0 = R.stored, 16 * (ROUTED0 // 2) * layer
        block = ctx.enter_context(nc.Block())
        pairs = tiles // 2

        @block.sync
        def _(sp):
            sem.clear_old(sp)
            def pair(sp, j):
                for u in range(2):
                    i = 2 * j + u
                    e = sp.value_load(R.tile_expert[0:1, bass.ds(i, 1)], min_val=0, max_val=E - 1 + layer)
                    wait_if(sp, down_ok[u], j)
                    sp.dma_start(x_in[u][:], D["slots_in"][bass.ds(SLOTS * i, SLOTS), :].rearrange(
                        "(t p) d -> p t d", p=P)).then_inc(in_ok[u], 16)
                    if layer == 0:
                        sp.dma_start(w_up[u][:].rearrange("p c m -> p (c m)"), D["W1"][e, :, :]).then_inc(in_ok[u], 16)
                        wait_if(sp, y_ok[u], 2 * j)
                        sp.dma_start(b_up[u][:], D["b1T"][e, :, :]).then_inc(in_ok[u], 16)
                        sp.dma_start(b_down[u][:], D["b2"][bass.ds(e, 1), :].to_broadcast([P, P])).then_inc(in_ok[u], 16)
                        sp.dma_start(w_down[u][:], D["W2"][e, :, :].rearrange("(c p) m -> p c m", p=P)
                                     ).then_inc(in_ok[u], 16)
                    else:
                        sp.dma_start(w_up[u][:, 0:2, :].rearrange("p c m -> p (c m)"), D["M1"][e, :, :]
                                     ).then_inc(in_ok[u], 16)
                        sp.dma_start(w_up[u][:, 2:4, :].rearrange("p c m -> p (c m)"), D["M3"][e, :, :]
                                     ).then_inc(in_ok[u], 16)
                        sp.dma_start(w_down[u][:], D["M2"][e, :, :].rearrange("(c p) m -> p c m", p=P)
                                     ).then_inc(in_ok[u], 16)
            pair(sp, 0)
            with sp.Fori(1, pairs) as j:
                pair(sp, j)

        @block.gpsimd
        def _(pool):
            with pool.Fori(0, pairs) as j:
                for u in range(2):
                    i = 2 * j + u
                    wait_if(pool, y_ok[u], 2 * (j + 1))
                    pool.dma_start(D["slots_out"][layer][bass.ds(SLOTS * i, SLOTS), :].rearrange(
                        "(t p) d -> p t d", p=P), y_out[u][:]).then_inc(stored[u], 16)
            for u in range(2):
                pool.wait_ge(stored[u], 16 * pairs + stored0)

        def up(pe, u, j):
            wait_if(pe, in_ok[u], 16 * loads * (j + 1))
            for k in range(2):
                mm = pe.transpose(pt[:, k * P:(k + 1) * P], x_in[u][:, k, :], R.ident[:])
            mm.then_inc(turned[u], 1)
            wait_if(pe, x_ok[u], j + 1)
            wait_if(pe, pre_ok[u], 2 * j)
            wait_if(pe, hid_ok[u], 2 * j)
            for c in range(4):
                mm = pe.matmul(ph[u][c // 2][:, c % 2, :], w_up[u][:, c, :], x_t[u][:], start=True, stop=True)
                if c % 2:
                    mm.then_inc(up_ok[u], 1)

        def down(pe, u, j):
            wait_if(pe, y_ok[u], 2 * j)
            wait_if(pe, hid_ok[u], 2 * (j + 1))
            for k in range(2):
                for c in range(C):
                    mm = pe.matmul(py[u][:, k * P:(k + 1) * P], hid[u][:, c, k * P:(k + 1) * P],
                                   w_down[u][:, c, :], start=(c == 0), stop=(c == C - 1))
            mm.then_inc(down_ok[u], 1)

        @block.tensor
        def _(pe):
            def pair(pe, j):
                up(pe, 1, j)
                down(pe, 0, j)
                up(pe, 0, j + 1)
                down(pe, 1, j)

            up(pe, 0, 0)
            pair(pe, 0)
            with pe.Fori(1, pairs - 1) as j:
                pair(pe, j)
            up(pe, 1, pairs - 1)
            down(pe, 0, pairs - 1)
            down(pe, 1, pairs - 1)

        def x_copy(act, u, j):
            wait_if(act, turned[u], j + 1)
            wait_if(act, up_ok[u], 2 * j)
            act.activation(x_t[u][:], pt[:, 0:SLOTS], ACT.Copy).then_inc(x_ok[u], 1)

        def act_fn(act, u, j):
            for n in range(2 if layer == 0 else 1):
                if layer == 0:
                    wait_if(act, pre_ok[u], 2 * j + n + 1)
                    wait_if(act, down_ok[u], j)
                    act.activation(hid[u][:, 2 * n:2 * n + 2, :], pre[u][:, 2 * n:2 * n + 2, :], ACT.Gelu
                                   ).then_inc(hid_ok[u], 1)
                else:
                    wait_if(act, up_ok[u], 2 * (j + 1))
                    wait_if(act, hid_ok[u], 2 * j)
                    act.activation(pre[u][:], ph[u][1][:], ACT.Silu).then_inc(pre_ok[u], 2)

        @block.scalar
        def _(act):
            def pair(act, j):
                x_copy(act, 1, j)
                act_fn(act, 0, j)
                x_copy(act, 0, j + 1)
                act_fn(act, 1, j)

            x_copy(act, 0, 0)
            pair(act, 0)
            with act.Fori(1, pairs - 1) as j:
                pair(act, j)
            x_copy(act, 1, pairs - 1)
            act_fn(act, 0, pairs - 1)
            act_fn(act, 1, pairs - 1)

        def vector_up(dve, u, j):
            if layer == 0:
                wait_if(dve, in_ok[u], 16 * loads * (j + 1))
                for n in range(2):
                    wait_if(dve, up_ok[u], 2 * j + n + 1)
                    wait_if(dve, hid_ok[u], 2 * j)
                    dve.tensor_tensor(pre[u][:, 2 * n:2 * n + 2, :], ph[u][n][:],
                                      b_up[u][:, 2 * n:2 * n + 2].unsqueeze(2).to_broadcast([P, 2, SLOTS]),
                                      ALU.add).then_inc(pre_ok[u], 1)
            else:
                wait_if(dve, pre_ok[u], 2 * (j + 1))
                wait_if(dve, down_ok[u], j)
                dve.tensor_tensor(hid[u][:], ph[u][0][:], pre[u][:], ALU.mult).then_inc(hid_ok[u], 2)

        def vector_down(dve, u, j):
            wait_if(dve, down_ok[u], j + 1)
            wait_if(dve, stored[u], 16 * j + stored0)
            got = py[u][:, 0:2 * P].rearrange("p (k d) -> p k d", k=2)
            if layer == 0:
                dve.tensor_tensor(y_out[u][:], got, b_down[u][:].unsqueeze(1).to_broadcast([P, 2, P]), ALU.add
                                  ).then_inc(y_ok[u], 2)
            else:
                dve.tensor_copy(y_out[u][:], got).then_inc(y_ok[u], 2)

        @block.vector
        def _(dve):
            def pair(dve, j):
                vector_up(dve, 1, j)
                vector_down(dve, 0, j)
                vector_up(dve, 0, j + 1)
                vector_down(dve, 1, j)

            vector_up(dve, 0, 0)
            pair(dve, 0)
            with dve.Fori(1, pairs - 1) as j:
                pair(dve, j)
            vector_up(dve, 1, pairs - 1)
            vector_down(dve, 0, pairs - 1)
            vector_down(dve, 1, pairs - 1)


def combine(nc, R, D, layer):
    tag = f"m{layer}_"
    tops = 1 + layer
    with ExitStack() as ctx:
        sem = Sems(nc, ctx)
        ctx.callback(sem.done)
        ring = 4

        def sb(name, shape, dt=F32):
            return ctx.enter_context(nc.sbuf_tensor(tag + name, shape, dt))

        f = [[sb(f"f{n}{r}", [P, P]) for r in range(ring)] for n in range(tops)]
        fs = [sb(f"fs{r}", [P, P]) for r in range(ring)]
        mixed = [sb(f"mixed{r}", [P, P]) for r in range(ring)]
        gate = [sb(f"gate{r}", [P, P]) for r in range(ring)]
        prod = [sb(f"prod{r}", [P, P]) for r in range(ring)]
        arrived, arrived0 = R.arrived, 16 * (NT // ring) * layer
        shared_in = [sem(f"{tag}shared_in{r}") for r in range(ring)]
        first_ok, mixed_ok, gate_ok = sem(tag + "first_ok"), sem(tag + "mixed_ok"), sem(tag + "gate_ok")
        prod_ok, x_ok, out_done = sem(tag + "prod_ok"), sem(tag + "x_ok"), sem(tag + "out_done")
        block = ctx.enter_context(nc.Block())

        @block.gpsimd
        def _(pool):
            for t in range(NT):
                r = t % ring
                if t >= ring:
                    pool.wait_ge(mixed_ok if layer else gate_ok, t - ring + 1)
                for n in range(tops):
                    pool.indirect_dma_start(f[n][r][:], None, D["slots_out"][layer],
                                            bass.IndirectOffsetOnAxis(ap=R.pos[n][:, t:t + 1], axis=0)
                                            ).then_inc(arrived[r], 16)

        @block.sync
        def _(sp):
            sem.clear_old(sp)
            if layer == 1:
                for t in range(NT):
                    r = t % ring
                    if t >= ring:
                        sp.wait_ge(mixed_ok, t - ring + 1)
                    sp.dma_start(fs[r][:], D["slots_out"][layer][t * P:(t + 1) * P, :]).then_inc(shared_in[r], 16)
                for g in range(NG):
                    sp.wait_ge(x_ok, GT * (g + 1))
                    sp.dma_start(D["out"][GT * P * g:GT * P * (g + 1), :].rearrange("(t p) d -> p t d", p=P),
                                 R.x[:, GT * g:GT * (g + 1), :]).then_inc(out_done, 16)
                sp.wait_ge(out_done, 16 * NG)

        @block.scalar
        def _(act):
            for t in range(NT):
                r = t % ring
                if layer == 0:
                    act.wait_ge(arrived[r], 16 * (t // ring + 1))
                else:
                    act.wait_ge(mixed_ok, t + 1)
                if t >= ring:
                    act.wait_ge(prod_ok, t - ring + 1)
                act.activation(gate[r][:], (mixed if layer else f[0])[r][:], ACT.Silu).then_inc(gate_ok, 1)

        @block.vector
        def _(dve):
            def mix(t):
                r = t % ring
                dve.wait_ge(arrived[r], 32 * (t // ring + 1) + arrived0)
                dve.wait_ge(shared_in[r], 16 * (t // ring + 1))
                dve.scalar_tensor_tensor(out=fs[r][:], in0=f[0][r][:], scalar=R.weight[0][:, t:t + 1], in1=fs[r][:],
                                         op0=ALU.mult, op1=ALU.add).then_inc(first_ok, 1)
                if t >= ring:
                    dve.wait_ge(gate_ok, t - ring + 1)
                dve.wait_ge(first_ok, t + 1)
                dve.scalar_tensor_tensor(out=mixed[r][:], in0=f[1][r][:], scalar=R.weight[1][:, t:t + 1],
                                         in1=fs[r][:], op0=ALU.mult, op1=ALU.add).then_inc(mixed_ok, 1)

            def add(t):
                r = t % ring
                dve.wait_ge(gate_ok, t + 1)
                if t >= ring:
                    dve.wait_ge(x_ok, t - ring + 1)
                dve.tensor_tensor(prod[r][:], R.s[:, t, :], gate[r][:], ALU.mult).then_inc(prod_ok, 1)
                dve.wait_ge(prod_ok, t + 1)
                dve.tensor_tensor(R.x[:, t, :], R.x[:, t, :], prod[r][:], ALU.add).then_inc(x_ok, 1)

            for t in range(NT):
                if layer == 1:
                    mix(t)
                    if t:
                        add(t - 1)
                else:
                    add(t)
            if layer == 1:
                add(NT - 1)


class Batch:

    def __init__(self, j, c):
        self.u, self.half, self.n = c % 2, j + c // 2, 2 * j + c

    def after(self, k):
        return k * self.n


def attention0(nc, R, D):
    tag = "a0_"
    with ExitStack() as ctx:
        sem = Sems(nc, ctx)
        ctx.callback(sem.done)

        def sb(name, shape, dt=F32):
            return ctx.enter_context(nc.sbuf_tensor(tag + name, shape, dt))

        def ps(name):
            return ctx.enter_context(nc.psum_tensor(tag + name, [P, 512], F32))

        bias_q = sb("bias_q", [P, H, S])
        bias_k = sb("bias_k", [P, H, S + P])
        xs = [sb(f"xs{u}", [P, S]) for u in range(2)]
        qk = sb("qk", [P, 2 * S])
        rest = sb("rest", [P, 2 * S])
        part = [sb(f"part{u}", [P, 3, 2 * S], BF16) for u in range(2)]
        qst = [sb(f"qst{u}", [MROWS, H, S], BF16) for u in range(2)]
        kst = [sb(f"kst{u}", [MROWS, H, S], BF16) for u in range(2)]
        va = [sb(f"va{u}", [P, 2, H, HD + 1]) for u in range(2)]
        sums = [sb(f"sums{r}", [P, S], BF16) for r in range(4)]
        neg_max = [sb(f"neg_max{u}", [P, H, 2]) for u in range(2)]
        max_f = [sb(f"max_f{f}", [H, P]) for f in range(2)]
        max_rest = [sb(f"max_rest{f}", [H, P]) for f in range(2)]
        max_part = [sb(f"max_part{f}", [H, 3, P], BF16) for f in range(2)]
        arg = [sb(f"arg{r}", [P, S + P]) for r in range(4)]
        prob = [sb(f"prob{r}", [P, S + P]) for r in range(4)]
        rden = sb("rden", [P, 2, H])
        o_sb = sb("o_sb", [P, 2, P])
        o_t = sb("o_t", [P, S])
        resid = sb("resid", [P, 2, P])
        y = sb("y", [P, 2, P])
        stats, mean_var = sb("stats", [P, 2, 6]), sb("mean_var", [P, 2, 2])
        var_eps, rstd = sb("var_eps", [P, 2]), sb("rstd", [P, 2])
        yn, yg = sb("yn", [P, 2, P]), sb("yg", [P, 2, P])
        p_qk, p_misc = ps("p_qk"), ps("p_misc")
        p_s = [ps(f"p_s{r}") for r in range(2)]
        p_t = [ps(f"p_t{r}") for r in range(2)]
        p_o = [ps(f"p_o{u}") for u in range(2)]

        s = {n: sem(tag + n) for n in (
            "bias_in", "bias_turned", "bias_neg", "bias_ok", "ones_ok", "rows_ok", "qk_mm", "qk_ok", "part1", "part2", "part3", "rest_ok",
            "v_mm", "v_ok", "scored", "max_ok", "max_turned", "max_read", "max_diff", "max_p2", "max_p3",
            "scored_t", "arg_ok", "prob_ok", "summed", "rden_ok", "o_ok", "o_turned", "o_t_ok", "projected",
            "resid_ok", "y_ok", "stats_ok", "mv_ok", "eps_ok", "rstd_ok", "yn_ok", "yg_ok", "s_ok")}
        xs_in, spilled = sem.pair(tag + "xs_in"), sem.pair(tag + "spilled")
        stacked = [[sem(f"{tag}stacked{u}{f}") for f in range(2)] for u in range(2)]
        max_in = [[sem(f"{tag}max_in{u}{f}") for f in range(2)] for u in range(2)]
        block = ctx.enter_context(nc.Block())

        def bank_o(u):
            return p_o[u][:, 0:2 * H * (HD + 1)].rearrange("p (t h d) -> p t h d", t=2, h=H)

        def steps(eng, do):
            do(eng, 0, 0)
            do(eng, 0, 1)
            with eng.Fori(1, B // 2 - 1) as j:
                do(eng, j, 0)
                do(eng, j, 1)
            do(eng, 0, B - 2)
            do(eng, 0, B - 1)

        def bias_pieces():
            return [bias_q[:, h:h + 2, :] for h in range(0, H, 2)] + [bias_k[:, h:h + 2, 0:S] for h in range(0, H, 2)]

        def has(j, c, ahead):
            return not isinstance(j, int) or 0 <= c + ahead < B

        def stage_x(sp, b):
            if not isinstance(b.n, int) or b.n >= 2:
                sp.wait_ge(s["v_mm"], b.n - 1)
            sp.dma_start(xs[b.u][:], R.xt[:, bass.ds(S * b.n, S)]).then_inc(xs_in[b.u], 16)

        def spill(sp, b):
            for name in ("part1", "part2", "part3"):
                sp.wait_ge(s[name], b.n + 1)
            for f in range(2):
                wait_if(sp, stacked[b.u][f], 64 * b.half)
                for k in range(2):
                    dst = bass.AP(tensor=D["parts"].tensor, offset=at_parts(b, k, f),
                                  ap=[[S, P // 2], [P // 2 * S, PARTS], [1, S]])
                    sp.dma_start(dst, part[b.u][P // 2 * f:P // 2 * (f + 1), :, k * S:(k + 1) * S]
                                 ).then_inc(spilled[b.u], 16)

        def at_parts(b, k, f):
            return ((b.u * 2 + k) * 2 + f) * PARTS * P // 2 * S

        def stack(sp, b, f):
            wait_if(sp, s["scored_t"], H * (b.n - 2) + HALF * (f + 1))
            sp.wait_ge(spilled[b.u], 64 * (b.half + 1))
            heads = slice(HALF * f, HALF * (f + 1))
            src = bass.AP(tensor=D["parts"].tensor, offset=at_parts(b, 1, f),
                          ap=[[0, PARTS], [HALF * S, PARTS * HD], [1, HALF * S]])
            sp.dma_start(kst[b.u][0:KROWS, heads, :], src).then_inc(stacked[b.u][f], 16)
            for i in range(PARTS):
                src = bass.AP(tensor=D["parts"].tensor, offset=at_parts(b, 0, f) + i * P // 2 * S,
                              ap=[[0, PARTS], [HALF * S, HD], [1, HALF * S]])
                sp.dma_start(qst[b.u][PARTS * HD * i:PARTS * HD * (i + 1), heads, :], src
                             ).then_inc(stacked[b.u][f], 16)

        def stack_max(sp, b, f):
            sp.wait_ge(s["max_read"], 2 * (2 * b.n + f + 1))
            sp.wait_ge(s["max_p2"], 2 * b.n + f + 1)
            sp.wait_ge(s["max_p3"], 2 * b.n + f + 1)
            for i in range(3):
                sp.dma_start(qst[b.u][KROWS + i:KROWS + i + 1, HALF * f:HALF * (f + 1), :],
                             max_part[f][:, i, :]).then_inc(max_in[b.u][f], 16)

        @block.sync
        def _(sp):
            sem.clear_old(sp)
            sp.dma_start(bias_q[:], bass.AP(tensor=D["rpbT"].tensor, offset=0,
                                            ap=[[1, P], [2 * S - 1, H], [1, S]])).then_inc(s["bias_in"], 16)
            sp.dma_start(bias_k[:, :, 0:S], bass.AP(tensor=D["rpbR"].tensor, offset=P,
                                                    ap=[[1, P], [2 * S - 1, H], [1, S]])).then_inc(s["bias_in"], 16)
            stage_x(sp, Batch(0, 0))
            stage_x(sp, Batch(0, 1))
            sp.wait_ge(s["rows_ok"], 2)
            for b in (Batch(0, 0), Batch(0, 1)):
                spill(sp, b)
                stack(sp, b, 0)
                stack(sp, b, 1)
            stack_max(sp, Batch(0, 0), 0)

            def step(sp, j, c):
                b = Batch(j, c)
                if has(j, c, 2):
                    stage_x(sp, Batch(j, c + 2))
                stack_max(sp, b, 1)
                if has(j, c, 2):
                    spill(sp, Batch(j, c + 2))
                    stack(sp, Batch(j, c + 2), 0)
                if has(j, c, 1):
                    stack_max(sp, Batch(j, c + 1), 0)
                if has(j, c, 2):
                    stack(sp, Batch(j, c + 2), 1)
            steps(sp, step)

        def project(pe, b):
            pe.wait_ge(xs_in[b.u], 16 * (b.half + 1))
            wait_if(pe, s["qk_ok"], 2 * b.n)
            pe.matmul(p_qk[:, 0:S], R.w_qkv[:, 0:P], xs[b.u][:], start=True, stop=True)
            pe.matmul(p_qk[:, S:2 * S], R.w_qkv[:, P:2 * P], xs[b.u][:], start=True, stop=True
                      ).then_inc(s["qk_mm"], 1)

        def values(pe, b):
            for k in range(2):
                mm = pe.matmul(p_misc[:, k * P:(k + 1) * P], xs[b.u][:, k * P:(k + 1) * P],
                               R.w_qkv[:, 2 * P:3 * P], start=True, stop=True)
            mm.then_inc(s["v_mm"], 1)

        def score(pe, b, h):
            n = H * b.n + h
            if h % HALF == 0:
                pe.wait_ge(stacked[b.u][h // HALF], 64 * (b.half + 1))
            wait_if(pe, s["max_ok"], 2 * (n - 1))
            q, k = qst[b.u][0:KROWS, h, :], kst[b.u][0:KROWS, h, :]
            pe.matmul(p_s[h % 2][:, 0:S], q[:, P:S], k, start=True, stop=True)
            pe.matmul(p_s[h % 2][:, S:S + P], q[:, 0:P], k[:, 0:P], start=True, stop=True).then_inc(s["scored"], 1)

        def turn_max(pe, b, f):
            pe.wait_ge(s["max_ok"], 2 * H * b.n + H * (f + 1))
            flat = neg_max[b.u][:].rearrange("p h t -> p (h t)")
            pe.transpose(p_misc[0:H, 0:P], flat[:, H * f:H * (f + 1)], R.ident[:]).then_inc(s["max_turned"], 1)

        def score_t(pe, b, h):
            n = H * b.n + h
            if h % HALF == 0:
                f = h // HALF
                pe.wait_ge(max_in[b.u][f], 48 * (b.half + 1))
            wait_if(pe, s["arg_ok"], n - 1)
            q, k = qst[b.u][:, h, :], kst[b.u][:, h, :]
            pe.matmul(p_t[h % 2][:, 0:S], k[:, 0:P], q, start=True, stop=True)
            pe.matmul(p_t[h % 2][:, S:S + P], k[:, P:S], q[:, P:S], start=True, stop=True).then_inc(s["scored_t"], 1)

        def weigh(pe, b, h):
            pe.wait_ge(s["prob_ok"], H * b.n + h + 1)
            if h == 0:
                pe.wait_ge(s["v_ok"], b.n + 1)
                if isinstance(b.n, int) and b.n < 2:
                    pe.wait_ge(s["ones_ok"], 2)
                wait_if(pe, s["o_ok"], b.n - 1)
            o, pr, v = bank_o(b.u), prob[h % 4], va[b.u]
            pe.matmul(o[:, 0, h, :], pr[:, 0:P], v[:, 0, h, :], start=True, stop=True)
            pe.matmul(o[:, 1, h, :], pr[:, P:S], v[:, 0, h, :], start=True, stop=False)
            pe.matmul(o[:, 1, h, :], pr[:, S:S + P], v[:, 1, h, :], start=False, stop=True).then_inc(s["summed"], 1)

        def turn_o(pe, b):
            pe.wait_ge(s["o_ok"], b.n + 1)
            for k in range(2):
                mm = pe.transpose(p_misc[:, k * P:(k + 1) * P], o_sb[:, k, :], R.ident[:])
            mm.then_inc(s["o_turned"], 1)

        def project_o(pe, b):
            pe.wait_ge(s["o_t_ok"], b.n + 1)
            for k in range(2):
                mm = pe.matmul(p_misc[:, k * P:(k + 1) * P], o_t[:, k * P:(k + 1) * P], R.w_proj[:],
                               start=True, stop=True)
            mm.then_inc(s["projected"], 1)

        def misc_free(pe, sem_name, count):
            wait_if(pe, s[sem_name], count)

        @block.tensor
        def _(pe):
            pe.wait_ge(s["bias_in"], 32)
            for n, part_of in enumerate(bias_pieces()):
                wait_if(pe, s["bias_neg"], n - 1)
                pe.matmul(p_t[n % 2][:], R.reverse[:], part_of, start=True, stop=True).then_inc(s["bias_turned"], 1)
            pe.wait_ge(s["bias_neg"], H)
            b0, b1 = Batch(0, 0), Batch(0, 1)
            project(pe, b0)
            values(pe, b0)
            project(pe, b1)
            for h in range(H):
                score(pe, b0, h)
                if h == HALF:
                    misc_free(pe, "v_ok", 1)
                    turn_max(pe, b0, 0)
            misc_free(pe, "max_read", 2)
            turn_max(pe, b0, 1)

            def step(pe, j, c):
                b, nxt, prev = Batch(j, c), Batch(j, c + 1), Batch(j, c - 1)
                for h in range(H):
                    if has(j, c, 1):
                        score(pe, nxt, h)
                    score_t(pe, b, h)
                    if h >= 2:
                        weigh(pe, b, h - 2)
                    elif has(j, c, -1):
                        weigh(pe, prev, H - 2 + h)
                    if h == 2 and has(j, c, 2):
                        project(pe, Batch(j, c + 2))
                    if h == 3 and has(j, c, 1):
                        misc_free(pe, "max_read", 2 * (2 * b.n + 2))
                        values(pe, nxt)
                    if h == 5 and has(j, c, -1):
                        if has(j, c, 1):
                            misc_free(pe, "v_ok", b.n + 2)
                        else:
                            misc_free(pe, "max_read", 2 * (2 * b.n + 2))
                        turn_o(pe, prev)
                    if h == 8 and has(j, c, -1):
                        project_o(pe, prev)
                    if h == 11 and has(j, c, 1):
                        if has(j, c, -1):
                            misc_free(pe, "y_ok", b.n)
                        else:
                            misc_free(pe, "v_ok", b.n + 2)
                        turn_max(pe, nxt, 0)
                if has(j, c, 1):
                    misc_free(pe, "max_read", 2 * (2 * nxt.n + 1))
                    turn_max(pe, nxt, 1)
            steps(pe, step)
            last = Batch(0, B - 1)
            weigh(pe, last, H - 2)
            weigh(pe, last, H - 1)
            misc_free(pe, "y_ok", B - 1)
            turn_o(pe, last)
            project_o(pe, last)

        def read_qk(act, b):
            act.wait_ge(s["qk_mm"], b.n + 1)
            wait_if(act, s["part1"], b.n)
            wait_if(act, s["rest_ok"], b.n)
            act.activation(qk[:, 0:S], p_qk[:, 0:S], ACT.Identity, bias=R.bq_neg[:], scale=-SCALE0
                           ).then_inc(s["qk_ok"], 1)
            act.activation(qk[:, S:2 * S], p_qk[:, S:2 * S], ACT.Identity, bias=R.b_qk[:, 1:2]
                           ).then_inc(s["qk_ok"], 1)

        def read_max(act, b, f):
            act.wait_ge(s["max_turned"], 2 * b.n + f + 1)
            wait_if(act, s["max_diff"], 2 * b.n + f - 1)
            if not isinstance(b.half, int) or b.half > 0 or b.u > 0:
                pu = 1 - b.u
                prev_half = b.half if b.u else b.half - 1
                act.wait_ge(max_in[pu][f], 48 * (prev_half + 1))
            act.activation(max_f[f][:], p_misc[0:H, 0:P], ACT.Copy).then_inc(s["max_read"], 1)
            act.activation(max_part[f][:, 0, :], p_misc[0:H, 0:P], ACT.Copy).then_inc(s["max_read"], 1)

        def second_max(act, b, f):
            act.wait_ge(s["max_diff"], 2 * b.n + f + 1)
            act.activation(max_part[f][:, 1, :], max_rest[f][:], ACT.Copy).then_inc(s["max_p2"], 1)

        def exponent(act, b, h):
            n = H * b.n + h
            act.wait_ge(s["arg_ok"], n + 1)
            wait_if(act, s["summed"], n - 3)
            act.activation(prob[h % 4][:], arg[h % 4][:], ACT.Exp, scale=-1.0).then_inc(s["prob_ok"], 1)

        def copy_o(act, b):
            act.wait_ge(s["o_turned"], b.n + 1)
            wait_if(act, s["projected"], b.n)
            act.activation(o_t[:], p_misc[:, 0:S], ACT.Copy).then_inc(s["o_t_ok"], 1)

        @block.scalar
        def _(act):
            for n, part_of in enumerate(bias_pieces()):
                act.wait_ge(s["bias_turned"], n + 1)
                act.mul(part_of, p_t[n % 2][:].rearrange("p (h k) -> p h k", h=2), -1.0).then_inc(s["bias_neg"], 1)
            b0, b1 = Batch(0, 0), Batch(0, 1)
            read_qk(act, b0)
            read_qk(act, b1)
            read_max(act, b0, 0)
            second_max(act, b0, 0)

            def step(act, j, c):
                b, nxt, prev = Batch(j, c), Batch(j, c + 1), Batch(j, c - 1)
                for h in range(H):
                    if h == 0:
                        read_max(act, b, 1)
                    if h == 1:
                        second_max(act, b, 1)
                    exponent(act, b, h)
                    if h == 3 and has(j, c, 2):
                        read_qk(act, Batch(j, c + 2))
                    if h == 6 and has(j, c, -1):
                        copy_o(act, prev)
                    if h == 12 and has(j, c, 1):
                        read_max(act, nxt, 0)
                    if h == 13 and has(j, c, 1):
                        second_max(act, nxt, 0)
            steps(act, step)
            copy_o(act, Batch(0, B - 1))

        def first_part(dve, b):
            dve.wait_ge(s["qk_ok"], 2 * (b.n + 1))
            wait_if(dve, spilled[b.u], 64 * b.half)
            dve.tensor_copy(part[b.u][:, 0, :], qk[:]).then_inc(s["part1"], 1)

        def second_part(dve, b):
            dve.wait_ge(s["rest_ok"], b.n + 1)
            dve.tensor_copy(part[b.u][:, 1, :], rest[:]).then_inc(s["part2"], 1)

        def read_v(dve, b):
            dve.wait_ge(s["v_mm"], b.n + 1)
            wait_if(dve, s["summed"], H * (b.n - 1) if not isinstance(b.n, int) or b.n >= 2 else 0)
            for k in range(2):
                ins = dve.tensor_tensor(va[b.u][:, k, :, 0:HD],
                                        p_misc[:, k * P:(k + 1) * P].rearrange("p (h d) -> p h d", h=H),
                                        R.b_v[:].rearrange("p (h d) -> p h d", h=H), ALU.add)
            ins.then_inc(s["v_ok"], 1)

        def row_max_waits(dve, b, h):
            n = H * b.n + h
            dve.wait_ge(s["scored"], n + 1)
            if h == 0:
                wait_if(dve, s["max_turned"], 2 * (b.n - 1) if not isinstance(b.n, int) or b.n >= 2 else 0)
            wait_if(dve, s["max_ok"], 2 * n - 2)

        def row_max(dve, b, h):
            for t, cols, at in ((1, slice(0, S), slice(0, S)), (0, slice(S, S + P), slice(P, S))):
                r = (2 * h + 1 - t) % 4
                w = cols.stop - cols.start
                dve.tensor_tensor_reduce(out=sums[r][:, 0:w], in0=p_s[h % 2][:, cols], in1=bias_q[:, h, at],
                                         scale=1.0, scalar=3.0e38, op0=ALU.add, op1=ALU.min,
                                         accum_out=neg_max[b.u][:, h, t:t + 1]).then_inc(s["max_ok"], 1)

        def add_bias(dve, b, h):
            n = H * b.n + h
            dve.wait_ge(s["scored_t"], n + 1)
            wait_if(dve, s["prob_ok"], n - 3)
            dve.tensor_tensor(arg[h % 4][:], p_t[h % 2][:, 0:S + P], bias_k[:, h, :], ALU.add
                              ).then_inc(s["arg_ok"], 1)

        def normalise(dve, b):
            dve.wait_ge(s["summed"], H * (b.n + 1))
            dve.reciprocal(rden[:], bank_o(b.u)[:, :, :, HD]).then_inc(s["rden_ok"], 1)
            dve.wait_ge(s["rden_ok"], b.n + 1)
            wait_if(dve, s["o_turned"], b.n)
            for k in range(2):
                ins = dve.tensor_tensor(o_sb[:, k, :].rearrange("p (h d) -> p h d", h=H),
                                        bank_o(b.u)[:, k, :, 0:HD],
                                        rden[:, k, :].unsqueeze(2).to_broadcast([P, H, HD]), ALU.mult)
            ins.then_inc(s["o_ok"], 1)

        def residual(dve, b):
            dve.wait_ge(s["projected"], b.n + 1)
            dve.wait_ge(s["resid_ok"], b.n + 1)
            wait_if(dve, s["yn_ok"], 2 * b.n)
            dve.tensor_tensor(y[:], p_misc[:, 0:S].rearrange("p (t d) -> p t d", t=2), resid[:], ALU.add
                              ).then_inc(s["y_ok"], 1)
            dve.wait_ge(s["y_ok"], b.n + 1)
            for k in range(2):
                dve.bn_stats(stats[:, k, :], y[:, k, :]).then_inc(s["stats_ok"], 1)

        def aggregate(dve, b):
            for k in range(2):
                dve.bn_aggr(mean_var[:, k, :], stats[:, k, :]).then_inc(s["mv_ok"], 1)

        def centre(dve, b):
            dve.wait_ge(s["rstd_ok"], b.n + 1)
            wait_if(dve, s["yg_ok"], b.n)
            for k in range(2):
                dve.tensor_scalar(yn[:, k, :], y[:, k, :], mean_var[:, k, 0:1], rstd[:, k:k + 1],
                                  ALU.subtract, ALU.mult).then_inc(s["yn_ok"], 1)

        @block.vector
        def _(dve):
            for u in range(2):
                dve.memset(kst[u][64:MROWS, :, :], -1.0).then_inc(s["rows_ok"], 1)
            b0, b1 = Batch(0, 0), Batch(0, 1)
            first_part(dve, b0)
            read_v(dve, b0)
            second_part(dve, b0)
            first_part(dve, b1)
            second_part(dve, b1)
            dve.wait_ge(s["bias_ok"], 3)
            for h in range(H):
                row_max_waits(dve, b0, h)
                row_max(dve, b0, h)

            def step(dve, j, c):
                b, nxt, prev = Batch(j, c), Batch(j, c + 1), Batch(j, c - 1)
                for h in range(H):
                    if has(j, c, 1):
                        row_max_waits(dve, nxt, h)
                    if h == 10 and has(j, c, -1):
                        dve.wait_ge(s["stats_ok"], 2 * prev.n + 2)
                        wait_if(dve, s["eps_ok"], prev.n)
                    add_bias(dve, b, h)
                    if has(j, c, 1):
                        row_max(dve, nxt, h)
                    if h == 2 and has(j, c, -1):
                        normalise(dve, prev)
                    if h == 4 and has(j, c, 2):
                        first_part(dve, Batch(j, c + 2))
                    if h == 4 and has(j, c, 1):
                        read_v(dve, nxt)
                    if h == 7 and has(j, c, 2):
                        second_part(dve, Batch(j, c + 2))
                    if h == 9 and has(j, c, -1):
                        residual(dve, prev)
                    if h == 10 and has(j, c, -1):
                        aggregate(dve, prev)
                    if h == 13 and has(j, c, -1):
                        centre(dve, prev)
            steps(dve, step)
            last = Batch(0, B - 1)
            normalise(dve, last)
            residual(dve, last)
            dve.wait_ge(s["stats_ok"], 2 * B)
            dve.wait_ge(s["eps_ok"], B - 1)
            aggregate(dve, last)
            centre(dve, last)

        def take_first(pool, b):
            pool.wait_ge(s["part1"], b.n + 1)
            wait_if(pool, s["part3"], b.n)
            wait_if(pool, s["part2"], b.n)
            pool.tensor_tensor(rest[:], qk[:], part[b.u][:, 0, :], ALU.subtract).then_inc(s["rest_ok"], 1)

        def third_part(pool, b):
            pool.wait_ge(s["part2"], b.n + 1)
            pool.tensor_tensor(part[b.u][:, 2, :], rest[:], part[b.u][:, 1, :], ALU.subtract
                               ).then_inc(s["part3"], 1)

        def max_diff(pool, b, f):
            pool.wait_ge(s["max_read"], 2 * (2 * b.n + f + 1))
            wait_if(pool, s["max_p3"], 2 * b.n + f - 1)
            pool.tensor_tensor(max_rest[f][:], max_f[f][:], max_part[f][:, 0, :], ALU.subtract
                               ).then_inc(s["max_diff"], 1)

        def third_max(pool, b, f):
            pool.wait_ge(s["max_p2"], 2 * b.n + f + 1)
            pool.tensor_tensor(max_part[f][:, 2, :], max_rest[f][:], max_part[f][:, 1, :], ALU.subtract
                               ).then_inc(s["max_p3"], 1)

        def prepare_residual(pool, b):
            wait_if(pool, s["y_ok"], b.n)
            pool.tensor_tensor(resid[:], R.xn[:, bass.ds(2 * b.n, 2), :],
                               R.b_proj[:].unsqueeze(1).to_broadcast([P, 2, P]), ALU.add).then_inc(s["resid_ok"], 1)

        def inverse_std(pool, b):
            pool.wait_ge(s["mv_ok"], 2 * (b.n + 1))
            pool.tensor_tensor(var_eps[:], mean_var[:, :, 1], R.eps[:, 0:2], ALU.add).then_inc(s["eps_ok"], 1)
            pool.wait_ge(s["eps_ok"], b.n + 1)
            wait_if(pool, s["yn_ok"], 2 * b.n)
            pool.tensor_tensor(rstd[:], var_eps[:], R.neg_half[:, 0:2], ALU.pow).then_inc(s["rstd_ok"], 1)

        def affine(pool, b):
            pool.wait_ge(s["yn_ok"], 2 * (b.n + 1))
            wait_if(pool, s["s_ok"], b.n)
            pool.tensor_tensor(yg[:], yn[:], R.ln_g[:].unsqueeze(1).to_broadcast([P, 2, P]), ALU.mult
                               ).then_inc(s["yg_ok"], 1)
            pool.wait_ge(s["yg_ok"], b.n + 1)
            pool.tensor_tensor(R.s[:, bass.ds(2 * b.n, 2), :], yg[:], R.ln_b[:].unsqueeze(1).to_broadcast([P, 2, P]),
                               ALU.add).then_inc(s["s_ok"], 1)

        @block.gpsimd
        def _(pool):
            for u in range(2):
                pool.memset(va[u][:, :, :, HD], 1.0).then_inc(s["ones_ok"], 1)
            pool.wait_ge(s["bias_neg"], H)
            pool.affine_select(out=bias_q[:, :, P:S], in_=bias_q[:, :, P:S], compare_op=ALU.is_ge, fill=BIG, base=0,
                               pattern=[[0, H], [-1, P]], channel_multiplier=1).then_inc(s["bias_ok"], 1)
            pool.affine_select(out=bias_k[:, :, 0:P], in_=bias_k[:, :, 0:P], compare_op=ALU.is_ge, fill=BIG, base=0,
                               pattern=[[0, H], [1, P]], channel_multiplier=-1).then_inc(s["bias_ok"], 1)
            pool.wait_ge(s["bias_ok"], 2)
            pool.tensor_copy(bias_k[:, :, S:S + P], bias_k[:, :, 0:P]).then_inc(s["bias_ok"], 1)
            b0, b1 = Batch(0, 0), Batch(0, 1)
            for b in (b0, b1):
                take_first(pool, b)
                third_part(pool, b)
            max_diff(pool, b0, 0)
            third_max(pool, b0, 0)

            def step(pool, j, c):
                b, nxt, prev = Batch(j, c), Batch(j, c + 1), Batch(j, c - 1)
                max_diff(pool, b, 1)
                third_max(pool, b, 1)
                if has(j, c, 2):
                    take_first(pool, Batch(j, c + 2))
                    third_part(pool, Batch(j, c + 2))
                if has(j, c, -1):
                    prepare_residual(pool, prev)
                    inverse_std(pool, prev)
                    affine(pool, prev)
                if has(j, c, 1):
                    max_diff(pool, nxt, 0)
                    third_max(pool, nxt, 0)
            steps(pool, step)
            last = Batch(0, B - 1)
            prepare_residual(pool, last)
            inverse_std(pool, last)
            affine(pool, last)


def attention1(nc, R, D):
    tag = "a1_"
    with ExitStack() as ctx:
        sem = Sems(nc, ctx)
        ctx.callback(sem.done)

        def sb(name, shape, dt=F32):
            return ctx.enter_context(nc.sbuf_tensor(tag + name, shape, dt))

        def ps(name):
            return ctx.enter_context(nc.psum_tensor(tag + name, [P, 512], F32))

        cos_sin = sb("cos_sin", [P, 2, 2 * S])
        decay = sb("decay", [P, 2, S])
        xs = [sb(f"xs{u}", [P, S]) for u in range(2)]
        along = sb("along", [P, 2 * S])
        across = sb("across", [P, 2 * S])
        qk = [sb(f"qk{u}", [P, 2 * S]) for u in range(2)]
        v = [sb(f"v{u}", [P, 2, P]) for u in range(2)]
        neg_max = sb("neg_max", [P, 2])
        total, rden = sb("total", [P, 2]), [sb(f"rden{u}", [P, 2]) for u in range(2)]
        prob, decayed = sb("prob", [P, 2, S]), sb("decayed", [P, 2, S])
        prob_t = [sb(f"prob_t{u}", [P, 2, S]) for u in range(2)]
        p_a, p_b, p_v = ps("p_a"), ps("p_b"), ps("p_v")
        p_s = [ps(f"p_s{u}") for u in range(2)]
        p_p = [ps(f"p_p{u}") for u in range(2)]
        p_o = ps("p_o")
        s = {n: sem(tag + n) for n in (
            "tables_in", "qk_mm", "along_ok", "across_ok", "qk_ok", "v_mm", "v_ok", "scored", "max_ok", "prob_ok",
            "decayed_ok", "turned", "turned_ok", "summed", "rden_ok", "s_ok")}
        xs_in = sem.pair(tag + "xs_in")
        block = ctx.enter_context(nc.Block())

        def steps(eng, do):
            do(eng, 0, 0)
            do(eng, 0, 1)
            with eng.Fori(1, B // 2 - 1) as j:
                do(eng, j, 0)
                do(eng, j, 1)
            do(eng, 0, B - 2)
            do(eng, 0, B - 1)

        def has(j, c, ahead):
            return not isinstance(j, int) or 0 <= c + ahead < B

        @block.sync
        def _(sp):
            sem.clear_old(sp)
            sp.dma_start(cos_sin[:], D["cos_sin"]).then_inc(s["tables_in"], 16)
            sp.dma_start(decay[:], D["decay"].rearrange("(t p) k -> p t k", p=P)).then_inc(s["tables_in"], 16)

            def step(sp, j, c):
                b = Batch(j, c)
                wait_if(sp, s["v_mm"], b.n - 1)
                sp.dma_start(xs[b.u][:], R.xt[:, bass.ds(S * b.n, S)]).then_inc(xs_in[b.u], 16)
            steps(sp, step)

        def project(pe, b):
            pe.wait_ge(xs_in[b.u], 16 * (b.half + 1))
            wait_if(pe, s["along_ok"], b.n)
            wait_if(pe, s["across_ok"], b.n)
            for bank, at in ((p_a, 0), (p_b, 2)):
                for k in range(2):
                    mm = pe.matmul(bank[:, k * S:(k + 1) * S], R.w_x1[:, (at + k) * P:(at + k + 1) * P], xs[b.u][:],
                                   start=True, stop=True)
            mm.then_inc(s["qk_mm"], 1)
            wait_if(pe, s["v_ok"], b.n)
            for k in range(2):
                mm = pe.matmul(p_v[:, k * P:(k + 1) * P], xs[b.u][:, k * P:(k + 1) * P], R.w_x1[:, 4 * P:5 * P],
                               start=True, stop=True)
            mm.then_inc(s["v_mm"], 1)

        def score(pe, b):
            pe.wait_ge(s["qk_ok"], b.n + 1)
            wait_if(pe, s["prob_ok"], 2 * (b.n - 1))
            for k in range(2):
                mm = pe.matmul(p_s[b.u][:, k * S:(k + 1) * S], qk[b.u][:, k * P:(k + 1) * P], qk[b.u][:, S:2 * S],
                               start=True, stop=True)
            mm.then_inc(s["scored"], 1)

        def turn(pe, b):
            pe.wait_ge(s["decayed_ok"], b.n + 1)
            wait_if(pe, s["turned_ok"], b.n - 1)
            for k in range(2):
                for q in range(2):
                    mm = pe.transpose(p_p[b.u][:, k * S + q * P:k * S + (q + 1) * P],
                                      decayed[:, q, k * P:(k + 1) * P], R.ident[:])
            mm.then_inc(s["turned"], 1)

        def weigh(pe, b):
            pe.wait_ge(s["turned_ok"], b.n + 1)
            pe.wait_ge(s["v_ok"], b.n + 1)
            wait_if(pe, s["s_ok"], 2 * b.n)
            for q in range(2):
                for k in range(2):
                    mm = pe.matmul(p_o[:, q * P:(q + 1) * P], prob_t[b.u][:, k, q * P:(q + 1) * P], v[b.u][:, k, :],
                                   start=(k == 0), stop=(k == 1))
            mm.then_inc(s["summed"], 1)

        @block.tensor
        def _(pe):
            project(pe, Batch(0, 0))

            def step(pe, j, c):
                b = Batch(j, c)
                score(pe, b)
                if has(j, c, -1):
                    turn(pe, Batch(j, c - 1))
                if has(j, c, 1):
                    project(pe, Batch(j, c + 1))
                if has(j, c, -1):
                    weigh(pe, Batch(j, c - 1))
            steps(pe, step)
            turn(pe, Batch(0, B - 1))
            weigh(pe, Batch(0, B - 1))

        @block.vector
        def _(dve):
            def rotate(dve, b):
                dve.wait_ge(s["qk_mm"], b.n + 1)
                wait_if(dve, s["qk_ok"], b.n)
                dve.tensor_tensor(along[:], p_a[:], cos_sin[:, 0, :], ALU.mult).then_inc(s["along_ok"], 1)
                dve.tensor_tensor(across[:], p_b[:], cos_sin[:, 1, :], ALU.mult).then_inc(s["across_ok"], 1)

            def row_max(dve, b):
                dve.wait_ge(s["scored"], b.n + 1)
                wait_if(dve, s["prob_ok"], 2 * b.n)
                dve.tensor_reduce(neg_max[:], p_s[b.u][:].rearrange("p (t k) -> p t k", t=2), X, ALU.max,
                                  negate=True).then_inc(s["max_ok"], 1)

            def decay_it(dve, b):
                dve.wait_ge(s["prob_ok"], 2 * (b.n + 1))
                wait_if(dve, s["turned"], b.n)
                dve.tensor_tensor(decayed[:], prob[:], decay[:], ALU.mult).then_inc(s["decayed_ok"], 1)
                wait_if(dve, s["s_ok"], 2 * (b.n - 1))
                dve.reciprocal(rden[b.u][:], total[:]).then_inc(s["rden_ok"], 1)

            dve.wait_ge(s["tables_in"], 32)
            rotate(dve, Batch(0, 0))

            def step(dve, j, c):
                b = Batch(j, c)
                row_max(dve, b)
                if has(j, c, 1):
                    rotate(dve, Batch(j, c + 1))
                decay_it(dve, b)
            steps(dve, step)

        @block.gpsimd
        def _(pool):
            def step(pool, j, c):
                b = Batch(j, c)
                pool.wait_ge(s["along_ok"], b.n + 1)
                pool.wait_ge(s["across_ok"], b.n + 1)
                wait_if(pool, s["scored"], b.n - 1)
                pool.tensor_tensor(qk[b.u][:], along[:], across[:], ALU.add).then_inc(s["qk_ok"], 1)
            steps(pool, step)

        @block.scalar
        def _(act):
            def read_v(act, b):
                act.wait_ge(s["v_mm"], b.n + 1)
                wait_if(act, s["summed"], b.n - 1)
                act.activation(v[b.u][:].rearrange("p t d -> p (t d)"), p_v[:, 0:S], ACT.Copy).then_inc(s["v_ok"], 1)

            def exponent(act, b):
                act.wait_ge(s["max_ok"], b.n + 1)
                wait_if(act, s["decayed_ok"], b.n)
                wait_if(act, s["rden_ok"], b.n)
                for k in range(2):
                    act.activation(prob[:, k, :], p_s[b.u][:, k * S:(k + 1) * S], ACT.Exp, bias=neg_max[:, k:k + 1],
                                   accum_out=total[:, k:k + 1]).then_inc(s["prob_ok"], 1)

            def read_turned(act, b):
                act.wait_ge(s["turned"], b.n + 1)
                wait_if(act, s["summed"], b.n - 1)
                act.activation(prob_t[b.u][:].rearrange("p t k -> p (t k)"), p_p[b.u][:], ACT.Copy
                               ).then_inc(s["turned_ok"], 1)

            def out(act, b):
                act.wait_ge(s["summed"], b.n + 1)
                act.wait_ge(s["rden_ok"], b.n + 1)
                for k in range(2):
                    act.activation(R.s[:, 2 * b.n + k, :], p_o[:, k * P:(k + 1) * P], ACT.Copy,
                                   scale=rden[b.u][:, k:k + 1]).then_inc(s["s_ok"], 1)

            read_v(act, Batch(0, 0))

            def step(act, j, c):
                b = Batch(j, c)
                exponent(act, b)
                if has(j, c, -1):
                    read_turned(act, Batch(j, c - 1))
                if has(j, c, 1):
                    read_v(act, Batch(j, c + 1))
                if has(j, c, -1):
                    out(act, Batch(j, c - 1))
            steps(act, step)
            read_turned(act, Batch(0, B - 1))
            out(act, Batch(0, B - 1))


class Resident:

    def __init__(self, nc, ctx):
        def sem(name):
            return ctx.enter_context(nc.semaphore("k_" + name))

        self.scattered = sem("scattered")
        self.stored = [sem(f"stored{u}") for u in range(2)]
        self.arrived = [sem(f"arrived{r}") for r in range(4)]

        def sb(name, shape, dt=F32):
            return ctx.enter_context(nc.sbuf_tensor("k_" + name, shape, dt))

        self.x, self.xn, self.s = sb("x", [P, NT, P]), sb("xn", [P, NT, P]), sb("s", [P, NT, P])
        self.xt = sb("xt", [P, B * S])
        self.gate_w = [sb(f"gate_w{n}", [P, E]) for n in range(2)]
        self.gb, self.rb = sb("gb", [P, E]), sb("rb", [P, E])
        self.w_qkv, self.b_qk, self.b_v = sb("w_qkv", [P, 3 * P]), sb("b_qk", [P, 2]), sb("b_v", [P, P])
        self.bq_neg = sb("bq_neg", [P, 1])
        self.w_proj, self.b_proj = sb("w_proj", [P, P]), sb("b_proj", [P, P])
        self.ln_g, self.ln_b = sb("ln_g", [P, P]), sb("ln_b", [P, P])
        self.w_x1 = sb("w_x1", [P, 5 * P])
        self.ident, self.reverse = sb("ident", [P, P]), sb("reverse", [P, P])
        self.ones_bf, self.upper_bf = sb("ones_bf", [P, P], BF16), sb("upper_bf", [P, P], BF16)
        self.neg_half, self.eps, self.zero32 = sb("neg_half", [P, GT]), sb("eps", [P, GT]), sb("zero32", [P, NT])
        self.expert_m8, self.tile_start = sb("expert_m8", [P, E]), sb("tile_start", [P, B * S // SLOTS])
        self.tile_no = sb("tile_no", [P, ROUTED1])
        self.logits = sb("logits", [P, NT, E])
        self.weight = [sb(f"weight{n}", [P, NT]) for n in range(2)]
        self.pos = [sb(f"pos{n}", [P, NT], I32) for n in range(2)]
        self.tile_expert = sb("tile_expert", [1, TILES], I32)


def build(nc, D):
    D["slots_in"] = nc.dram_tensor("slots_in", [TILES * SLOTS, P], F32, kind="Internal").ap()
    D["slots_out"] = [nc.dram_tensor(f"slots_out{n}", [tiles * SLOTS, P], F32, kind="Internal").ap()
                      for n, tiles in enumerate((ROUTED0, TILES))]
    D["parts"] = nc.dram_tensor("parts", [2 * PARTS * 2 * P, S], BF16, kind="Internal").ap()
    Sems.before = None
    with ExitStack() as ctx:
        R = Resident(nc, ctx)
        build_constants(nc, R, D)
        layer_norm_gate(nc, R, D, 0)
        route(nc, R, D, 0)
        experts(nc, R, D, 0)
        attention0(nc, R, D)
        combine(nc, R, D, 0)
        layer_norm_gate(nc, R, D, 1)
        route(nc, R, D, 1)
        experts(nc, R, D, 1)
        attention1(nc, R, D)
        combine(nc, R, D, 1)


def xpos_tables():
    f = np.float32
    scale_vec = (np.arange(0, P, 2, dtype=f) + f(0.4 * P)) / f(1.4 * P)
    scale = scale_vec[None, :] ** (np.arange(S, dtype=f) / f(512.0))[:, None]
    inv_freq = f(1.0) / f(10000.0) ** (np.arange(P // 2, dtype=f) / f(P // 2))
    angle = np.arange(S, dtype=f)[:, None] * inv_freq[None, :]
    sign = np.where(np.arange(P) % 2 == 0, f(-1), f(1))
    out = np.zeros((P, 2, 2 * S), f)
    for k, sc in enumerate((scale, f(1.0) / scale)):
        out[:, 0, k * S:(k + 1) * S] = np.repeat(np.cos(angle) * sc, 2, axis=-1).T
        out[:, 1, k * S:(k + 1) * S] = (np.repeat(np.sin(angle) * sc, 2, axis=-1) * sign).T
    return out


def kernel(**inputs):
    import concourse.bacc as _bacc
    from concourse.bass_utils import run_bass_kernel_spmd as _run

    a = {k: np.asarray(v) for k, v in inputs.items()}
    by_part = a["L0_attn_W_w"].reshape(3, 2, HALF, HD, P)
    w_q, w_k = (by_part[n].transpose(3, 0, 2, 1).reshape(P, P) for n in range(2))
    w_v = a["L0_attn_W_w"][2 * P:].T
    b_part = a["L0_attn_W_b"].reshape(3, 2, HALF, HD)
    swap = np.arange(P) ^ 1
    wq1, wk1, wv1 = a["L1_attn_W_Q"], a["L1_attn_W_K"], a["L1_attn_W_V"]
    rpb_t = a["L0_attn_rpb"].T
    step = np.arange(S)
    arrays = {
        "x": a["L0_attn_x"].reshape(B * S, P),
        "gate_W": a["L0_ffn_gate_W"], "gate_b": a["L0_ffn_gate_b"], "Wr": a["L1_ffn_Wr"], "rb": a["L1_ffn_rb"],
        "w_qkv": np.concatenate([w_q, w_k, w_v], axis=1),
        "b_qk": np.stack([b_part[n].transpose(0, 2, 1).reshape(P) for n in range(2)], axis=1),
        "b_v": a["L0_attn_W_b"][2 * P:], "w_proj": a["L0_attn_proj_w"].T, "b_proj": a["L0_attn_proj_b"],
        "ln_g": a["L0_attn_ln_g"], "ln_b": a["L0_attn_ln_b"],
        "rpbT": rpb_t, "rpbR": rpb_t[:, ::-1],
        "W1": a["L0_ffn_W1"], "W2": a["L0_ffn_W2"], "b2": a["L0_ffn_b2"],
        "b1T": a["L0_ffn_b1"].reshape(E, F0 // P, P).transpose(0, 2, 1),
        "M1": np.concatenate([a["L1_ffn_W1"], a["L1_ffn_Ws1"][None]]),
        "M2": np.concatenate([a["L1_ffn_W2"], a["L1_ffn_Ws2"][None]]),
        "M3": np.concatenate([a["L1_ffn_W3"], a["L1_ffn_Ws3"][None]]),
        "w_x1": np.concatenate([wq1, wk1, wq1[:, swap], wk1[:, swap], wv1], axis=1),
        "cos_sin": xpos_tables(),
        "decay": np.float32(0.9) ** np.abs(step[:, None] - step[None, :]).astype(np.float32),
    }
    arrays = {k: np.ascontiguousarray(v) for k, v in arrays.items()}
    nc = _bacc.Bacc("TRN2", target_bir_lowering=False, num_devices=1)
    D = {k: nc.dram_tensor("in_" + k, v.shape, mybir.dt.from_np(v.dtype), kind="ExternalInput").ap()
         for k, v in arrays.items()}
    D["out"] = nc.dram_tensor("out_0", (B * S, P), F32, kind="ExternalOutput").ap()
    build(nc, D)
    r = _run(nc, [{"in_" + k: v for k, v in arrays.items()}], core_ids=[0])
    return r.results[0]["out_0"].reshape(B, S, P)
```

```python
from contextlib import ExitStack

import numpy as np

import concourse.bass as bass
from concourse import mybir

F32 = mybir.dt.float32
BF16 = mybir.dt.bfloat16
I32 = mybir.dt.int32
ALU = mybir.AluOpType
ACT = mybir.ActivationFunctionType
X = mybir.AxisListType.X

P = 128
B, S = 16, 256
NT = B * S // P
GT = 4
NG = NT // GT
H, HD = 16, 8
E = 8
F0 = 512
F1 = 256
SLOTS = 256
SHARED = B * S // SLOTS
ROUTED0 = (B * S + E * (SLOTS - 1)) // SLOTS
ROUTED1 = (2 * B * S + E * (SLOTS - 1)) // SLOTS
AHEAD = 4
ROUTED0 += -ROUTED0 % AHEAD
ROUTED1 += -ROUTED1 % AHEAD
TILES = SHARED + ROUTED1
LN_EPS = 1e-5
BIG = 1e30
PARTS = 3
KROWS = PARTS * PARTS * HD
MROWS = KROWS + PARTS
HALF = H // 2
SCALE0 = float(1.0 / np.sqrt(np.float32(P)))
SCALE1 = 1.0 / float(np.sqrt(P))


class Sems:

    before = None

    def __init__(self, nc, _):
        self.nc, self.stack, self.all = nc, ExitStack(), []
        self.old, Sems.before = Sems.before, self

    def __call__(self, name):
        self.all.append(self.stack.enter_context(self.nc.semaphore(name)))
        return self.all[-1]

    def pair(self, name):
        return [self(f"{name}{u}") for u in range(2)]

    def clear_old(self, sp):
        for one in self.old.all if self.old else ():
            sp.sem_clear(one)

    def done(self):
        if self.old:
            self.old.stack.close()


def build_constants(nc, R, D):
    with ExitStack() as ctx:
        sem = Sems(nc, ctx)
        ctx.callback(sem.done)
        zeros = ctx.enter_context(nc.sbuf_tensor("zeros", [P, 2048], F32))
        loaded, filled, flags, tables = sem("c_loaded"), sem("c_filled"), sem("c_flags"), sem("c_tables")
        slots_zero, bias_loaded = sem("c_slots_zero"), sem("c_bias_loaded")
        block = ctx.enter_context(nc.Block())

        loads = [(R.x[:], D["x"].rearrange("(t p) d -> p t d", p=P)),
                 (R.gate_w[0][:], D["gate_W"]), (R.gate_w[1][:], D["Wr"]),
                 (R.gb[:], bass.AP(tensor=D["gate_b"].tensor, offset=0, ap=[[0, P], [1, E]])),
                 (R.rb[:], bass.AP(tensor=D["rb"].tensor, offset=0, ap=[[0, P], [1, E]])),
                 (R.w_qkv[:], D["w_qkv"]), (R.b_qk[:], D["b_qk"]),
                 (R.b_v[:], bass.AP(tensor=D["b_v"].tensor, offset=0, ap=[[0, P], [1, P]])),
                 (R.w_proj[:], D["w_proj"]),
                 (R.b_proj[:], bass.AP(tensor=D["b_proj"].tensor, offset=0, ap=[[0, P], [1, P]])),
                 (R.ln_g[:], bass.AP(tensor=D["ln_g"].tensor, offset=0, ap=[[0, P], [1, P]])),
                 (R.ln_b[:], bass.AP(tensor=D["ln_b"].tensor, offset=0, ap=[[0, P], [1, P]])),
                 (R.w_x1[:], D["w_x1"])]

        @block.sync
        def _(sp):
            sem.clear_old(sp)
            for dst, src in loads:
                sp.dma_start(dst, src).then_inc(loaded, 16)
            sp.wait_ge(filled, 1)
            zt = zeros[:].rearrange("p (n d) -> p n d", d=P)
            n = 2048 // P
            for r in range(0, TILES * SLOTS, n * P):
                m = min(n, (TILES * SLOTS - r) // P)
                sp.dma_start(D["slots_in"][r:r + m * P, :].rearrange("(n p) d -> p n d", p=P),
                             zt[:, 0:m, :]).then_inc(slots_zero, 16)
            sp.wait_ge(slots_zero, 16 * (-(-TILES * SLOTS // (n * P))))
            sp.wait_ge(loaded, 16 * len(loads))

        @block.gpsimd
        def _(pool):
            pool.memset(zeros[:], 0.0).then_inc(filled, 1)
            pool.memset(R.ident[:], 0.0).then_inc(flags, 1)
            pool.memset(R.ones_bf[:], 1.0).then_inc(flags, 1)
            pool.memset(R.reverse[:], 0.0).then_inc(flags, 1)
            pool.memset(R.neg_half[:], -0.5).then_inc(flags, 1)
            pool.memset(R.eps[:], LN_EPS).then_inc(flags, 1)
            pool.wait_ge(flags, 5)
            pool.affine_select(out=R.ident[:], in_=R.ident[:], compare_op=ALU.not_equal, fill=1.0, base=0,
                               pattern=[[-1, P]], channel_multiplier=1).then_inc(flags, 1)
            pool.affine_select(out=R.reverse[:], in_=R.reverse[:], compare_op=ALU.not_equal, fill=1.0, base=1 - P,
                               pattern=[[1, P]], channel_multiplier=1).then_inc(flags, 1)
            pool.affine_select(out=R.upper_bf[:], in_=R.ones_bf[:], compare_op=ALU.is_gt, fill=0.0, base=0,
                               pattern=[[1, P]], channel_multiplier=-1).then_inc(flags, 1)
            pool.iota(R.expert_m8[:], [[1, E]], base=-E, channel_multiplier=0,
                      allow_small_or_imprecise_dtypes=True).then_inc(tables, 1)
            pool.iota(R.tile_start[:], [[SLOTS, S * B // SLOTS]], base=0, channel_multiplier=0,
                      allow_small_or_imprecise_dtypes=True).then_inc(tables, 1)
            pool.iota(R.tile_no[:], [[1, ROUTED1]], base=0, channel_multiplier=0,
                      allow_small_or_imprecise_dtypes=True).then_inc(tables, 1)

        @block.vector
        def _(dve):
            dve.memset(R.zero32[:], 0.0)
            dve.wait_ge(loaded, 16 * len(loads))
            dve.tensor_scalar(R.bq_neg[:], R.b_qk[:, 0:1], -SCALE0, None, ALU.mult)


def wait_if(eng, sem, value):
    if not isinstance(value, int) or value > 0:
        eng.wait_ge(sem, value)


def pairs_of_groups(eng, pair):
    pair(eng, 0)
    with eng.Fori(1, NG // 2) as j:
        pair(eng, j)


def layer_norm_gate(nc, R, D, layer):
    tag = f"n{layer}_"
    with ExitStack() as ctx:
        sem = Sems(nc, ctx)
        ctx.callback(sem.done)

        def sb(name, shape, dt=F32):
            return ctx.enter_context(nc.sbuf_tensor(tag + name, shape, dt))

        stats = [sb(f"stats{u}", [P, GT, 6]) for u in range(2)]
        mean_var = [sb(f"mean_var{u}", [P, GT, 2]) for u in range(2)]
        var_eps = [sb(f"var_eps{u}", [P, GT]) for u in range(2)]
        rstd = [sb(f"rstd{u}", [P, GT]) for u in range(2)]
        xn = [sb(f"xn{u}", [P, GT, P]) for u in range(2)]
        xt = [sb(f"xt{u}", [P, GT * P]) for u in range(2)]
        pt = [ctx.enter_context(nc.psum_tensor(f"{tag}pt{u}", [P, GT * P], F32)) for u in range(2)]
        pg = [ctx.enter_context(nc.psum_tensor(f"{tag}pg{u}", [P, 512], F32)) for u in range(2)]
        stats_ok, mv_ok, eps_ok = sem(tag + "stats_ok"), sem.pair(tag + "mv_ok"), sem.pair(tag + "eps_ok")
        rstd_ok, xn_ok = sem.pair(tag + "rstd_ok"), sem.pair(tag + "xn_ok")
        turned, xt_ok = sem.pair(tag + "turned"), sem.pair(tag + "xt_ok")
        gated, logits_ok = sem.pair(tag + "gated"), sem.pair(tag + "logits_ok")
        xn_kept, xt_kept, xn_slots = sem.pair(tag + "xn_kept"), sem.pair(tag + "xt_kept"), sem.pair(tag + "xn_slots")
        block = ctx.enter_context(nc.Block())

        @block.sync
        def _(sp):
            sem.clear_old(sp)
            def pair(sp, j):
                for u in range(2):
                    g = 2 * j + u
                    wait_if(sp, xn_ok[u], GT * (j + 1))
                    sp.dma_start(R.xn[:, bass.ds(GT * g, GT), :], xn[u][:]).then_inc(xn_kept[u], 16)
                    if layer == 1:
                        sp.dma_start(D["slots_in"][bass.ds(GT * P * g, GT * P), :].rearrange(
                            "(t p) d -> p t d", p=P), xn[u][:]).then_inc(xn_slots[u], 16)
                    wait_if(sp, xt_ok[u], j + 1)
                    sp.dma_start(R.xt[:, bass.ds(GT * P * g, GT * P)], xt[u][:]).then_inc(xt_kept[u], 16)
            pairs_of_groups(sp, pair)
            for u in range(2):
                sp.wait_ge(xn_kept[u], 16 * (NG // 2))
                sp.wait_ge(xt_kept[u], 16 * (NG // 2))
                if layer == 1:
                    sp.wait_ge(xn_slots[u], 16 * (NG // 2))

        @block.vector
        def _(dve):
            def pair(dve, j):
                for u in range(2):
                    g = 2 * j + u
                    for k in range(GT):
                        if u and k == GT - 1:
                            dve.wait_ge(stats_ok, 2 * GT * j + GT)
                        dve.bn_stats(stats[u][:, k, :], R.x[:, GT * g + k, :]).then_inc(stats_ok, 1)
                for k in range(GT):
                    dve.bn_aggr(mean_var[0][:, k, :], stats[0][:, k, :]).then_inc(mv_ok[0], 1)
                for u in range(2):
                    g = 2 * j + u
                    wait_if(dve, rstd_ok[u], j + 1)
                    wait_if(dve, turned[u], j)
                    wait_if(dve, xn_kept[u], 16 * j)
                    if layer == 1:
                        wait_if(dve, xn_slots[u], 16 * j)
                    if u == 0:
                        dve.wait_ge(stats_ok, 2 * GT * j + 2 * GT)
                    for k in range(GT):
                        dve.tensor_scalar(xn[u][:, k, :], R.x[:, GT * g + k, :], mean_var[u][:, k, 0:1],
                                          rstd[u][:, k:k + 1], ALU.subtract, ALU.mult).then_inc(xn_ok[u], 1)
                        if u == 0:
                            dve.bn_aggr(mean_var[1][:, k, :], stats[1][:, k, :]).then_inc(mv_ok[1], 1)
                for u in range(2):
                    g = 2 * j + u
                    wait_if(dve, gated[u], j + 1)
                    got = pg[u][:, 0:GT * E].rearrange("p (k e) -> p k e", e=E)
                    if layer == 0:
                        dve.tensor_tensor(R.logits[:, bass.ds(GT * g, GT), :], got,
                                          R.gb[:].unsqueeze(1).to_broadcast([P, GT, E]), ALU.add
                                          ).then_inc(logits_ok[u], 1)
                    else:
                        dve.tensor_scalar(R.logits[:, bass.ds(GT * g, GT), :], got, SCALE1, None, ALU.mult
                                          ).then_inc(logits_ok[u], 1)
            pairs_of_groups(dve, pair)

        @block.gpsimd
        def _(pool):
            def pair(pool, j):
                for u in range(2):
                    wait_if(pool, mv_ok[u], GT * (j + 1))
                    pool.tensor_tensor(var_eps[u][:], mean_var[u][:, :, 1], R.eps[:], ALU.add
                                       ).then_inc(eps_ok[u], 1)
                    wait_if(pool, eps_ok[u], j + 1)
                    wait_if(pool, xn_ok[u], GT * j)
                    pool.tensor_tensor(rstd[u][:], var_eps[u][:], R.neg_half[:, 0:GT], ALU.pow
                                       ).then_inc(rstd_ok[u], 1)
            pairs_of_groups(pool, pair)

        @block.tensor
        def _(pe):
            def pair(pe, j):
                for u in range(2):
                    wait_if(pe, xt_ok[u], j)
                    for k in range(GT):
                        wait_if(pe, xn_ok[u], GT * j + k + 1)
                        mm = pe.transpose(pt[u][:, k * P:(k + 1) * P], xn[u][:, k, :], R.ident[:])
                    mm.then_inc(turned[u], 1)
                for u in range(2):
                    wait_if(pe, xt_ok[u], j + 1)
                    wait_if(pe, logits_ok[u], j)
                    for k in range(GT):
                        mm = pe.matmul(pg[u][:, k * E:(k + 1) * E], xt[u][:, k * P:(k + 1) * P],
                                       R.gate_w[layer][:], start=True, stop=True)
                    mm.then_inc(gated[u], 1)
            pairs_of_groups(pe, pair)

        @block.scalar
        def _(act):
            def pair(act, j):
                for u in range(2):
                    wait_if(act, turned[u], j + 1)
                    wait_if(act, gated[u], j)
                    wait_if(act, xt_kept[u], 16 * j)
                    act.activation(xt[u][:], pt[u][:], ACT.Copy).then_inc(xt_ok[u], 1)
            pairs_of_groups(act, pair)


def route(nc, R, D, layer):
    tag = f"r{layer}_"
    tops = 1 + layer
    routed = (ROUTED0, ROUTED1)[layer]
    with ExitStack() as ctx:
        sem = Sems(nc, ctx)
        ctx.callback(sem.done)

        def sb(name, shape, dt=F32):
            return ctx.enter_context(nc.sbuf_tensor(tag + name, shape, dt))

        best, first = sb("best", [P, NT]), sb("first", [P, NT])
        hit = sb("hit", [P, NT, E])
        pick = [sb(f"pick{n}", [P, NT, E]) for n in range(tops)]
        chosen = sb("chosen", [P, NT, E])
        sel = sb("sel", [P, NT, E])
        mask_bf = sb("mask_bf", [P, E, NT], BF16)
        count, upto, slot = sb("count", [P, E, NT]), sb("upto", [P, E, NT]), sb("slot", [P, E, NT])
        over = sb("over", [P, E, B * S // SLOTS])
        tiles, last, start = sb("tiles", [P, E]), sb("last", [P, E]), sb("start", [P, E])
        before = sb("before", [P, ROUTED1, E])
        owner = sb("owner", [P, ROUTED1])
        pos_f = sb("pos_f", [P, NT])
        top_logit = [sb(f"top_logit{n}", [P, NT]) for n in range(tops)]
        prank = ctx.enter_context(nc.psum_tensor(tag + "prank", [P, 512], F32))
        pcount = ctx.enter_context(nc.psum_tensor(tag + "pcount", [P, 512], F32))
        steps, mask_ok, ranked = sem(tag + "steps"), sem(tag + "mask_ok"), sem(tag + "ranked")
        exps = sem(tag + "exps")
        diff_ok = sem(tag + "diff_ok")
        block = ctx.enter_context(nc.Block())
        per_tile = [P, NT, E]

        @block.vector
        def _(dve):
            done = [0]

            def step(ins):
                done[0] += 1
                ins.then_inc(steps, 1)
                dve.wait_ge(steps, done[0])

            em8 = R.expert_m8[:].unsqueeze(1).to_broadcast(per_tile)

            def one_hot(out, logits):
                step(dve.tensor_reduce(best[:], logits, X, ALU.max))
                step(dve.tensor_tensor(hit[:], logits, best[:].unsqueeze(2).to_broadcast(per_tile), ALU.is_equal))
                step(dve.tensor_tensor(hit[:], hit[:], em8, ALU.mult))
                step(dve.tensor_reduce(first[:], hit[:], X, ALU.min))
                step(dve.tensor_tensor(out[:], em8, first[:].unsqueeze(2).to_broadcast(per_tile), ALU.is_equal))

            def logit_of(out, chose):
                step(dve.tensor_tensor(hit[:], R.logits[:], chose[:], ALU.mult))
                step(dve.tensor_reduce(out[:], hit[:], X, ALU.add))

            if layer == 0:
                one_hot(pick[0], R.logits[:])
                marked = pick[0]
            else:
                step(dve.tensor_tensor(sel[:], R.logits[:], R.rb[:].unsqueeze(1).to_broadcast(per_tile), ALU.add))
                one_hot(pick[0], sel[:])
                step(dve.scalar_tensor_tensor(out=sel[:], in0=pick[0][:], scalar=-BIG, in1=sel[:],
                                              op0=ALU.mult, op1=ALU.add))
                one_hot(pick[1], sel[:])
                step(dve.tensor_tensor(chosen[:], pick[0][:], pick[1][:], ALU.add))
                marked = chosen
            dve.tensor_copy(mask_bf[:].rearrange("p e t -> p t e"), marked[:]).then_inc(mask_ok, 1)
            if layer == 1:
                for n in range(2):
                    logit_of(top_logit[n], pick[n])
                step(dve.tensor_tensor(best[:], top_logit[0][:], top_logit[1][:], ALU.max))
                for n in range(2):
                    ins = dve.tensor_tensor(top_logit[n][:], top_logit[n][:], best[:], ALU.subtract)
                    ins.then_inc(diff_ok, 1)
                dve.wait_ge(exps, 2)
                step(dve.tensor_tensor(first[:], R.weight[0][:], R.weight[1][:], ALU.add))
                step(dve.reciprocal(best[:], first[:]))
                for n in range(2):
                    step(dve.tensor_tensor(R.weight[n][:], R.weight[n][:], best[:], ALU.mult))
            dve.wait_ge(ranked, 1)
            step(dve.tensor_copy(count[:].rearrange("p e t -> p (e t)"), pcount[:, 0:E * NT]))
            for e in range(E):
                ins = dve.tensor_tensor_scan(upto[:, e, :], count[:, e, :], R.zero32[:], 0.0, ALU.add, ALU.add)
                step(ins)
            step(dve.tensor_tensor(over[:], upto[:, :, NT - 1:NT].to_broadcast([P, E, B * S // SLOTS]),
                                   R.tile_start[:].unsqueeze(1).to_broadcast([P, E, B * S // SLOTS]), ALU.is_gt))
            step(dve.tensor_reduce(tiles[:], over[:], X, ALU.add))
            step(dve.tensor_tensor_scan(last[:], tiles[:], R.zero32[:, 0:E], 0.0, ALU.add, ALU.add))
            step(dve.tensor_tensor(start[:], last[:], tiles[:], ALU.subtract))
            step(dve.tensor_scalar(start[:], start[:], float(SLOTS), float(SHARED * SLOTS * layer), ALU.mult, ALU.add))
            step(dve.tensor_tensor(slot[:], prank[:, 0:E * NT].rearrange("p (e t) -> p e t", e=E), upto[:], ALU.add))
            step(dve.tensor_tensor(slot[:], slot[:], count[:], ALU.subtract))
            step(dve.tensor_tensor(slot[:], slot[:], start[:].unsqueeze(2).to_broadcast([P, E, NT]), ALU.add))
            for n in range(tops):
                step(dve.tensor_tensor(hit[:], slot[:].rearrange("p e t -> p t e"), pick[n][:], ALU.mult))
                step(dve.tensor_reduce(pos_f[:], hit[:], X, ALU.add))
                step(dve.tensor_copy(R.pos[n][:], pos_f[:]))
            step(dve.tensor_tensor(before[:], R.tile_no[:].unsqueeze(2).to_broadcast([P, ROUTED1, E]),
                                   last[:].unsqueeze(1).to_broadcast([P, ROUTED1, E]), ALU.is_ge))
            step(dve.tensor_reduce(owner[:], before[:], X, ALU.add))
            step(dve.tensor_scalar(owner[:], owner[:], float(E - 1), None, ALU.min))
            at = SHARED if layer else 0
            step(dve.tensor_copy(R.tile_expert[0:1, at:at + routed], owner[0:1, 0:routed]))
            if layer == 1:
                step(dve.memset(R.tile_expert[0:1, 0:SHARED], E))

        @block.sync
        def _(sp):
            sem.clear_old(sp)

        @block.scalar
        def _(act):
            if layer == 1:
                for n in range(2):
                    act.wait_ge(diff_ok, n + 1)
                    act.activation(R.weight[n][:], top_logit[n][:], ACT.Exp).then_inc(exps, 1)

        @block.tensor
        def _(pe):
            pe.wait_ge(mask_ok, 1)
            flat = mask_bf[:].rearrange("p e t -> p (e t)")
            pe.matmul(prank[:, 0:E * NT], R.upper_bf[:], flat, start=True, stop=True)
            pe.matmul(pcount[:, 0:E * NT], R.ones_bf[:], flat, start=True, stop=True).then_inc(ranked, 1)


def scatter(pool, R, D, layer, tiles):
    for t in tiles:
        for n in range(1 + layer):
            pool.indirect_dma_start(D["slots_in"], bass.IndirectOffsetOnAxis(ap=R.pos[n][:, t:t + 1], axis=0),
                                    R.xn[:, t, :], None).then_inc(R.scattered, 16)


def experts(nc, R, D, layer):
    tag = f"e{layer}_"
    tiles = (ROUTED0, TILES)[layer]
    C = (F0, F1)[layer] // P
    tops = 1 + layer
    with ExitStack() as ctx:
        sem = Sems(nc, ctx)
        ctx.callback(sem.done)

        def sb(name, shape, n=2, dt=F32):
            return [ctx.enter_context(nc.sbuf_tensor(f"{tag}{name}{u}", shape, dt)) for u in range(n)]

        w_up, w_down = sb("w_up", [P, 4, P], AHEAD), sb("w_down", [P, C, P], AHEAD)
        x_in = sb("x_in", [P, 2, P], AHEAD)
        b_up = sb("b_up", [P, 4], AHEAD) if layer == 0 else None
        b_down = sb("b_down", [P, P], AHEAD) if layer == 0 else None
        x_t = sb("x_t", [P, SLOTS])
        hid = sb("hid", [P, C, SLOTS])
        pre = sb("pre", [P, C, SLOTS])
        y_out = sb("y_out", [P, 2, P], AHEAD)
        loads = 5 if layer == 0 else 4
        pt = ctx.enter_context(nc.psum_tensor(tag + "pt", [P, 512], F32))
        ph = [[ctx.enter_context(nc.psum_tensor(f"{tag}ph{u}{n}", [P, 2, SLOTS], F32)) for n in range(2)]
              for u in range(2)]
        py = [ctx.enter_context(nc.psum_tensor(f"{tag}py{u}", [P, 512], F32)) for u in range(2)]
        in_ok = [sem(f"{tag}in_ok{r}") for r in range(AHEAD)]
        stored = [sem(f"{tag}stored{r}") for r in range(AHEAD)]
        turned, x_ok, up_ok, pre_ok = sem(tag + "turned"), sem(tag + "x_ok"), sem(tag + "up_ok"), sem(tag + "pre_ok")
        hid_ok, down_ok, y_ok = sem(tag + "hid_ok"), sem(tag + "down_ok"), sem(tag + "y_ok")
        block = ctx.enter_context(nc.Block())
        rounds = tiles // AHEAD

        def over_tiles(eng, do, until=rounds, begin=0):
            at = begin
            if begin == 0:
                for r in range(AHEAD):
                    do(eng, 0, r)
                at = 1
            with eng.Fori(at, min(until, rounds - 1)) as j:
                for r in range(AHEAD):
                    do(eng, j, r)
            if until == rounds:
                for r in range(AHEAD):
                    do(eng, rounds - 1, r)

        def exists(j, r):
            return not isinstance(j, int) or 0 <= AHEAD * j + r < tiles

        def ring(j, r):
            return j + r // AHEAD, r % AHEAD, AHEAD * j + r

        def load(sp, j, r):
            j, r, i = ring(j, r)
            e = sp.value_load(R.tile_expert[0:1, bass.ds(i, 1)], min_val=0, max_val=E - 1 + layer)
            wait_if(sp, down_ok, i - AHEAD + 1)
            sp.dma_start(x_in[r][:], D["slots_in"][bass.ds(SLOTS * i, SLOTS), :].rearrange(
                "(t p) d -> p t d", p=P)).then_inc(in_ok[r], 16)
            if layer == 0:
                sp.dma_start(w_up[r][:].rearrange("p c m -> p (c m)"), D["W1"][e, :, :]).then_inc(in_ok[r], 16)
                sp.dma_start(b_up[r][:], D["b1T"][e, :, :]).then_inc(in_ok[r], 16)
                sp.dma_start(b_down[r][:], D["b2"][bass.ds(e, 1), :].to_broadcast([P, P])).then_inc(in_ok[r], 16)
                sp.dma_start(w_down[r][:], D["W2"][e, :, :].rearrange("(c p) m -> p c m", p=P)).then_inc(in_ok[r], 16)
            else:
                sp.dma_start(w_up[r][:, 0:2, :].rearrange("p c m -> p (c m)"), D["M1"][e, :, :]
                             ).then_inc(in_ok[r], 16)
                sp.dma_start(w_up[r][:, 2:4, :].rearrange("p c m -> p (c m)"), D["M3"][e, :, :]
                             ).then_inc(in_ok[r], 16)
                sp.dma_start(w_down[r][:], D["M2"][e, :, :].rearrange("(c p) m -> p c m", p=P)).then_inc(in_ok[r], 16)

        @block.sync
        def _(sp):
            sem.clear_old(sp)
            if layer == 0:
                sp.wait_ge(R.scattered, 16 * NT)
            for r in range(AHEAD):
                load(sp, 0, r)

            def tile(sp, j, r):
                i = AHEAD * j + r
                sp.wait_ge(y_ok, i + 1)
                sp.dma_start(D["slots_out"][layer][bass.ds(SLOTS * i, SLOTS), :].rearrange(
                    "(t p) d -> p t d", p=P), y_out[r][:]).then_inc(stored[r], 16)
                if exists(j, r + AHEAD):
                    load(sp, j, r + AHEAD)

            if layer == 0:
                over_tiles(sp, tile)
            else:
                over_tiles(sp, tile, until=SHARED // AHEAD - 1)
                sp.wait_ge(R.scattered, 16 * NT * 3)
                over_tiles(sp, tile, begin=SHARED // AHEAD - 1)
            for r in range(AHEAD):
                sp.wait_ge(stored[r], 16 * rounds)

        @block.gpsimd
        def _(pool):
            if layer == 1:
                scatter(pool, R, D, layer, range(NT))

        def turn(pe, j, r):
            j, r, i = ring(j, r)
            pe.wait_ge(in_ok[r], 16 * loads * (j + 1))
            wait_if(pe, x_ok, i)
            for k in range(2):
                mm = pe.transpose(pt[:, k * P:(k + 1) * P], x_in[r][:, k, :], R.ident[:])
            mm.then_inc(turned, 1)

        def up(pe, j, r):
            j, r, i = ring(j, r)
            u = r % 2
            pe.wait_ge(x_ok, i + 1)
            wait_if(pe, pre_ok, 2 * (i - 1))
            wait_if(pe, hid_ok, 2 * (i - 1))
            for c in range(4):
                mm = pe.matmul(ph[u][c // 2][:, c % 2, :], w_up[r][:, c, :], x_t[u][:], start=True, stop=True)
                if c % 2:
                    mm.then_inc(up_ok, 1)

        def down(pe, j, r):
            i, u = AHEAD * j + r, r % 2
            wait_if(pe, y_ok, i - 1)
            pe.wait_ge(hid_ok, 2 * (i + 1))
            for k in range(2):
                for c in range(C):
                    mm = pe.matmul(py[u][:, k * P:(k + 1) * P], hid[u][:, c, k * P:(k + 1) * P],
                                   w_down[r][:, c, :], start=(c == 0), stop=(c == C - 1))
            mm.then_inc(down_ok, 1)

        @block.tensor
        def _(pe):
            turn(pe, 0, 0)
            turn(pe, 0, 1)
            up(pe, 0, 0)

            def tile(pe, j, r):
                if exists(j, r + 2):
                    turn(pe, j, r + 2)
                if exists(j, r + 1):
                    up(pe, j, r + 1)
                down(pe, j, r)
            over_tiles(pe, tile)

        def x_copy(act, j, r):
            j, r, i = ring(j, r)
            act.wait_ge(turned, i + 1)
            wait_if(act, up_ok, 2 * (i - 1))
            act.activation(x_t[r % 2][:], pt[:, 0:SLOTS], ACT.Copy).then_inc(x_ok, 1)

        def act_fn(act, j, r):
            j, r, i = ring(j, r)
            u = r % 2
            if layer == 0:
                for n in range(2):
                    act.wait_ge(pre_ok, 2 * i + n + 1)
                    wait_if(act, down_ok, i - 1)
                    act.activation(hid[u][:, 2 * n:2 * n + 2, :], pre[u][:, 2 * n:2 * n + 2, :], ACT.Gelu
                                   ).then_inc(hid_ok, 1)
            else:
                act.wait_ge(up_ok, 2 * (i + 1))
                wait_if(act, hid_ok, 2 * (i - 1))
                act.activation(pre[u][:], ph[u][1][:], ACT.Silu).then_inc(pre_ok, 2)

        @block.scalar
        def _(act):
            x_copy(act, 0, 0)
            x_copy(act, 0, 1)
            act_fn(act, 0, 0)

            def tile(act, j, r):
                if exists(j, r + 2):
                    x_copy(act, j, r + 2)
                if exists(j, r + 1):
                    act_fn(act, j, r + 1)
            over_tiles(act, tile)

        def vector_up(dve, j, r):
            j, r, i = ring(j, r)
            u = r % 2
            if layer == 0:
                dve.wait_ge(in_ok[r], 16 * loads * (j + 1))
                for n in range(2):
                    dve.wait_ge(up_ok, 2 * i + n + 1)
                    wait_if(dve, hid_ok, 2 * (i - 1))
                    dve.tensor_tensor(pre[u][:, 2 * n:2 * n + 2, :], ph[u][n][:],
                                      b_up[r][:, 2 * n:2 * n + 2].unsqueeze(2).to_broadcast([P, 2, SLOTS]),
                                      ALU.add).then_inc(pre_ok, 1)
            else:
                dve.wait_ge(pre_ok, 2 * (i + 1))
                wait_if(dve, down_ok, i - 1)
                dve.tensor_tensor(hid[u][:], ph[u][0][:], pre[u][:], ALU.mult).then_inc(hid_ok, 2)

        def vector_down(dve, j, r):
            i = AHEAD * j + r
            dve.wait_ge(down_ok, i + 1)
            wait_if(dve, stored[r], 16 * j)
            got = py[r % 2][:, 0:2 * P].rearrange("p (k d) -> p k d", k=2)
            if layer == 0:
                dve.tensor_tensor(y_out[r][:], got, b_down[r][:].unsqueeze(1).to_broadcast([P, 2, P]), ALU.add
                                  ).then_inc(y_ok, 1)
            else:
                dve.tensor_copy(y_out[r][:], got).then_inc(y_ok, 1)

        @block.vector
        def _(dve):
            vector_up(dve, 0, 0)

            def tile(dve, j, r):
                if exists(j, r + 1):
                    vector_up(dve, j, r + 1)
                vector_down(dve, j, r)
            over_tiles(dve, tile)


def combine0(nc, R, D):
    tag = "m0_"
    with ExitStack() as ctx:
        sem = Sems(nc, ctx)
        ctx.callback(sem.done)
        ring = len(R.arrived)

        def sb(name):
            return [ctx.enter_context(nc.sbuf_tensor(f"{tag}{name}{r}", [P, P], F32)) for r in range(ring)]

        f, gate, prod = sb("f"), sb("gate"), sb("prod")
        gate_ok, prod_ok, x_ok = sem(tag + "gate_ok"), sem(tag + "prod_ok"), sem(tag + "x_ok")
        block = ctx.enter_context(nc.Block())

        @block.gpsimd
        def _(pool):
            for t in range(NT):
                r = t % ring
                if t >= ring:
                    pool.wait_ge(gate_ok, t - ring + 1)
                pool.indirect_dma_start(f[r][:], None, D["slots_out"][0],
                                        bass.IndirectOffsetOnAxis(ap=R.pos[0][:, t:t + 1], axis=0)
                                        ).then_inc(R.arrived[r], 16)

        @block.sync
        def _(sp):
            sem.clear_old(sp)

        @block.scalar
        def _(act):
            for t in range(NT):
                r = t % ring
                act.wait_ge(R.arrived[r], 16 * (t // ring + 1))
                if t >= ring:
                    act.wait_ge(prod_ok, t - ring + 1)
                act.activation(gate[r][:], f[r][:], ACT.Silu).then_inc(gate_ok, 1)

        @block.vector
        def _(dve):
            for t in range(NT):
                r = t % ring
                dve.wait_ge(gate_ok, t + 1)
                if t >= ring:
                    dve.wait_ge(x_ok, t - ring + 1)
                dve.tensor_tensor(prod[r][:], R.s[:, t, :], gate[r][:], ALU.mult).then_inc(prod_ok, 1)
                dve.wait_ge(prod_ok, t + 1)
                dve.tensor_tensor(R.x[:, t, :], R.x[:, t, :], prod[r][:], ALU.add).then_inc(x_ok, 1)


def combine1(nc, R, D, f):
    tag = "m1_"
    with ExitStack() as ctx:
        sem = Sems(nc, ctx)
        ctx.callback(sem.done)
        first_ok, mixed_ok, gate_ok = sem(tag + "first_ok"), sem(tag + "mixed_ok"), sem(tag + "gate_ok")
        prod_ok, x_ok, out_done = sem(tag + "prod_ok"), sem(tag + "x_ok"), sem(tag + "out_done")
        block = ctx.enter_context(nc.Block())

        def group(g):
            return slice(GT * g, GT * (g + 1))

        @block.sync
        def _(sp):
            sem.clear_old(sp)
            for g in range(NG):
                sp.wait_ge(x_ok, g + 1)
                sp.dma_start(D["out"][GT * P * g:GT * P * (g + 1), :].rearrange("(t p) d -> p t d", p=P),
                             R.x[:, group(g), :]).then_inc(out_done, 16)
            sp.wait_ge(out_done, 16 * NG)

        @block.vector
        def _(dve):
            for g in range(NG):
                for t in range(GT * g, GT * (g + 1)):
                    dve.scalar_tensor_tensor(out=f.shared[:, t, :], in0=f.top[0][:, t, :],
                                             scalar=R.weight[0][:, t:t + 1], in1=f.shared[:, t, :],
                                             op0=ALU.mult, op1=ALU.add).then_inc(first_ok, 1)
                for t in range(GT * g, GT * (g + 1)):
                    dve.wait_ge(first_ok, t + 1)
                    dve.scalar_tensor_tensor(out=f.top[0][:, t, :], in0=f.top[1][:, t, :],
                                             scalar=R.weight[1][:, t:t + 1], in1=f.shared[:, t, :],
                                             op0=ALU.mult, op1=ALU.add).then_inc(mixed_ok, 1)

        @block.scalar
        def _(act):
            for g in range(NG):
                act.wait_ge(mixed_ok, GT * (g + 1))
                act.activation(f.top[1][:, group(g), :], f.top[0][:, group(g), :], ACT.Silu).then_inc(gate_ok, 1)

        @block.gpsimd
        def _(pool):
            for g in range(NG):
                pool.wait_ge(gate_ok, g + 1)
                pool.tensor_tensor(f.shared[:, group(g), :], R.s[:, group(g), :], f.top[1][:, group(g), :], ALU.mult
                                   ).then_inc(prod_ok, 1)
                pool.wait_ge(prod_ok, g + 1)
                pool.tensor_tensor(R.x[:, group(g), :], R.x[:, group(g), :], f.shared[:, group(g), :], ALU.add
                                   ).then_inc(x_ok, 1)


class Gathered:

    def __init__(self, nc, ctx):
        self.top = [ctx.enter_context(nc.sbuf_tensor(f"f_top{n}", [P, NT, P], F32)) for n in range(2)]
        self.shared = ctx.enter_context(nc.sbuf_tensor("f_shared", [P, NT, P], F32))


class Batch:

    def __init__(self, j, c):
        self.u, self.half, self.n = c % 2, j + c // 2, 2 * j + c

    def after(self, k):
        return k * self.n


def attention0(nc, R, D):
    tag = "a0_"
    with ExitStack() as ctx:
        sem = Sems(nc, ctx)
        ctx.callback(sem.done)

        def sb(name, shape, dt=F32):
            return ctx.enter_context(nc.sbuf_tensor(tag + name, shape, dt))

        def ps(name):
            return ctx.enter_context(nc.psum_tensor(tag + name, [P, 512], F32))

        bias_q = sb("bias_q", [P, H, S])
        bias_k = sb("bias_k", [P, H, S + P])
        xs = [sb(f"xs{u}", [P, S]) for u in range(2)]
        qk = sb("qk", [P, 2 * S])
        rest = sb("rest", [P, 2 * S])
        part = [sb(f"part{u}", [P, 3, 2 * S], BF16) for u in range(2)]
        qst = [sb(f"qst{u}", [MROWS, H, S], BF16) for u in range(2)]
        kst = [sb(f"kst{u}", [MROWS, H, S], BF16) for u in range(2)]
        va = [sb(f"va{u}", [P, 2, H, HD + 1]) for u in range(2)]
        sums = [sb(f"sums{r}", [P, S], BF16) for r in range(4)]
        neg_max = [sb(f"neg_max{u}", [P, H, 2]) for u in range(2)]
        max_f = [sb(f"max_f{f}", [H, P]) for f in range(2)]
        max_rest = [sb(f"max_rest{f}", [H, P]) for f in range(2)]
        max_part = [sb(f"max_part{f}", [H, 3, P], BF16) for f in range(2)]
        arg = [sb(f"arg{r}", [P, S + P]) for r in range(4)]
        prob = [sb(f"prob{r}", [P, S + P]) for r in range(4)]
        rden = sb("rden", [P, 2, H])
        o_sb = sb("o_sb", [P, 2, P])
        o_t = sb("o_t", [P, S])
        resid = sb("resid", [P, 2, P])
        y = sb("y", [P, 2, P])
        stats, mean_var = sb("stats", [P, 2, 6]), sb("mean_var", [P, 2, 2])
        var_eps, rstd = sb("var_eps", [P, 2]), sb("rstd", [P, 2])
        yn, yg = sb("yn", [P, 2, P]), sb("yg", [P, 2, P])
        p_qk, p_misc = ps("p_qk"), ps("p_misc")
        p_s = [ps(f"p_s{r}") for r in range(2)]
        p_t = [ps(f"p_t{r}") for r in range(2)]
        p_o = [ps(f"p_o{u}") for u in range(2)]

        s = {n: sem(tag + n) for n in (
            "bias_in", "bias_turned", "bias_neg", "bias_ok", "ones_ok", "rows_ok", "qk_mm", "qk_ok", "part1", "part2", "part3", "rest_ok",
            "v_mm", "v_ok", "scored", "max_ok", "max_turned", "max_read", "max_diff", "max_p2", "max_p3",
            "scored_t", "arg_ok", "prob_ok", "summed", "rden_ok", "o_ok", "o_turned", "o_t_ok", "projected",
            "resid_ok", "y_ok", "stats_ok", "mv_ok", "eps_ok", "rstd_ok", "yn_ok", "yg_ok", "s_ok")}
        xs_in, spilled = sem.pair(tag + "xs_in"), sem.pair(tag + "spilled")
        stacked = [[sem(f"{tag}stacked{u}{f}") for f in range(2)] for u in range(2)]
        max_in = [[sem(f"{tag}max_in{u}{f}") for f in range(2)] for u in range(2)]
        block = ctx.enter_context(nc.Block())

        def bank_o(u):
            return p_o[u][:, 0:2 * H * (HD + 1)].rearrange("p (t h d) -> p t h d", t=2, h=H)

        def steps(eng, do):
            do(eng, 0, 0)
            do(eng, 0, 1)
            with eng.Fori(1, B // 2 - 1) as j:
                do(eng, j, 0)
                do(eng, j, 1)
            do(eng, 0, B - 2)
            do(eng, 0, B - 1)

        def bias_pieces():
            return [bias_q[:, h:h + 2, :] for h in range(0, H, 2)] + [bias_k[:, h:h + 2, 0:S] for h in range(0, H, 2)]

        def has(j, c, ahead):
            return not isinstance(j, int) or 0 <= c + ahead < B

        def stage_x(sp, b):
            if not isinstance(b.n, int) or b.n >= 2:
                sp.wait_ge(s["v_mm"], b.n - 1)
            sp.dma_start(xs[b.u][:], R.xt[:, bass.ds(S * b.n, S)]).then_inc(xs_in[b.u], 16)

        def spill(sp, b):
            for name in ("part1", "part2", "part3"):
                sp.wait_ge(s[name], b.n + 1)
            for f in range(2):
                wait_if(sp, stacked[b.u][f], 64 * b.half)
                for k in range(2):
                    dst = bass.AP(tensor=D["parts"].tensor, offset=at_parts(b, k, f),
                                  ap=[[S, P // 2], [P // 2 * S, PARTS], [1, S]])
                    sp.dma_start(dst, part[b.u][P // 2 * f:P // 2 * (f + 1), :, k * S:(k + 1) * S]
                                 ).then_inc(spilled[b.u], 16)

        def at_parts(b, k, f):
            return ((b.u * 2 + k) * 2 + f) * PARTS * P // 2 * S

        def stack(sp, b, f):
            wait_if(sp, s["scored_t"], H * (b.n - 2) + HALF * (f + 1))
            sp.wait_ge(spilled[b.u], 64 * (b.half + 1))
            heads = slice(HALF * f, HALF * (f + 1))
            src = bass.AP(tensor=D["parts"].tensor, offset=at_parts(b, 1, f),
                          ap=[[0, PARTS], [HALF * S, PARTS * HD], [1, HALF * S]])
            sp.dma_start(kst[b.u][0:KROWS, heads, :], src).then_inc(stacked[b.u][f], 16)
            for i in range(PARTS):
                src = bass.AP(tensor=D["parts"].tensor, offset=at_parts(b, 0, f) + i * P // 2 * S,
                              ap=[[0, PARTS], [HALF * S, HD], [1, HALF * S]])
                sp.dma_start(qst[b.u][PARTS * HD * i:PARTS * HD * (i + 1), heads, :], src
                             ).then_inc(stacked[b.u][f], 16)

        def stack_max(sp, b, f):
            sp.wait_ge(s["max_read"], 2 * (2 * b.n + f + 1))
            sp.wait_ge(s["max_p2"], 2 * b.n + f + 1)
            sp.wait_ge(s["max_p3"], 2 * b.n + f + 1)
            for i in range(3):
                sp.dma_start(qst[b.u][KROWS + i:KROWS + i + 1, HALF * f:HALF * (f + 1), :],
                             max_part[f][:, i, :]).then_inc(max_in[b.u][f], 16)

        @block.sync
        def _(sp):
            sem.clear_old(sp)
            sp.dma_start(bias_q[:], bass.AP(tensor=D["rpbT"].tensor, offset=0,
                                            ap=[[1, P], [2 * S - 1, H], [1, S]])).then_inc(s["bias_in"], 16)
            sp.dma_start(bias_k[:, :, 0:S], bass.AP(tensor=D["rpbR"].tensor, offset=P,
                                                    ap=[[1, P], [2 * S - 1, H], [1, S]])).then_inc(s["bias_in"], 16)
            stage_x(sp, Batch(0, 0))
            stage_x(sp, Batch(0, 1))
            sp.wait_ge(s["rows_ok"], 2)
            for b in (Batch(0, 0), Batch(0, 1)):
                spill(sp, b)
                stack(sp, b, 0)
                stack(sp, b, 1)
            stack_max(sp, Batch(0, 0), 0)

            def step(sp, j, c):
                b = Batch(j, c)
                if has(j, c, 2):
                    stage_x(sp, Batch(j, c + 2))
                stack_max(sp, b, 1)
                if has(j, c, 2):
                    spill(sp, Batch(j, c + 2))
                    stack(sp, Batch(j, c + 2), 0)
                if has(j, c, 1):
                    stack_max(sp, Batch(j, c + 1), 0)
                if has(j, c, 2):
                    stack(sp, Batch(j, c + 2), 1)
            steps(sp, step)

        def project(pe, b):
            pe.wait_ge(xs_in[b.u], 16 * (b.half + 1))
            wait_if(pe, s["qk_ok"], 2 * b.n)
            pe.matmul(p_qk[:, 0:S], R.w_qkv[:, 0:P], xs[b.u][:], start=True, stop=True)
            pe.matmul(p_qk[:, S:2 * S], R.w_qkv[:, P:2 * P], xs[b.u][:], start=True, stop=True
                      ).then_inc(s["qk_mm"], 1)

        def values(pe, b):
            for k in range(2):
                mm = pe.matmul(p_misc[:, k * P:(k + 1) * P], xs[b.u][:, k * P:(k + 1) * P],
                               R.w_qkv[:, 2 * P:3 * P], start=True, stop=True)
            mm.then_inc(s["v_mm"], 1)

        def score(pe, b, h):
            n = H * b.n + h
            if h % HALF == 0:
                pe.wait_ge(stacked[b.u][h // HALF], 64 * (b.half + 1))
            wait_if(pe, s["max_ok"], 2 * (n - 1))
            q, k = qst[b.u][0:KROWS, h, :], kst[b.u][0:KROWS, h, :]
            pe.matmul(p_s[h % 2][:, 0:S], q[:, P:S], k, start=True, stop=True)
            pe.matmul(p_s[h % 2][:, S:S + P], q[:, 0:P], k[:, 0:P], start=True, stop=True).then_inc(s["scored"], 1)

        def turn_max(pe, b, f):
            pe.wait_ge(s["max_ok"], 2 * H * b.n + H * (f + 1))
            flat = neg_max[b.u][:].rearrange("p h t -> p (h t)")
            pe.transpose(p_misc[0:H, 0:P], flat[:, H * f:H * (f + 1)], R.ident[:]).then_inc(s["max_turned"], 1)

        def score_t(pe, b, h):
            n = H * b.n + h
            if h % HALF == 0:
                f = h // HALF
                pe.wait_ge(max_in[b.u][f], 48 * (b.half + 1))
            wait_if(pe, s["arg_ok"], n - 1)
            q, k = qst[b.u][:, h, :], kst[b.u][:, h, :]
            pe.matmul(p_t[h % 2][:, 0:S], k[:, 0:P], q, start=True, stop=True)
            pe.matmul(p_t[h % 2][:, S:S + P], k[:, P:S], q[:, P:S], start=True, stop=True).then_inc(s["scored_t"], 1)

        def weigh(pe, b, h):
            pe.wait_ge(s["prob_ok"], H * b.n + h + 1)
            if h == 0:
                pe.wait_ge(s["v_ok"], b.n + 1)
                if isinstance(b.n, int) and b.n < 2:
                    pe.wait_ge(s["ones_ok"], 2)
                wait_if(pe, s["o_ok"], b.n - 1)
            o, pr, v = bank_o(b.u), prob[h % 4], va[b.u]
            pe.matmul(o[:, 0, h, :], pr[:, 0:P], v[:, 0, h, :], start=True, stop=True)
            pe.matmul(o[:, 1, h, :], pr[:, P:S], v[:, 0, h, :], start=True, stop=False)
            pe.matmul(o[:, 1, h, :], pr[:, S:S + P], v[:, 1, h, :], start=False, stop=True).then_inc(s["summed"], 1)

        def turn_o(pe, b):
            pe.wait_ge(s["o_ok"], b.n + 1)
            for k in range(2):
                mm = pe.transpose(p_misc[:, k * P:(k + 1) * P], o_sb[:, k, :], R.ident[:])
            mm.then_inc(s["o_turned"], 1)

        def project_o(pe, b):
            pe.wait_ge(s["o_t_ok"], b.n + 1)
            for k in range(2):
                mm = pe.matmul(p_misc[:, k * P:(k + 1) * P], o_t[:, k * P:(k + 1) * P], R.w_proj[:],
                               start=True, stop=True)
            mm.then_inc(s["projected"], 1)

        def misc_free(pe, sem_name, count):
            wait_if(pe, s[sem_name], count)

        @block.tensor
        def _(pe):
            pe.wait_ge(s["bias_in"], 32)
            for n, part_of in enumerate(bias_pieces()):
                wait_if(pe, s["bias_neg"], n - 1)
                pe.matmul(p_t[n % 2][:], R.reverse[:], part_of, start=True, stop=True).then_inc(s["bias_turned"], 1)
            pe.wait_ge(s["bias_neg"], H)
            b0, b1 = Batch(0, 0), Batch(0, 1)
            project(pe, b0)
            values(pe, b0)
            project(pe, b1)
            for h in range(H):
                score(pe, b0, h)
                if h == HALF:
                    misc_free(pe, "v_ok", 1)
                    turn_max(pe, b0, 0)
            misc_free(pe, "max_read", 2)
            turn_max(pe, b0, 1)

            def step(pe, j, c):
                b, nxt, prev = Batch(j, c), Batch(j, c + 1), Batch(j, c - 1)
                for h in range(H):
                    if has(j, c, 1):
                        score(pe, nxt, h)
                    score_t(pe, b, h)
                    if h >= 2:
                        weigh(pe, b, h - 2)
                    elif has(j, c, -1):
                        weigh(pe, prev, H - 2 + h)
                    if h == 2 and has(j, c, 2):
                        project(pe, Batch(j, c + 2))
                    if h == 3 and has(j, c, 1):
                        misc_free(pe, "max_read", 2 * (2 * b.n + 2))
                        values(pe, nxt)
                    if h == 5 and has(j, c, -1):
                        if has(j, c, 1):
                            misc_free(pe, "v_ok", b.n + 2)
                        else:
                            misc_free(pe, "max_read", 2 * (2 * b.n + 2))
                        turn_o(pe, prev)
                    if h == 8 and has(j, c, -1):
                        project_o(pe, prev)
                    if h == 11 and has(j, c, 1):
                        if has(j, c, -1):
                            misc_free(pe, "y_ok", b.n)
                        else:
                            misc_free(pe, "v_ok", b.n + 2)
                        turn_max(pe, nxt, 0)
                if has(j, c, 1):
                    misc_free(pe, "max_read", 2 * (2 * nxt.n + 1))
                    turn_max(pe, nxt, 1)
            steps(pe, step)
            last = Batch(0, B - 1)
            weigh(pe, last, H - 2)
            weigh(pe, last, H - 1)
            misc_free(pe, "y_ok", B - 1)
            turn_o(pe, last)
            project_o(pe, last)

        def read_qk(act, b):
            act.wait_ge(s["qk_mm"], b.n + 1)
            wait_if(act, s["part1"], b.n)
            wait_if(act, s["rest_ok"], b.n)
            act.activation(qk[:, 0:S], p_qk[:, 0:S], ACT.Identity, bias=R.bq_neg[:], scale=-SCALE0
                           ).then_inc(s["qk_ok"], 1)
            act.activation(qk[:, S:2 * S], p_qk[:, S:2 * S], ACT.Identity, bias=R.b_qk[:, 1:2]
                           ).then_inc(s["qk_ok"], 1)

        def read_max(act, b, f):
            act.wait_ge(s["max_turned"], 2 * b.n + f + 1)
            wait_if(act, s["max_diff"], 2 * b.n + f - 1)
            if not isinstance(b.half, int) or b.half > 0 or b.u > 0:
                pu = 1 - b.u
                prev_half = b.half if b.u else b.half - 1
                act.wait_ge(max_in[pu][f], 48 * (prev_half + 1))
            act.activation(max_f[f][:], p_misc[0:H, 0:P], ACT.Copy).then_inc(s["max_read"], 1)
            act.activation(max_part[f][:, 0, :], p_misc[0:H, 0:P], ACT.Copy).then_inc(s["max_read"], 1)

        def second_max(act, b, f):
            act.wait_ge(s["max_diff"], 2 * b.n + f + 1)
            act.activation(max_part[f][:, 1, :], max_rest[f][:], ACT.Copy).then_inc(s["max_p2"], 1)

        def exponent(act, b, h):
            n = H * b.n + h
            act.wait_ge(s["arg_ok"], n + 1)
            wait_if(act, s["summed"], n - 3)
            act.activation(prob[h % 4][:], arg[h % 4][:], ACT.Exp, scale=-1.0).then_inc(s["prob_ok"], 1)

        def copy_o(act, b):
            act.wait_ge(s["o_turned"], b.n + 1)
            wait_if(act, s["projected"], b.n)
            act.activation(o_t[:], p_misc[:, 0:S], ACT.Copy).then_inc(s["o_t_ok"], 1)

        @block.scalar
        def _(act):
            for n, part_of in enumerate(bias_pieces()):
                act.wait_ge(s["bias_turned"], n + 1)
                act.mul(part_of, p_t[n % 2][:].rearrange("p (h k) -> p h k", h=2), -1.0).then_inc(s["bias_neg"], 1)
            b0, b1 = Batch(0, 0), Batch(0, 1)
            read_qk(act, b0)
            read_qk(act, b1)
            read_max(act, b0, 0)
            second_max(act, b0, 0)

            def step(act, j, c):
                b, nxt, prev = Batch(j, c), Batch(j, c + 1), Batch(j, c - 1)
                for h in range(H):
                    if h == 0:
                        read_max(act, b, 1)
                    if h == 1:
                        second_max(act, b, 1)
                    exponent(act, b, h)
                    if h == 3 and has(j, c, 2):
                        read_qk(act, Batch(j, c + 2))
                    if h == 6 and has(j, c, -1):
                        copy_o(act, prev)
                    if h == 12 and has(j, c, 1):
                        read_max(act, nxt, 0)
                    if h == 13 and has(j, c, 1):
                        second_max(act, nxt, 0)
            steps(act, step)
            copy_o(act, Batch(0, B - 1))

        def first_part(dve, b):
            dve.wait_ge(s["qk_ok"], 2 * (b.n + 1))
            wait_if(dve, spilled[b.u], 64 * b.half)
            dve.tensor_copy(part[b.u][:, 0, :], qk[:]).then_inc(s["part1"], 1)

        def second_part(dve, b):
            dve.wait_ge(s["rest_ok"], b.n + 1)
            dve.tensor_copy(part[b.u][:, 1, :], rest[:]).then_inc(s["part2"], 1)

        def read_v(dve, b):
            dve.wait_ge(s["v_mm"], b.n + 1)
            wait_if(dve, s["summed"], H * (b.n - 1) if not isinstance(b.n, int) or b.n >= 2 else 0)
            for k in range(2):
                ins = dve.tensor_tensor(va[b.u][:, k, :, 0:HD],
                                        p_misc[:, k * P:(k + 1) * P].rearrange("p (h d) -> p h d", h=H),
                                        R.b_v[:].rearrange("p (h d) -> p h d", h=H), ALU.add)
            ins.then_inc(s["v_ok"], 1)

        def row_max_waits(dve, b, h):
            n = H * b.n + h
            dve.wait_ge(s["scored"], n + 1)
            if h == 0:
                wait_if(dve, s["max_turned"], 2 * (b.n - 1) if not isinstance(b.n, int) or b.n >= 2 else 0)
            wait_if(dve, s["max_ok"], 2 * n - 2)

        def row_max(dve, b, h):
            for t, cols, at in ((1, slice(0, S), slice(0, S)), (0, slice(S, S + P), slice(P, S))):
                r = (2 * h + 1 - t) % 4
                w = cols.stop - cols.start
                dve.tensor_tensor_reduce(out=sums[r][:, 0:w], in0=p_s[h % 2][:, cols], in1=bias_q[:, h, at],
                                         scale=1.0, scalar=3.0e38, op0=ALU.add, op1=ALU.min,
                                         accum_out=neg_max[b.u][:, h, t:t + 1]).then_inc(s["max_ok"], 1)

        def add_bias(dve, b, h):
            n = H * b.n + h
            dve.wait_ge(s["scored_t"], n + 1)
            wait_if(dve, s["prob_ok"], n - 3)
            dve.tensor_tensor(arg[h % 4][:], p_t[h % 2][:, 0:S + P], bias_k[:, h, :], ALU.add
                              ).then_inc(s["arg_ok"], 1)

        def normalise(dve, b):
            dve.wait_ge(s["summed"], H * (b.n + 1))
            dve.reciprocal(rden[:], bank_o(b.u)[:, :, :, HD]).then_inc(s["rden_ok"], 1)
            dve.wait_ge(s["rden_ok"], b.n + 1)
            wait_if(dve, s["o_turned"], b.n)
            for k in range(2):
                ins = dve.tensor_tensor(o_sb[:, k, :].rearrange("p (h d) -> p h d", h=H),
                                        bank_o(b.u)[:, k, :, 0:HD],
                                        rden[:, k, :].unsqueeze(2).to_broadcast([P, H, HD]), ALU.mult)
            ins.then_inc(s["o_ok"], 1)

        def residual(dve, b):
            dve.wait_ge(s["projected"], b.n + 1)
            dve.wait_ge(s["resid_ok"], b.n + 1)
            wait_if(dve, s["yn_ok"], 2 * b.n)
            dve.tensor_tensor(y[:], p_misc[:, 0:S].rearrange("p (t d) -> p t d", t=2), resid[:], ALU.add
                              ).then_inc(s["y_ok"], 1)
            dve.wait_ge(s["y_ok"], b.n + 1)
            for k in range(2):
                dve.bn_stats(stats[:, k, :], y[:, k, :]).then_inc(s["stats_ok"], 1)

        def aggregate(dve, b):
            for k in range(2):
                dve.bn_aggr(mean_var[:, k, :], stats[:, k, :]).then_inc(s["mv_ok"], 1)

        def centre(dve, b):
            dve.wait_ge(s["rstd_ok"], b.n + 1)
            wait_if(dve, s["yg_ok"], b.n)
            for k in range(2):
                dve.tensor_scalar(yn[:, k, :], y[:, k, :], mean_var[:, k, 0:1], rstd[:, k:k + 1],
                                  ALU.subtract, ALU.mult).then_inc(s["yn_ok"], 1)

        @block.vector
        def _(dve):
            for u in range(2):
                dve.memset(kst[u][64:MROWS, :, :], -1.0).then_inc(s["rows_ok"], 1)
            b0, b1 = Batch(0, 0), Batch(0, 1)
            first_part(dve, b0)
            read_v(dve, b0)
            second_part(dve, b0)
            first_part(dve, b1)
            second_part(dve, b1)
            dve.wait_ge(s["bias_ok"], 3)
            for h in range(H):
                row_max_waits(dve, b0, h)
                row_max(dve, b0, h)

            def step(dve, j, c):
                b, nxt, prev = Batch(j, c), Batch(j, c + 1), Batch(j, c - 1)
                for h in range(H):
                    if has(j, c, 1):
                        row_max_waits(dve, nxt, h)
                    if h == 10 and has(j, c, -1):
                        dve.wait_ge(s["stats_ok"], 2 * prev.n + 2)
                        wait_if(dve, s["eps_ok"], prev.n)
                    add_bias(dve, b, h)
                    if has(j, c, 1):
                        row_max(dve, nxt, h)
                    if h == 2 and has(j, c, -1):
                        normalise(dve, prev)
                    if h == 4 and has(j, c, 2):
                        first_part(dve, Batch(j, c + 2))
                    if h == 4 and has(j, c, 1):
                        read_v(dve, nxt)
                    if h == 7 and has(j, c, 2):
                        second_part(dve, Batch(j, c + 2))
                    if h == 9 and has(j, c, -1):
                        residual(dve, prev)
                    if h == 10 and has(j, c, -1):
                        aggregate(dve, prev)
                    if h == 13 and has(j, c, -1):
                        centre(dve, prev)
            steps(dve, step)
            last = Batch(0, B - 1)
            normalise(dve, last)
            residual(dve, last)
            dve.wait_ge(s["stats_ok"], 2 * B)
            dve.wait_ge(s["eps_ok"], B - 1)
            aggregate(dve, last)
            centre(dve, last)

        def take_first(pool, b):
            pool.wait_ge(s["part1"], b.n + 1)
            wait_if(pool, s["part3"], b.n)
            wait_if(pool, s["part2"], b.n)
            pool.tensor_tensor(rest[:], qk[:], part[b.u][:, 0, :], ALU.subtract).then_inc(s["rest_ok"], 1)

        def third_part(pool, b):
            pool.wait_ge(s["part2"], b.n + 1)
            pool.tensor_tensor(part[b.u][:, 2, :], rest[:], part[b.u][:, 1, :], ALU.subtract
                               ).then_inc(s["part3"], 1)

        def max_diff(pool, b, f):
            pool.wait_ge(s["max_read"], 2 * (2 * b.n + f + 1))
            wait_if(pool, s["max_p3"], 2 * b.n + f - 1)
            pool.tensor_tensor(max_rest[f][:], max_f[f][:], max_part[f][:, 0, :], ALU.subtract
                               ).then_inc(s["max_diff"], 1)

        def third_max(pool, b, f):
            pool.wait_ge(s["max_p2"], 2 * b.n + f + 1)
            pool.tensor_tensor(max_part[f][:, 2, :], max_rest[f][:], max_part[f][:, 1, :], ALU.subtract
                               ).then_inc(s["max_p3"], 1)

        def prepare_residual(pool, b):
            wait_if(pool, s["y_ok"], b.n)
            pool.tensor_tensor(resid[:], R.xn[:, bass.ds(2 * b.n, 2), :],
                               R.b_proj[:].unsqueeze(1).to_broadcast([P, 2, P]), ALU.add).then_inc(s["resid_ok"], 1)

        def inverse_std(pool, b):
            pool.wait_ge(s["mv_ok"], 2 * (b.n + 1))
            pool.tensor_tensor(var_eps[:], mean_var[:, :, 1], R.eps[:, 0:2], ALU.add).then_inc(s["eps_ok"], 1)
            pool.wait_ge(s["eps_ok"], b.n + 1)
            wait_if(pool, s["yn_ok"], 2 * b.n)
            pool.tensor_tensor(rstd[:], var_eps[:], R.neg_half[:, 0:2], ALU.pow).then_inc(s["rstd_ok"], 1)

        def affine(pool, b):
            pool.wait_ge(s["yn_ok"], 2 * (b.n + 1))
            wait_if(pool, s["s_ok"], b.n)
            pool.tensor_tensor(yg[:], yn[:], R.ln_g[:].unsqueeze(1).to_broadcast([P, 2, P]), ALU.mult
                               ).then_inc(s["yg_ok"], 1)
            pool.wait_ge(s["yg_ok"], b.n + 1)
            pool.tensor_tensor(R.s[:, bass.ds(2 * b.n, 2), :], yg[:], R.ln_b[:].unsqueeze(1).to_broadcast([P, 2, P]),
                               ALU.add).then_inc(s["s_ok"], 1)

        @block.gpsimd
        def _(pool):
            for u in range(2):
                pool.memset(va[u][:, :, :, HD], 1.0).then_inc(s["ones_ok"], 1)
            pool.wait_ge(s["bias_neg"], H)
            pool.affine_select(out=bias_q[:, :, P:S], in_=bias_q[:, :, P:S], compare_op=ALU.is_ge, fill=BIG, base=0,
                               pattern=[[0, H], [-1, P]], channel_multiplier=1).then_inc(s["bias_ok"], 1)
            pool.affine_select(out=bias_k[:, :, 0:P], in_=bias_k[:, :, 0:P], compare_op=ALU.is_ge, fill=BIG, base=0,
                               pattern=[[0, H], [1, P]], channel_multiplier=-1).then_inc(s["bias_ok"], 1)
            pool.wait_ge(s["bias_ok"], 2)
            pool.tensor_copy(bias_k[:, :, S:S + P], bias_k[:, :, 0:P]).then_inc(s["bias_ok"], 1)
            b0, b1 = Batch(0, 0), Batch(0, 1)
            for b in (b0, b1):
                take_first(pool, b)
                third_part(pool, b)
            max_diff(pool, b0, 0)
            third_max(pool, b0, 0)

            def step(pool, j, c):
                b, nxt, prev = Batch(j, c), Batch(j, c + 1), Batch(j, c - 1)
                if isinstance(j, int):
                    n = c if c < 2 else c - B + 4
                    scatter(pool, R, D, 0, range(NT // 4 * n, NT // 4 * (n + 1)))
                max_diff(pool, b, 1)
                third_max(pool, b, 1)
                if has(j, c, 2):
                    take_first(pool, Batch(j, c + 2))
                    third_part(pool, Batch(j, c + 2))
                if has(j, c, -1):
                    prepare_residual(pool, prev)
                    inverse_std(pool, prev)
                    affine(pool, prev)
                if has(j, c, 1):
                    max_diff(pool, nxt, 0)
                    third_max(pool, nxt, 0)
            steps(pool, step)
            last = Batch(0, B - 1)
            prepare_residual(pool, last)
            inverse_std(pool, last)
            affine(pool, last)


def attention1(nc, R, D, f):
    tag = "a1_"
    with ExitStack() as ctx:
        sem = Sems(nc, ctx)
        ctx.callback(sem.done)

        def sb(name, shape, dt=F32):
            return ctx.enter_context(nc.sbuf_tensor(tag + name, shape, dt))

        def ps(name):
            return ctx.enter_context(nc.psum_tensor(tag + name, [P, 512], F32))

        cos_sin = sb("cos_sin", [P, 2, 2 * S])
        decay = sb("decay", [P, 2, S])
        xs = [sb(f"xs{u}", [P, S]) for u in range(2)]
        along = sb("along", [P, 2 * S])
        across = sb("across", [P, 2 * S])
        qk = [sb(f"qk{u}", [P, 2 * S]) for u in range(2)]
        v = [sb(f"v{u}", [P, 2, P]) for u in range(2)]
        neg_max = sb("neg_max", [P, 2])
        total, rden = sb("total", [P, 2]), [sb(f"rden{u}", [P, 2]) for u in range(2)]
        prob, decayed = sb("prob", [P, 2, S]), sb("decayed", [P, 2, S])
        prob_t = [sb(f"prob_t{u}", [P, 2, S]) for u in range(2)]
        p_a, p_b, p_v = ps("p_a"), ps("p_b"), ps("p_v")
        p_s = [ps(f"p_s{u}") for u in range(2)]
        p_p = [ps(f"p_p{u}") for u in range(2)]
        p_o = ps("p_o")
        s = {n: sem(tag + n) for n in (
            "tables_in", "qk_mm", "along_ok", "across_ok", "qk_ok", "v_mm", "v_ok", "scored", "max_ok", "prob_ok",
            "decayed_ok", "turned", "turned_ok", "summed", "rden_ok", "s_ok", "shared_in")}
        xs_in = sem.pair(tag + "xs_in")
        block = ctx.enter_context(nc.Block())

        def steps(eng, do):
            do(eng, 0, 0)
            do(eng, 0, 1)
            with eng.Fori(1, B // 2 - 1) as j:
                do(eng, j, 0)
                do(eng, j, 1)
            do(eng, 0, B - 2)
            do(eng, 0, B - 1)

        def has(j, c, ahead):
            return not isinstance(j, int) or 0 <= c + ahead < B

        @block.sync
        def _(sp):
            sem.clear_old(sp)
            sp.dma_start(cos_sin[:], D["cos_sin"]).then_inc(s["tables_in"], 16)
            sp.dma_start(decay[:], D["decay"].rearrange("(t p) k -> p t k", p=P)).then_inc(s["tables_in"], 16)
            sp.dma_start(f.shared[:], D["slots_out"][1][0:B * S, :].rearrange("(t p) d -> p t d", p=P)
                         ).then_inc(s["shared_in"], 16)

            def step(sp, j, c):
                b = Batch(j, c)
                wait_if(sp, s["v_mm"], b.n - 1)
                sp.dma_start(xs[b.u][:], R.xt[:, bass.ds(S * b.n, S)]).then_inc(xs_in[b.u], 16)
            steps(sp, step)
            sp.wait_ge(s["shared_in"], 16)

        def project(pe, b):
            pe.wait_ge(xs_in[b.u], 16 * (b.half + 1))
            wait_if(pe, s["along_ok"], b.n)
            wait_if(pe, s["across_ok"], b.n)
            for bank, at in ((p_a, 0), (p_b, 2)):
                for k in range(2):
                    mm = pe.matmul(bank[:, k * S:(k + 1) * S], R.w_x1[:, (at + k) * P:(at + k + 1) * P], xs[b.u][:],
                                   start=True, stop=True)
            mm.then_inc(s["qk_mm"], 1)
            wait_if(pe, s["v_ok"], b.n)
            for k in range(2):
                mm = pe.matmul(p_v[:, k * P:(k + 1) * P], xs[b.u][:, k * P:(k + 1) * P], R.w_x1[:, 4 * P:5 * P],
                               start=True, stop=True)
            mm.then_inc(s["v_mm"], 1)

        def score(pe, b):
            pe.wait_ge(s["qk_ok"], b.n + 1)
            wait_if(pe, s["prob_ok"], 2 * (b.n - 1))
            for k in range(2):
                mm = pe.matmul(p_s[b.u][:, k * S:(k + 1) * S], qk[b.u][:, k * P:(k + 1) * P], qk[b.u][:, S:2 * S],
                               start=True, stop=True)
            mm.then_inc(s["scored"], 1)

        def turn(pe, b):
            pe.wait_ge(s["decayed_ok"], b.n + 1)
            wait_if(pe, s["turned_ok"], b.n - 1)
            for k in range(2):
                for q in range(2):
                    mm = pe.transpose(p_p[b.u][:, k * S + q * P:k * S + (q + 1) * P],
                                      decayed[:, q, k * P:(k + 1) * P], R.ident[:])
            mm.then_inc(s["turned"], 1)

        def weigh(pe, b):
            pe.wait_ge(s["turned_ok"], b.n + 1)
            pe.wait_ge(s["v_ok"], b.n + 1)
            wait_if(pe, s["s_ok"], 2 * b.n)
            for q in range(2):
                for k in range(2):
                    mm = pe.matmul(p_o[:, q * P:(q + 1) * P], prob_t[b.u][:, k, q * P:(q + 1) * P], v[b.u][:, k, :],
                                   start=(k == 0), stop=(k == 1))
            mm.then_inc(s["summed"], 1)

        @block.tensor
        def _(pe):
            project(pe, Batch(0, 0))

            def step(pe, j, c):
                b = Batch(j, c)
                score(pe, b)
                if has(j, c, -1):
                    turn(pe, Batch(j, c - 1))
                if has(j, c, 1):
                    project(pe, Batch(j, c + 1))
                if has(j, c, -1):
                    weigh(pe, Batch(j, c - 1))
            steps(pe, step)
            turn(pe, Batch(0, B - 1))
            weigh(pe, Batch(0, B - 1))

        @block.vector
        def _(dve):
            def rotate(dve, b):
                dve.wait_ge(s["qk_mm"], b.n + 1)
                wait_if(dve, s["qk_ok"], b.n)
                dve.tensor_tensor(along[:], p_a[:], cos_sin[:, 0, :], ALU.mult).then_inc(s["along_ok"], 1)
                dve.tensor_tensor(across[:], p_b[:], cos_sin[:, 1, :], ALU.mult).then_inc(s["across_ok"], 1)

            def add_across(dve, b):
                dve.wait_ge(s["across_ok"], b.n + 1)
                wait_if(dve, s["scored"], b.n - 1)
                dve.tensor_tensor(qk[b.u][:], along[:], across[:], ALU.add).then_inc(s["qk_ok"], 1)

            def row_max(dve, b):
                dve.wait_ge(s["scored"], b.n + 1)
                wait_if(dve, s["prob_ok"], 2 * b.n)
                dve.tensor_reduce(neg_max[:], p_s[b.u][:].rearrange("p (t k) -> p t k", t=2), X, ALU.max,
                                  negate=True).then_inc(s["max_ok"], 1)

            def decay_it(dve, b):
                dve.wait_ge(s["prob_ok"], 2 * (b.n + 1))
                wait_if(dve, s["turned"], b.n)
                dve.tensor_tensor(decayed[:], prob[:], decay[:], ALU.mult).then_inc(s["decayed_ok"], 1)
                wait_if(dve, s["s_ok"], 2 * (b.n - 1))
                dve.reciprocal(rden[b.u][:], total[:]).then_inc(s["rden_ok"], 1)

            dve.wait_ge(s["tables_in"], 32)
            rotate(dve, Batch(0, 0))
            add_across(dve, Batch(0, 0))

            def step(dve, j, c):
                b = Batch(j, c)
                row_max(dve, b)
                if has(j, c, 1):
                    rotate(dve, Batch(j, c + 1))
                    add_across(dve, Batch(j, c + 1))
                decay_it(dve, b)
            steps(dve, step)

        @block.gpsimd
        def _(pool):
            for t in range(NT):
                for n in range(2):
                    pool.indirect_dma_start(f.top[n][:, t, :], None, D["slots_out"][1],
                                            bass.IndirectOffsetOnAxis(ap=R.pos[n][:, t:t + 1], axis=0)
                                            ).then_inc(R.gathered, 16)
            pool.wait_ge(R.gathered, 16 * 2 * NT)

        @block.scalar
        def _(act):
            def read_v(act, b):
                act.wait_ge(s["v_mm"], b.n + 1)
                wait_if(act, s["summed"], b.n - 1)
                act.activation(v[b.u][:].rearrange("p t d -> p (t d)"), p_v[:, 0:S], ACT.Copy).then_inc(s["v_ok"], 1)

            def exponent(act, b):
                act.wait_ge(s["max_ok"], b.n + 1)
                wait_if(act, s["decayed_ok"], b.n)
                wait_if(act, s["rden_ok"], b.n)
                for k in range(2):
                    act.activation(prob[:, k, :], p_s[b.u][:, k * S:(k + 1) * S], ACT.Exp, bias=neg_max[:, k:k + 1],
                                   accum_out=total[:, k:k + 1]).then_inc(s["prob_ok"], 1)

            def read_turned(act, b):
                act.wait_ge(s["turned"], b.n + 1)
                wait_if(act, s["summed"], b.n - 1)
                act.activation(prob_t[b.u][:].rearrange("p t k -> p (t k)"), p_p[b.u][:], ACT.Copy
                               ).then_inc(s["turned_ok"], 1)

            def out(act, b):
                act.wait_ge(s["summed"], b.n + 1)
                act.wait_ge(s["rden_ok"], b.n + 1)
                for k in range(2):
                    act.activation(R.s[:, 2 * b.n + k, :], p_o[:, k * P:(k + 1) * P], ACT.Copy,
                                   scale=rden[b.u][:, k:k + 1]).then_inc(s["s_ok"], 1)

            read_v(act, Batch(0, 0))

            def step(act, j, c):
                b = Batch(j, c)
                exponent(act, b)
                if has(j, c, -1):
                    read_turned(act, Batch(j, c - 1))
                if has(j, c, 1):
                    read_v(act, Batch(j, c + 1))
                if has(j, c, -1):
                    out(act, Batch(j, c - 1))
            steps(act, step)
            read_turned(act, Batch(0, B - 1))
            out(act, Batch(0, B - 1))


class Resident:

    def __init__(self, nc, ctx):
        def sem(name):
            return ctx.enter_context(nc.semaphore("k_" + name))

        self.scattered, self.gathered = sem("scattered"), sem("gathered")
        self.arrived = [sem(f"arrived{r}") for r in range(8)]

        def sb(name, shape, dt=F32):
            return ctx.enter_context(nc.sbuf_tensor("k_" + name, shape, dt))

        self.x, self.xn, self.s = sb("x", [P, NT, P]), sb("xn", [P, NT, P]), sb("s", [P, NT, P])
        self.xt = sb("xt", [P, B * S])
        self.gate_w = [sb(f"gate_w{n}", [P, E]) for n in range(2)]
        self.gb, self.rb = sb("gb", [P, E]), sb("rb", [P, E])
        self.w_qkv, self.b_qk, self.b_v = sb("w_qkv", [P, 3 * P]), sb("b_qk", [P, 2]), sb("b_v", [P, P])
        self.bq_neg = sb("bq_neg", [P, 1])
        self.w_proj, self.b_proj = sb("w_proj", [P, P]), sb("b_proj", [P, P])
        self.ln_g, self.ln_b = sb("ln_g", [P, P]), sb("ln_b", [P, P])
        self.w_x1 = sb("w_x1", [P, 5 * P])
        self.ident, self.reverse = sb("ident", [P, P]), sb("reverse", [P, P])
        self.ones_bf, self.upper_bf = sb("ones_bf", [P, P], BF16), sb("upper_bf", [P, P], BF16)
        self.neg_half, self.eps, self.zero32 = sb("neg_half", [P, GT]), sb("eps", [P, GT]), sb("zero32", [P, NT])
        self.expert_m8, self.tile_start = sb("expert_m8", [P, E]), sb("tile_start", [P, B * S // SLOTS])
        self.tile_no = sb("tile_no", [P, ROUTED1])
        self.logits = sb("logits", [P, NT, E])
        self.weight = [sb(f"weight{n}", [P, NT]) for n in range(2)]
        self.pos = [sb(f"pos{n}", [P, NT], I32) for n in range(2)]
        self.tile_expert = sb("tile_expert", [1, TILES], I32)


def build(nc, D):
    D["slots_in"] = nc.dram_tensor("slots_in", [TILES * SLOTS, P], F32, kind="Internal").ap()
    D["slots_out"] = [nc.dram_tensor(f"slots_out{n}", [tiles * SLOTS, P], F32, kind="Internal").ap()
                      for n, tiles in enumerate((ROUTED0, TILES))]
    D["parts"] = nc.dram_tensor("parts", [2 * PARTS * 2 * P, S], BF16, kind="Internal").ap()
    Sems.before = None
    with ExitStack() as ctx:
        R = Resident(nc, ctx)
        build_constants(nc, R, D)
        layer_norm_gate(nc, R, D, 0)
        route(nc, R, D, 0)
        attention0(nc, R, D)
        experts(nc, R, D, 0)
        combine0(nc, R, D)
        layer_norm_gate(nc, R, D, 1)
        route(nc, R, D, 1)
        experts(nc, R, D, 1)
        f = Gathered(nc, ctx)
        attention1(nc, R, D, f)
        combine1(nc, R, D, f)


def xpos_tables():
    f = np.float32
    scale_vec = (np.arange(0, P, 2, dtype=f) + f(0.4 * P)) / f(1.4 * P)
    scale = scale_vec[None, :] ** (np.arange(S, dtype=f) / f(512.0))[:, None]
    inv_freq = f(1.0) / f(10000.0) ** (np.arange(P // 2, dtype=f) / f(P // 2))
    angle = np.arange(S, dtype=f)[:, None] * inv_freq[None, :]
    sign = np.where(np.arange(P) % 2 == 0, f(-1), f(1))
    out = np.zeros((P, 2, 2 * S), f)
    for k, sc in enumerate((scale, f(1.0) / scale)):
        out[:, 0, k * S:(k + 1) * S] = np.repeat(np.cos(angle) * sc, 2, axis=-1).T
        out[:, 1, k * S:(k + 1) * S] = (np.repeat(np.sin(angle) * sc, 2, axis=-1) * sign).T
    return out


def kernel(**inputs):
    import concourse.bacc as _bacc
    from concourse.bass_utils import run_bass_kernel_spmd as _run

    a = {k: np.asarray(v) for k, v in inputs.items()}
    by_part = a["L0_attn_W_w"].reshape(3, 2, HALF, HD, P)
    w_q, w_k = (by_part[n].transpose(3, 0, 2, 1).reshape(P, P) for n in range(2))
    w_v = a["L0_attn_W_w"][2 * P:].T
    b_part = a["L0_attn_W_b"].reshape(3, 2, HALF, HD)
    swap = np.arange(P) ^ 1
    wq1, wk1, wv1 = a["L1_attn_W_Q"], a["L1_attn_W_K"], a["L1_attn_W_V"]
    rpb_t = a["L0_attn_rpb"].T
    step = np.arange(S)
    arrays = {
        "x": a["L0_attn_x"].reshape(B * S, P),
        "gate_W": a["L0_ffn_gate_W"], "gate_b": a["L0_ffn_gate_b"], "Wr": a["L1_ffn_Wr"], "rb": a["L1_ffn_rb"],
        "w_qkv": np.concatenate([w_q, w_k, w_v], axis=1),
        "b_qk": np.stack([b_part[n].transpose(0, 2, 1).reshape(P) for n in range(2)], axis=1),
        "b_v": a["L0_attn_W_b"][2 * P:], "w_proj": a["L0_attn_proj_w"].T, "b_proj": a["L0_attn_proj_b"],
        "ln_g": a["L0_attn_ln_g"], "ln_b": a["L0_attn_ln_b"],
        "rpbT": rpb_t, "rpbR": rpb_t[:, ::-1],
        "W1": a["L0_ffn_W1"], "W2": a["L0_ffn_W2"], "b2": a["L0_ffn_b2"],
        "b1T": a["L0_ffn_b1"].reshape(E, F0 // P, P).transpose(0, 2, 1),
        "M1": np.concatenate([a["L1_ffn_W1"], a["L1_ffn_Ws1"][None]]),
        "M2": np.concatenate([a["L1_ffn_W2"], a["L1_ffn_Ws2"][None]]),
        "M3": np.concatenate([a["L1_ffn_W3"], a["L1_ffn_Ws3"][None]]),
        "w_x1": np.concatenate([wq1, wk1, wq1[:, swap], wk1[:, swap], wv1], axis=1),
        "cos_sin": xpos_tables(),
        "decay": np.float32(0.9) ** np.abs(step[:, None] - step[None, :]).astype(np.float32),
    }
    arrays = {k: np.ascontiguousarray(v) for k, v in arrays.items()}
    nc = _bacc.Bacc("TRN2", target_bir_lowering=False, num_devices=1)
    D = {k: nc.dram_tensor("in_" + k, v.shape, mybir.dt.from_np(v.dtype), kind="ExternalInput").ap()
         for k, v in arrays.items()}
    D["out"] = nc.dram_tensor("out_0", (B * S, P), F32, kind="ExternalOutput").ap()
    build(nc, D)
    r = _run(nc, [{"in_" + k: v for k, v in arrays.items()}], core_ids=[0])
    return r.results[0]["out_0"].reshape(B, S, P)
```

```python
from contextlib import ExitStack

import numpy as np

import concourse.bass as bass
from concourse import mybir

F32 = mybir.dt.float32
BF16 = mybir.dt.bfloat16
I32 = mybir.dt.int32
ALU = mybir.AluOpType
ACT = mybir.ActivationFunctionType
X = mybir.AxisListType.X

P = 128
B, S = 16, 256
NT = B * S // P
GT = 4
NG = NT // GT
H, HD = 16, 8
E = 8
F0 = 512
F1 = 256
SLOTS = 256
SHARED = B * S // SLOTS
ROUTED0 = (B * S + E * (SLOTS - 1)) // SLOTS
ROUTED1 = (2 * B * S + E * (SLOTS - 1)) // SLOTS
AHEAD = (6, 8)
ROUTED0 += -ROUTED0 % AHEAD[0]
ROUTED1 += -(SHARED + ROUTED1) % AHEAD[1]
TILES = SHARED + ROUTED1
LN_EPS = 1e-5
BIG = 1e30
PARTS = 3
OROWS = P // 2 + H // 2
KROWS = PARTS * PARTS * HD
MROWS = KROWS + PARTS
LAG = 3
HALF = H // 2
SCALE0 = float(1.0 / np.sqrt(np.float32(P)))
SCALE1 = 1.0 / float(np.sqrt(P))


class Sems:

    before = None

    def __init__(self, nc, _):
        self.nc, self.stack, self.all = nc, ExitStack(), []
        self.old, Sems.before = Sems.before, self

    def __call__(self, name):
        self.all.append(self.stack.enter_context(self.nc.semaphore(name)))
        return self.all[-1]

    def pair(self, name):
        return [self(f"{name}{u}") for u in range(2)]

    def clear_old(self, sp):
        for one in self.old.all if self.old else ():
            sp.sem_clear(one)

    def done(self):
        if self.old:
            self.old.stack.close()


class Bias:

    def __init__(self, nc, ctx):
        self.q = ctx.enter_context(nc.sbuf_tensor("bias_q", [P, H, S], F32))
        self.k = ctx.enter_context(nc.sbuf_tensor("bias_k", [P, H, S + P], F32))

    def piece_q(self, n):
        return self.q[:, 2 * n:2 * n + 2, :]

    def piece_k(self, n):
        return self.k[:, bass.ds(2 * n, 2), 0:S]


def build_constants(nc, R, D, bias):
    with ExitStack() as ctx:
        sem = Sems(nc, ctx)
        ctx.callback(sem.done)
        stats = ctx.enter_context(nc.sbuf_tensor("c_stats", [P, NT, 6], F32))
        loaded, x_in, flags, tables = sem("c_loaded"), sem("c_x_in"), sem("c_flags"), sem("c_tables")
        bias_in, stats_ok, mv_ok = sem("c_bias_in"), sem("c_stats_ok"), sem("c_mv_ok")
        eps_ok, rstd_ok = sem("c_eps_ok"), sem("c_rstd_ok")
        bias_turned, bias_neg, reverse_ok = sem("c_bias_turned"), sem("c_bias_neg"), sem("c_reverse_ok")
        bank = [ctx.enter_context(nc.psum_tensor(f"c_bank{u}", [P, 512], F32)) for u in range(2)]
        block = ctx.enter_context(nc.Block())

        loads = [(R.gate_w[0][:], D["gate_W"]), (R.gate_w[1][:], D["Wr"]),
                 (R.gb[:], bass.AP(tensor=D["gate_b"].tensor, offset=0, ap=[[0, P], [1, E]])),
                 (R.rb[:], bass.AP(tensor=D["rb"].tensor, offset=0, ap=[[0, P], [1, E]])),
                 (R.w_qkv[:], D["w_qkv"]), (R.b_qk[:], D["b_qk"]),
                 (R.b_v[:], bass.AP(tensor=D["b_v"].tensor, offset=0, ap=[[0, P], [1, P]])),
                 (R.w_proj[:], D["w_proj"].rearrange("(f r) m -> r f m", f=2)),
                 (R.b_proj[:], bass.AP(tensor=D["b_proj"].tensor, offset=0, ap=[[0, P], [1, P]])),
                 (R.ln_g[:], bass.AP(tensor=D["ln_g"].tensor, offset=0, ap=[[0, P], [1, P]])),
                 (R.ln_b[:], bass.AP(tensor=D["ln_b"].tensor, offset=0, ap=[[0, P], [1, P]])),
                 (R.w_x1[:], D["w_x1"])]

        @block.sync
        def _(sp):
            sem.clear_old(sp)
            sp.dma_start(R.x[:], D["x"].rearrange("(t p) d -> p t d", p=P)).then_inc(x_in, 16)
            sp.dma_start(bias.q[:], bass.AP(tensor=D["rpbT"].tensor, offset=0,
                                            ap=[[1, P], [2 * S - 1, H], [1, S]])).then_inc(bias_in, 16)
            sp.dma_start(bias.k[:, :, 0:S], bass.AP(tensor=D["rpbR"].tensor, offset=P,
                                                    ap=[[1, P], [2 * S - 1, H], [1, S]])).then_inc(bias_in, 16)
            for dst, src in loads:
                sp.dma_start(dst, src).then_inc(loaded, 16)
            sp.wait_ge(loaded, 16 * len(loads))

        @block.gpsimd
        def _(pool):
            pool.memset(R.zeros[:], 0.0).then_inc(tables, 1)
            pool.memset(R.ident[:], 0.0).then_inc(flags, 1)
            pool.memset(R.ones_bf[:], 1.0).then_inc(flags, 1)
            pool.memset(R.reverse[:], 0.0).then_inc(flags, 1)
            pool.memset(R.neg_half[:], -0.5).then_inc(flags, 1)
            pool.memset(R.eps[:], LN_EPS).then_inc(flags, 1)
            pool.wait_ge(flags, 5)
            pool.affine_select(out=R.ident[:], in_=R.ident[:], compare_op=ALU.not_equal, fill=1.0, base=0,
                               pattern=[[-1, P]], channel_multiplier=1).then_inc(flags, 1)
            pool.affine_select(out=R.reverse[:], in_=R.reverse[:], compare_op=ALU.not_equal, fill=1.0, base=1 - P,
                               pattern=[[1, P]], channel_multiplier=1).then_inc(flags, 1)
            pool.wait_ge(flags, 7)
            pool.sem_inc(reverse_ok, 1)
            pool.affine_select(out=R.upper_bf[:], in_=R.ones_bf[:], compare_op=ALU.is_gt, fill=0.0, base=0,
                               pattern=[[1, P]], channel_multiplier=-1).then_inc(flags, 1)
            pool.iota(R.expert_m8[:], [[1, E]], base=-E, channel_multiplier=0,
                      allow_small_or_imprecise_dtypes=True).then_inc(tables, 1)
            pool.iota(R.tile_start[:], [[SLOTS, S * B // SLOTS]], base=0, channel_multiplier=0,
                      allow_small_or_imprecise_dtypes=True).then_inc(tables, 1)
            pool.iota(R.tile_no[:], [[1, ROUTED1]], base=0, channel_multiplier=0,
                      allow_small_or_imprecise_dtypes=True).then_inc(tables, 1)

            row_rstd(pool, R, mv_ok, eps_ok, rstd_ok)

        @block.tensor
        def _(pe):
            pe.wait_ge(bias_in, 32)
            pe.wait_ge(reverse_ok, 1)
            for n in range(H // 2):
                wait_if(pe, bias_neg, n - 1)
                pe.matmul(bank[n % 2][:], R.reverse[:], bias.piece_q(n), start=True, stop=True
                          ).then_inc(bias_turned, 1)

        @block.scalar
        def _(act):
            for n in range(H // 2):
                act.wait_ge(bias_turned, n + 1)
                act.mul(bias.piece_q(n), bank[n % 2][:].rearrange("p (h k) -> p h k", h=2), -1.0).then_inc(bias_neg, 1)

        @block.vector
        def _(dve):
            dve.memset(R.zero32[:], 0.0)
            dve.wait_ge(x_in, 16)
            with dve.Fori(0, NG) as g:
                for k in range(GT):
                    dve.bn_stats(stats[:, bass.ds(GT * g + k, 1), :], R.x[:, GT * g + k, :]).then_inc(stats_ok, 1)
            dve.wait_ge(stats_ok, NT)
            for t in range(NT):
                dve.bn_aggr(R.mean_var[:, t, :], stats[:, t, :]).then_inc(mv_ok, 1)
            dve.wait_ge(loaded, 16 * len(loads))
            dve.tensor_scalar(R.bq_neg[:], R.b_qk[:, 0:1], -SCALE0, None, ALU.mult)


def wait_if(eng, sem, value):
    if not isinstance(value, int) or value > 0:
        eng.wait_ge(sem, value)


def pairs_of_groups(eng, pair):
    pair(eng, 0)
    with eng.Fori(1, NG // 2) as j:
        pair(eng, j)


def row_rstd(pool, R, mv_ok, eps_ok, rstd_ok):
    pool.wait_ge(mv_ok, NT)
    pool.tensor_tensor(R.var_eps[:], R.mean_var[:, :, 1], R.eps[:].to_broadcast([P, NT]), ALU.add).then_inc(eps_ok, 1)
    pool.wait_ge(eps_ok, 1)
    pool.tensor_tensor(R.rstd[:], R.var_eps[:], R.neg_half[:].to_broadcast([P, NT]), ALU.pow).then_inc(rstd_ok, 1)


def layer_norm_gate(nc, R, D, bias):
    tag = "n0_"
    with ExitStack() as ctx:
        sem = Sems(nc, ctx)
        ctx.callback(sem.done)

        def sb(name, shape, dt=F32):
            return ctx.enter_context(nc.sbuf_tensor(tag + name, shape, dt))

        xn = [sb(f"xn{u}", [P, GT, P]) for u in range(2)]
        xt = [sb(f"xt{u}", [P, GT * P]) for u in range(2)]
        pt = [ctx.enter_context(nc.psum_tensor(f"{tag}pt{u}", [P, GT * P], F32)) for u in range(2)]
        pg = [ctx.enter_context(nc.psum_tensor(f"{tag}pg{u}", [P, 512], F32)) for u in range(2)]
        bank = [ctx.enter_context(nc.psum_tensor(f"{tag}bank{u}", [P, 512], F32)) for u in range(2)]
        xn_ok = sem.pair(tag + "xn_ok")
        bias_turned, bias_neg = sem.pair(tag + "bias_turned"), sem.pair(tag + "bias_neg")
        turned, xt_ok = sem.pair(tag + "turned"), sem.pair(tag + "xt_ok")
        gated, logits_ok = sem.pair(tag + "gated"), sem.pair(tag + "logits_ok")
        xn_kept, xt_kept = sem.pair(tag + "xn_kept"), sem.pair(tag + "xt_kept")
        block = ctx.enter_context(nc.Block())

        @block.sync
        def _(sp):
            sem.clear_old(sp)
            def pair(sp, j):
                for u in range(2):
                    g = 2 * j + u
                    wait_if(sp, xn_ok[u], GT * (j + 1))
                    sp.dma_start(R.xn[:, bass.ds(GT * g, GT), :], xn[u][:]).then_inc(xn_kept[u], 16)
                    wait_if(sp, xt_ok[u], j + 1)
                    sp.dma_start(R.xt[:, bass.ds(GT * P * g, GT * P)], xt[u][:]).then_inc(xt_kept[u], 16)
            pairs_of_groups(sp, pair)
            for u in range(2):
                sp.wait_ge(xn_kept[u], 16 * (NG // 2))
                sp.wait_ge(xt_kept[u], 16 * (NG // 2))

        @block.vector
        def _(dve):
            def centre(dve, j):
                for u in range(2):
                    wait_if(dve, turned[u], j)
                    wait_if(dve, xn_kept[u], 16 * j)
                    for k in range(GT):
                        t = GT * (2 * j + u) + k
                        dve.tensor_scalar(xn[u][:, k, :], R.x[:, t, :], R.mean_var[:, t, 0:1],
                                          R.rstd[:, bass.ds(t, 1)], ALU.subtract, ALU.mult).then_inc(xn_ok[u], 1)

            def logits(dve, j):
                for u in range(2):
                    g = 2 * j + u
                    wait_if(dve, gated[u], j + 1)
                    got = pg[u][:, 0:GT * E].rearrange("p (k e) -> p k e", e=E)
                    dve.tensor_tensor(R.logits[:, bass.ds(GT * g, GT), :], got,
                                      R.gb[:].unsqueeze(1).to_broadcast([P, GT, E]), ALU.add
                                      ).then_inc(logits_ok[u], 1)

            centre(dve, 0)
            centre(dve, 1)
            logits(dve, 0)
            with dve.Fori(2, NG // 2) as j:
                centre(dve, j)
                logits(dve, j - 1)
            logits(dve, NG // 2 - 1)

        @block.gpsimd
        def _(pool):
            q = bias.q[:, :, P:S]
            pool.affine_select(out=q, in_=q, compare_op=ALU.is_ge, fill=BIG, base=0,
                               pattern=[[0, H], [-1, P]], channel_multiplier=1)

        @block.tensor
        def _(pe):
            def turn(pe, j):
                for u in range(2):
                    wait_if(pe, xt_ok[u], j)
                    for k in range(GT):
                        wait_if(pe, xn_ok[u], GT * j + k + 1)
                        mm = pe.transpose(pt[u][:, k * P:(k + 1) * P], xn[u][:, k, :], R.ident[:])
                    mm.then_inc(turned[u], 1)

            def gate(pe, j):
                for u in range(2):
                    wait_if(pe, xt_ok[u], j + 1)
                    wait_if(pe, logits_ok[u], j)
                    for k in range(GT):
                        mm = pe.matmul(pg[u][:, k * E:(k + 1) * E], xt[u][:, k * P:(k + 1) * P],
                                       R.gate_w[0][:], start=True, stop=True)
                    mm.then_inc(gated[u], 1)

            def reverse_bias(pe, j):
                for u in range(2):
                    wait_if(pe, bias_neg[u], j)
                    pe.matmul(bank[u][:], R.reverse[:], bias.piece_k(2 * j + u), start=True, stop=True
                              ).then_inc(bias_turned[u], 1)

            def pair(pe, j):
                turn(pe, j)
                gate(pe, j)
                reverse_bias(pe, j)
            pairs_of_groups(pe, pair)

        @block.scalar
        def _(act):
            def pair(act, j):
                for u in range(2):
                    wait_if(act, turned[u], j + 1)
                    wait_if(act, gated[u], j)
                    wait_if(act, xt_kept[u], 16 * j)
                    act.activation(xt[u][:], pt[u][:], ACT.Copy).then_inc(xt_ok[u], 1)
                for u in range(2):
                    wait_if(act, bias_turned[u], j + 1)
                    act.mul(bias.piece_k(2 * j + u), bank[u][:].rearrange("p (h k) -> p h k", h=2), -1.0
                            ).then_inc(bias_neg[u], 1)
            pairs_of_groups(act, pair)


def route(nc, R, D, layer, bias):
    tag = f"r{layer}_"
    tops = 1 + layer
    routed = (ROUTED0, ROUTED1)[layer]
    with ExitStack() as ctx:
        sem = Sems(nc, ctx)
        ctx.callback(sem.done)

        def sb(name, shape, dt=F32):
            return ctx.enter_context(nc.sbuf_tensor(tag + name, shape, dt))

        best, first = sb("best", [P, NT]), sb("first", [P, NT])
        hit = sb("hit", [P, NT, E])
        pick = [sb(f"pick{n}", [P, NT, E]) for n in range(tops)]
        chosen = sb("chosen", [P, NT, E])
        sel = sb("sel", [P, NT, E])
        mask_bf = sb("mask_bf", [P, E, NT], BF16)
        count, upto, slot = sb("count", [P, E, NT]), sb("upto", [P, E, NT]), sb("slot", [P, E, NT])
        over = sb("over", [P, E, B * S // SLOTS])
        tiles, last, start = sb("tiles", [P, E]), sb("last", [P, E]), sb("start", [P, E])
        before = sb("before", [P, ROUTED1, E])
        owner = sb("owner", [P, ROUTED1])
        pos_f = sb("pos_f", [P, NT])
        top_logit = [sb(f"top_logit{n}", [P, NT]) for n in range(tops)]
        prank = ctx.enter_context(nc.psum_tensor(tag + "prank", [P, 512], F32))
        pcount = ctx.enter_context(nc.psum_tensor(tag + "pcount", [P, 512], F32))
        steps, mask_ok, ranked = sem(tag + "steps"), sem(tag + "mask_ok"), sem(tag + "ranked")
        exps, zeroed = sem(tag + "exps"), sem(tag + "zeroed")
        bias_ok = sem(tag + "bias_ok")
        diff_ok = sem(tag + "diff_ok")
        block = ctx.enter_context(nc.Block())
        per_tile = [P, NT, E]

        @block.vector
        def _(dve):
            done = [0]

            def step(ins):
                done[0] += 1
                ins.then_inc(steps, 1)
                dve.wait_ge(steps, done[0])

            em8 = R.expert_m8[:].unsqueeze(1).to_broadcast(per_tile)

            def one_hot(out, logits):
                step(dve.tensor_reduce(best[:], logits, X, ALU.max))
                step(dve.tensor_tensor(hit[:], logits, best[:].unsqueeze(2).to_broadcast(per_tile), ALU.is_equal))
                step(dve.tensor_tensor(hit[:], hit[:], em8, ALU.mult))
                step(dve.tensor_reduce(first[:], hit[:], X, ALU.min))
                step(dve.tensor_tensor(out[:], em8, first[:].unsqueeze(2).to_broadcast(per_tile), ALU.is_equal))

            def logit_of(out, chose):
                step(dve.tensor_tensor(hit[:], R.logits[:], chose[:], ALU.mult))
                step(dve.tensor_reduce(out[:], hit[:], X, ALU.add))

            if layer == 0:
                one_hot(pick[0], R.logits[:])
                marked = pick[0]
            else:
                step(dve.tensor_tensor(sel[:], R.logits[:], R.rb[:].unsqueeze(1).to_broadcast(per_tile), ALU.add))
                one_hot(pick[0], sel[:])
                step(dve.scalar_tensor_tensor(out=sel[:], in0=pick[0][:], scalar=-BIG, in1=sel[:],
                                              op0=ALU.mult, op1=ALU.add))
                one_hot(pick[1], sel[:])
                step(dve.tensor_tensor(chosen[:], pick[0][:], pick[1][:], ALU.add))
                marked = chosen
            dve.tensor_copy(mask_bf[:].rearrange("p e t -> p t e"), marked[:]).then_inc(mask_ok, 1)
            if layer == 1:
                for n in range(2):
                    logit_of(top_logit[n], pick[n])
                step(dve.tensor_tensor(best[:], top_logit[0][:], top_logit[1][:], ALU.max))
                for n in range(2):
                    ins = dve.tensor_tensor(top_logit[n][:], top_logit[n][:], best[:], ALU.subtract)
                    ins.then_inc(diff_ok, 1)
                dve.wait_ge(exps, 2)
                step(dve.tensor_tensor(first[:], R.weight[0][:], R.weight[1][:], ALU.add))
                step(dve.reciprocal(best[:], first[:]))
                for n in range(2):
                    step(dve.tensor_tensor(R.weight[n][:], R.weight[n][:], best[:], ALU.mult))
            dve.wait_ge(ranked, 1)
            step(dve.tensor_copy(count[:].rearrange("p e t -> p (e t)"), pcount[:, 0:E * NT]))
            for e in range(E):
                ins = dve.tensor_tensor_scan(upto[:, e, :], count[:, e, :], R.zero32[:], 0.0, ALU.add, ALU.add)
                step(ins)
            step(dve.tensor_tensor(over[:], upto[:, :, NT - 1:NT].to_broadcast([P, E, B * S // SLOTS]),
                                   R.tile_start[:].unsqueeze(1).to_broadcast([P, E, B * S // SLOTS]), ALU.is_gt))
            step(dve.tensor_reduce(tiles[:], over[:], X, ALU.add))
            step(dve.tensor_tensor_scan(last[:], tiles[:], R.zero32[:, 0:E], 0.0, ALU.add, ALU.add))
            step(dve.tensor_tensor(start[:], last[:], tiles[:], ALU.subtract))
            step(dve.tensor_scalar(start[:], start[:], float(SLOTS), float(SHARED * SLOTS * layer), ALU.mult, ALU.add))
            step(dve.tensor_tensor(slot[:], prank[:, 0:E * NT].rearrange("p (e t) -> p e t", e=E), upto[:], ALU.add))
            step(dve.tensor_tensor(slot[:], slot[:], count[:], ALU.subtract))
            step(dve.tensor_tensor(slot[:], slot[:], start[:].unsqueeze(2).to_broadcast([P, E, NT]), ALU.add))
            for n in range(tops):
                step(dve.tensor_tensor(hit[:], slot[:].rearrange("p e t -> p t e"), pick[n][:], ALU.mult))
                step(dve.tensor_reduce(pos_f[:], hit[:], X, ALU.add))
                step(dve.tensor_copy(R.pos[n][:], pos_f[:]))
            step(dve.tensor_tensor(before[:], R.tile_no[:].unsqueeze(2).to_broadcast([P, ROUTED1, E]),
                                   last[:].unsqueeze(1).to_broadcast([P, ROUTED1, E]), ALU.is_ge))
            step(dve.tensor_reduce(owner[:], before[:], X, ALU.add))
            step(dve.tensor_scalar(owner[:], owner[:], float(E - 1), None, ALU.min))
            at = SHARED if layer else 0
            step(dve.tensor_copy(R.tile_expert[0:1, at:at + routed], owner[0:1, 0:routed]))
            if layer == 1:
                step(dve.memset(R.tile_expert[0:1, 0:SHARED], E))

        @block.sync
        def _(sp):
            sem.clear_old(sp)
            if layer == 0:
                sp.wait_ge(zeroed, zero_slots(sp, R, D, 0, ROUTED0, zeroed))

        @block.gpsimd
        def _(pool):
            if layer == 0:
                k = bias.k[:, :, 0:P]
                pool.affine_select(out=k, in_=k, compare_op=ALU.is_ge, fill=BIG, base=0,
                                   pattern=[[0, H], [1, P]], channel_multiplier=-1).then_inc(bias_ok, 1)
                pool.wait_ge(bias_ok, 1)
                pool.tensor_copy(bias.k[:, :, S:S + P], k)

        @block.scalar
        def _(act):
            if layer == 1:
                for n in range(2):
                    act.wait_ge(diff_ok, n + 1)
                    act.activation(R.weight[n][:], top_logit[n][:], ACT.Exp).then_inc(exps, 1)

        @block.tensor
        def _(pe):
            pe.wait_ge(mask_ok, 1)
            flat = mask_bf[:].rearrange("p e t -> p (e t)")
            pe.matmul(prank[:, 0:E * NT], R.upper_bf[:], flat, start=True, stop=True)
            pe.matmul(pcount[:, 0:E * NT], R.ones_bf[:], flat, start=True, stop=True).then_inc(ranked, 1)


def zero_slots(eng, R, D, first, until, done):
    n = 4
    for i in range(first, until, n):
        m = (min(i + n, until) - i) * SLOTS // P
        eng.dma_start(D["slots_in"][i * SLOTS:i * SLOTS + m * P, :].rearrange("(n p) d -> p n d", p=P),
                      R.zeros[:].unsqueeze(1).to_broadcast([P, m, P])).then_inc(done, 16)
    return 16 * -(-(until - first) // n)


def scatter(pool, R, D, layer, tiles):
    for t in tiles:
        for n in range(1 + layer):
            pool.indirect_dma_start(D["slots_in"], bass.IndirectOffsetOnAxis(ap=R.pos[n][:, t:t + 1], axis=0),
                                    R.xn[:, t, :], None).then_inc(R.scattered, 16)


def experts(nc, R, D, layer):
    tag = f"e{layer}_"
    tiles, ahead = (ROUTED0, TILES)[layer], AHEAD[layer]
    C = (F0, F1)[layer] // P
    tops = 1 + layer
    with ExitStack() as ctx:
        sem = Sems(nc, ctx)
        ctx.callback(sem.done)

        def sb(name, shape, n=2, dt=F32):
            return [ctx.enter_context(nc.sbuf_tensor(f"{tag}{name}{u}", shape, dt)) for u in range(n)]

        w = sb("w", [P, D["W"][layer].shape[2]], ahead)
        x_in = sb("x_in", [P, 2, P], ahead)
        b_down = sb("b_down", [P, P], ahead) if layer == 0 else None
        x_t = sb("x_t", [P, SLOTS])
        hid = sb("hid", [P, C, SLOTS])
        pre = sb("pre", [P, C, SLOTS])
        y_out = sb("y_out", [P, 2, P], ahead)
        loads = 3 if layer == 0 else 2
        pt = ctx.enter_context(nc.psum_tensor(tag + "pt", [P, 512], F32))
        ph = [[ctx.enter_context(nc.psum_tensor(f"{tag}ph{u}{n}", [P, 2, SLOTS], F32)) for n in range(2)]
              for u in range(2)]
        py = [ctx.enter_context(nc.psum_tensor(f"{tag}py{u}", [P, 512], F32)) for u in range(2)]
        in_ok = [sem(f"{tag}in_ok{r}") for r in range(ahead)]
        stored = [sem(f"{tag}stored{r}") for r in range(ahead)]
        turned, x_ok, up_ok, pre_ok = sem(tag + "turned"), sem(tag + "x_ok"), sem(tag + "up_ok"), sem(tag + "pre_ok")
        hid_ok, down_ok, y_ok = sem(tag + "hid_ok"), sem(tag + "down_ok"), sem(tag + "y_ok")
        block = ctx.enter_context(nc.Block())
        rounds = tiles // ahead
        b_up = (4 + C) * P

        def over_tiles(eng, do, until=rounds, begin=0):
            at = begin
            if begin == 0:
                for r in range(ahead):
                    do(eng, 0, r)
                at = 1
            if at < min(until, rounds - 1):
                with eng.Fori(at, min(until, rounds - 1)) as j:
                    for r in range(ahead):
                        do(eng, j, r)
            if until == rounds:
                for r in range(ahead):
                    do(eng, rounds - 1, r)

        def exists(j, r):
            return not isinstance(j, int) or 0 <= ahead * j + r < tiles

        def ring(j, r):
            return j + r // ahead, r % ahead, ahead * j + r

        def load(sp, j, r):
            j, r, i = ring(j, r)
            e = sp.value_load(R.tile_expert[0:1, bass.ds(i, 1)], min_val=0, max_val=E - 1 + layer)
            wait_if(sp, down_ok, i - ahead + 1)
            sp.dma_start(x_in[r][:], D["slots_in"][bass.ds(SLOTS * i, SLOTS), :].rearrange(
                "(t p) d -> p t d", p=P)).then_inc(in_ok[r], 16)
            sp.dma_start(w[r][:], D["W"][layer][e, :, :]).then_inc(in_ok[r], 16)
            if layer == 0:
                sp.dma_start(b_down[r][:], D["b2"][bass.ds(e, 1), :].to_broadcast([P, P])).then_inc(in_ok[r], 16)

        @block.sync
        def _(sp):
            sem.clear_old(sp)
            if layer == 0:
                sp.wait_ge(R.scattered, 16 * NT)
            for r in range(ahead):
                load(sp, 0, r)

            def tile(sp, j, r):
                i = ahead * j + r
                sp.wait_ge(y_ok, i + 1)
                sp.dma_start(D["slots_out"][layer][bass.ds(SLOTS * i, SLOTS), :].rearrange(
                    "(t p) d -> p t d", p=P), y_out[r][:]).then_inc(stored[r], 16)
                if exists(j, r + ahead):
                    load(sp, j, r + ahead)

            if layer == 0:
                over_tiles(sp, tile)
            else:
                over_tiles(sp, tile, until=SHARED // ahead - 1)
                sp.wait_ge(R.scattered, 16 * NT * 3)
                over_tiles(sp, tile, begin=SHARED // ahead - 1)
            for r in range(ahead):
                sp.wait_ge(stored[r], 16 * rounds)

        @block.gpsimd
        def _(pool):
            if layer == 0:
                pool.wait_ge(R.zeroed, zero_slots(pool, R, D, ROUTED0, TILES, R.zeroed))
            else:
                scatter(pool, R, D, layer, range(NT))

        def turn(pe, j, r):
            j, r, i = ring(j, r)
            pe.wait_ge(in_ok[r], 16 * loads * (j + 1))
            wait_if(pe, x_ok, i)
            for k in range(2):
                mm = pe.transpose(pt[:, k * P:(k + 1) * P], x_in[r][:, k, :], R.ident[:])
            mm.then_inc(turned, 1)

        def up(pe, j, r):
            j, r, i = ring(j, r)
            u = r % 2
            pe.wait_ge(x_ok, i + 1)
            wait_if(pe, pre_ok, 2 * (i - 1))
            wait_if(pe, hid_ok, 2 * (i - 1))
            for c in range(4):
                mm = pe.matmul(ph[u][c // 2][:, c % 2, :], w[r][:, c * P:(c + 1) * P], x_t[u][:], start=True, stop=True)
                if c % 2:
                    mm.then_inc(up_ok, 1)

        def down(pe, j, r):
            i, u = ahead * j + r, r % 2
            wait_if(pe, y_ok, i - 1)
            pe.wait_ge(hid_ok, 2 * (i + 1))
            for k in range(2):
                for c in range(C):
                    mm = pe.matmul(py[u][:, k * P:(k + 1) * P], hid[u][:, c, k * P:(k + 1) * P],
                                   w[r][:, (4 + c) * P:(5 + c) * P], start=(c == 0), stop=(c == C - 1))
            mm.then_inc(down_ok, 1)

        @block.tensor
        def _(pe):
            turn(pe, 0, 0)
            turn(pe, 0, 1)
            up(pe, 0, 0)

            def tile(pe, j, r):
                if exists(j, r + 2):
                    turn(pe, j, r + 2)
                if exists(j, r + 1):
                    up(pe, j, r + 1)
                down(pe, j, r)
            over_tiles(pe, tile)

        def x_copy(act, j, r):
            j, r, i = ring(j, r)
            act.wait_ge(turned, i + 1)
            wait_if(act, up_ok, 2 * (i - 1))
            act.activation(x_t[r % 2][:], pt[:, 0:SLOTS], ACT.Copy).then_inc(x_ok, 1)

        def act_fn(act, j, r):
            j, r, i = ring(j, r)
            u = r % 2
            if layer == 0:
                for n in range(2):
                    act.wait_ge(pre_ok, 2 * i + n + 1)
                    wait_if(act, down_ok, i - 1)
                    act.activation(hid[u][:, 2 * n:2 * n + 2, :], pre[u][:, 2 * n:2 * n + 2, :], ACT.Gelu
                                   ).then_inc(hid_ok, 1)
            else:
                act.wait_ge(up_ok, 2 * (i + 1))
                wait_if(act, hid_ok, 2 * (i - 1))
                act.activation(pre[u][:], ph[u][1][:], ACT.Silu).then_inc(pre_ok, 2)

        @block.scalar
        def _(act):
            x_copy(act, 0, 0)
            x_copy(act, 0, 1)
            act_fn(act, 0, 0)

            def tile(act, j, r):
                if exists(j, r + 2):
                    x_copy(act, j, r + 2)
                if exists(j, r + 1):
                    act_fn(act, j, r + 1)
            over_tiles(act, tile)

        def vector_up(dve, j, r):
            j, r, i = ring(j, r)
            u = r % 2
            if layer == 0:
                dve.wait_ge(in_ok[r], 16 * loads * (j + 1))
                for n in range(2):
                    dve.wait_ge(up_ok, 2 * i + n + 1)
                    wait_if(dve, hid_ok, 2 * (i - 1))
                    dve.tensor_tensor(pre[u][:, 2 * n:2 * n + 2, :], ph[u][n][:],
                                      w[r][:, b_up + 2 * n:b_up + 2 * n + 2].unsqueeze(2).to_broadcast([P, 2, SLOTS]),
                                      ALU.add).then_inc(pre_ok, 1)
            else:
                dve.wait_ge(pre_ok, 2 * (i + 1))
                wait_if(dve, down_ok, i - 1)
                dve.tensor_tensor(hid[u][:], ph[u][0][:], pre[u][:], ALU.mult).then_inc(hid_ok, 2)

        def vector_down(dve, j, r):
            i = ahead * j + r
            dve.wait_ge(down_ok, i + 1)
            wait_if(dve, stored[r], 16 * j)
            got = py[r % 2][:, 0:2 * P].rearrange("p (k d) -> p k d", k=2)
            if layer == 0:
                dve.tensor_tensor(y_out[r][:], got, b_down[r][:].unsqueeze(1).to_broadcast([P, 2, P]), ALU.add
                                  ).then_inc(y_ok, 1)
            else:
                dve.tensor_copy(y_out[r][:], got).then_inc(y_ok, 1)

        @block.vector
        def _(dve):
            vector_up(dve, 0, 0)

            def tile(dve, j, r):
                if exists(j, r + 1):
                    vector_up(dve, j, r + 1)
                vector_down(dve, j, r)
            over_tiles(dve, tile)


def combine0(nc, R, D):
    tag = "m0_"
    octet = 8
    behind = 13
    with ExitStack() as ctx:
        sem = Sems(nc, ctx)
        ctx.callback(sem.done)
        ring = len(R.arrived)

        def sb(name):
            return [ctx.enter_context(nc.sbuf_tensor(f"{tag}{name}{r}", [P, P], F32)) for r in range(ring)]

        f, gate, prod = sb("f"), sb("gate"), sb("prod")
        stats = ctx.enter_context(nc.sbuf_tensor(tag + "stats", [P, NT, 6], F32))
        pt = [ctx.enter_context(nc.psum_tensor(f"{tag}pt{u}", [P, GT * P], F32)) for u in range(2)]
        pg = [ctx.enter_context(nc.psum_tensor(f"{tag}pg{u}", [P, 512], F32)) for u in range(2)]
        gate_ok, prod_ok, x_ok = sem(tag + "gate_ok"), sem(tag + "prod_ok"), sem(tag + "x_ok")
        stats_ok, mv_ok = sem(tag + "stats_ok"), sem(tag + "mv_ok")
        eps_ok, rstd_ok = sem(tag + "eps_ok"), sem(tag + "rstd_ok")
        xn_ok, turned, xt_ok = sem(tag + "xn_ok"), sem(tag + "turned"), sem(tag + "xt_ok")
        gated, logits_ok, xn_slots = sem(tag + "gated"), sem(tag + "logits_ok"), sem(tag + "xn_slots")
        block = ctx.enter_context(nc.Block())

        @block.gpsimd
        def _(pool):
            def inverse_std(o):
                tiles = slice(octet * o, octet * (o + 1))
                pool.wait_ge(mv_ok, octet * (o + 1))
                pool.tensor_tensor(R.var_eps[:, tiles], R.mean_var[:, tiles, 1], R.eps[:].to_broadcast([P, octet]),
                                   ALU.add).then_inc(eps_ok, 1)
                pool.wait_ge(eps_ok, o + 1)
                pool.tensor_tensor(R.rstd[:, tiles], R.var_eps[:, tiles], R.neg_half[:].to_broadcast([P, octet]),
                                   ALU.pow).then_inc(rstd_ok, 1)

            for t in range(NT):
                r = t % ring
                if t >= ring:
                    pool.wait_ge(gate_ok, t - ring + 1)
                pool.indirect_dma_start(f[r][:], None, D["slots_out"][0],
                                        bass.IndirectOffsetOnAxis(ap=R.pos[0][:, t:t + 1], axis=0)
                                        ).then_inc(R.arrived[r], 16)
                if t > octet and t % octet == 3:
                    inverse_std(t // octet - 1)
            inverse_std(NT // octet - 1)

        @block.sync
        def _(sp):
            sem.clear_old(sp)
            for g in range(NG):
                sp.wait_ge(xn_ok, GT * (g + 1))
                sp.dma_start(D["slots_in"][GT * P * g:GT * P * (g + 1), :].rearrange("(t p) d -> p t d", p=P),
                             R.xn[:, GT * g:GT * (g + 1), :]).then_inc(xn_slots, 16)
            sp.wait_ge(xn_slots, 16 * NG)

        @block.scalar
        def _(act):
            def copy_xt(g):
                act.wait_ge(turned, g + 1)
                act.activation(R.xt[:, GT * P * g:GT * P * (g + 1)], pt[g % 2][:], ACT.Copy).then_inc(xt_ok, 1)

            copied = 0
            for t in range(NT):
                r = t % ring
                act.wait_ge(R.arrived[r], 16 * (t // ring + 1))
                if t >= ring:
                    act.wait_ge(prod_ok, t - ring + 1)
                act.activation(gate[r][:], f[r][:], ACT.Silu).then_inc(gate_ok, 1)
                if t >= GT * (copied + 1) + behind + 2:
                    copy_xt(copied)
                    copied += 1
            for g in range(copied, NG):
                copy_xt(g)

        @block.tensor
        def _(pe):
            def turn(g):
                if g >= 2:
                    pe.wait_ge(xt_ok, g - 1)
                for k in range(GT):
                    pe.wait_ge(xn_ok, GT * g + k + 1)
                    mm = pe.transpose(pt[g % 2][:, k * P:(k + 1) * P], R.xn[:, GT * g + k, :], R.ident[:])
                mm.then_inc(turned, 1)

            def router(g):
                pe.wait_ge(xt_ok, g + 1)
                if g >= 2:
                    pe.wait_ge(logits_ok, g - 1)
                for k in range(GT):
                    t = GT * g + k
                    mm = pe.matmul(pg[g % 2][:, k * E:(k + 1) * E], R.xt[:, t * P:(t + 1) * P], R.gate_w[1][:],
                                   start=True, stop=True)
                mm.then_inc(gated, 1)

            for g in range(NG):
                turn(g)
                if g:
                    router(g - 1)
            router(NG - 1)

        @block.vector
        def _(dve):
            def add(t):
                r = t % ring
                dve.wait_ge(gate_ok, t + 1)
                if t >= ring:
                    dve.wait_ge(x_ok, t - ring + 1)
                dve.tensor_tensor(prod[r][:], R.s[:, t, :], gate[r][:], ALU.mult).then_inc(prod_ok, 1)
                if t:
                    statistics(t - 1)
                dve.wait_ge(prod_ok, t + 1)
                dve.tensor_tensor(R.x[:, t, :], R.x[:, t, :], prod[r][:], ALU.add).then_inc(x_ok, 1)
                if t:
                    aggregate(t - 1)

            def statistics(t):
                dve.wait_ge(x_ok, t + 1)
                dve.bn_stats(stats[:, t, :], R.x[:, t, :]).then_inc(stats_ok, 1)

            def aggregate(t):
                dve.wait_ge(stats_ok, t + 1)
                dve.bn_aggr(R.mean_var[:, t, :], stats[:, t, :]).then_inc(mv_ok, 1)

            def centre(t):
                dve.wait_ge(rstd_ok, t // octet + 1)
                dve.tensor_scalar(R.xn[:, t, :], R.x[:, t, :], R.mean_var[:, t, 0:1], R.rstd[:, t:t + 1],
                                  ALU.subtract, ALU.mult).then_inc(xn_ok, 1)

            def logits(g):
                dve.wait_ge(gated, g + 1)
                dve.tensor_scalar(R.logits[:, GT * g:GT * (g + 1), :],
                                  pg[g % 2][:, 0:GT * E].rearrange("p (k e) -> p k e", e=E), SCALE1, None, ALU.mult
                                  ).then_inc(logits_ok, 1)

            for t in range(NT + behind):
                if t < NT:
                    add(t)
                if t == NT - 1:
                    statistics(t)
                    aggregate(t)
                if t >= behind:
                    centre(t - behind)
                    if (t - behind) % GT == GT - 1 and t - behind >= 2 * GT:
                        logits((t - behind) // GT - 2)
            logits(NG - 2)
            logits(NG - 1)


def combine1(nc, R, D, f):
    tag = "m1_"
    with ExitStack() as ctx:
        sem = Sems(nc, ctx)
        ctx.callback(sem.done)
        gate_ok, out_done = sem(tag + "gate_ok"), sem(tag + "out_done")
        of_pool = [g for g in range(NG) if g % 4 == 1]
        of_dve = [g for g in range(NG) if g % 4 != 1]
        prod_ok = {"pool": sem(tag + "pool_prod_ok"), "dve": sem(tag + "dve_prod_ok")}
        x_ok = {"pool": sem(tag + "pool_x_ok"), "dve": sem(tag + "dve_x_ok")}
        block = ctx.enter_context(nc.Block())

        def group(g):
            return slice(GT * g, GT * (g + 1))

        @block.sync
        def _(sp):
            sem.clear_old(sp)
            for g in range(NG):
                who, among = ("pool", of_pool) if g in of_pool else ("dve", of_dve)
                sp.wait_ge(x_ok[who], among.index(g) + 1)
                sp.dma_start(D["out"][GT * P * g:GT * P * (g + 1), :].rearrange("(t p) d -> p t d", p=P),
                             R.x[:, group(g), :]).then_inc(out_done, 16)
            sp.wait_ge(out_done, 16 * NG)

        @block.scalar
        def _(act):
            for g in range(NG):
                act.activation(f.top[1][:, group(g), :], f.top[0][:, group(g), :], ACT.Silu).then_inc(gate_ok, 1)

        def add(eng, who, groups):
            for n, g in enumerate(groups):
                eng.wait_ge(gate_ok, g + 1)
                eng.tensor_tensor(f.shared[:, group(g), :], R.s[:, group(g), :], f.top[1][:, group(g), :], ALU.mult
                                  ).then_inc(prod_ok[who], 1)
                eng.wait_ge(prod_ok[who], n + 1)
                eng.tensor_tensor(R.x[:, group(g), :], R.x[:, group(g), :], f.shared[:, group(g), :], ALU.add
                                  ).then_inc(x_ok[who], 1)

        @block.vector
        def _(dve):
            add(dve, "dve", of_dve)

        @block.gpsimd
        def _(pool):
            add(pool, "pool", of_pool)


class Gathered:

    def __init__(self, nc, ctx):
        self.top = [ctx.enter_context(nc.sbuf_tensor(f"f_top{n}", [P, NT, P], F32)) for n in range(2)]
        self.shared = ctx.enter_context(nc.sbuf_tensor("f_shared", [P, NT, P], F32))


class Batch:

    def __init__(self, j, c):
        self.u, self.half, self.n = c % 2, j + c // 2, 2 * j + c


def attention0(nc, R, D, bias):
    tag = "a0_"
    with ExitStack() as ctx:
        sem = Sems(nc, ctx)
        ctx.callback(sem.done)

        def sb(name, shape, dt=F32):
            return ctx.enter_context(nc.sbuf_tensor(tag + name, shape, dt))

        def ps(name):
            return ctx.enter_context(nc.psum_tensor(tag + name, [P, 512], F32))

        bias_q, bias_k = bias.q, bias.k
        xs = [sb(f"xs{u}", [P, S]) for u in range(2)]
        qk = sb("qk", [P, 2 * S])
        rest = sb("rest", [P, 2 * S])
        part = [sb(f"part{u}", [P, 3, 2 * S], BF16) for u in range(2)]
        qst = [sb(f"qst{u}", [MROWS, H, S], BF16) for u in range(2)]
        kst = [sb(f"kst{u}", [MROWS, H, S], BF16) for u in range(2)]
        va = [sb(f"va{u}", [P, 2, H, OROWS]) for u in range(2)]
        sums = [sb(f"sums{r}", [P, S], BF16) for r in range(4)]
        neg_max = [sb(f"neg_max{u}", [P, H, 2]) for u in range(2)]
        max_f = [sb(f"max_f{f}", [H, P]) for f in range(2)]
        max_rest = [sb(f"max_rest{f}", [H, P]) for f in range(2)]
        max_part = [sb(f"max_part{f}", [H, 3, P], BF16) for f in range(2)]
        arg = [sb(f"arg{r}", [P, S + P]) for r in range(4)]
        prob = [sb(f"prob{r}", [P, S + P]) for r in range(4)]
        o_raw, rden = sb("o_raw", [OROWS, 2, S]), sb("rden", [P, 4, HALF])
        rden_wide = sb("rden_wide", [P, 4, P // 2])
        o_t = sb("o_t", [P // 2, 2, S])
        resid = sb("resid", [P, 2, P])
        y = sb("y", [P, 2, P])
        stats, mean_var = sb("stats", [P, 2, 6]), sb("mean_var", [P, 2, 2])
        var_eps, rstd = sb("var_eps", [P, 2]), sb("rstd", [P, 2])
        yn, yg = sb("yn", [P, 2, P]), sb("yg", [P, 2, P])
        p_qk, p_misc = ps("p_qk"), ps("p_misc")
        p_s = [ps(f"p_s{r}") for r in range(2)]
        p_t = [ps(f"p_t{r}") for r in range(2)]
        p_o = [ps(f"p_o{u}") for u in range(2)]

        s = {n: sem(tag + n) for n in (
            "zeros_ok", "ones_ok", "rows_ok", "qk_mm", "qk_ok", "part1", "part2", "part3", "rest_ok",
            "v_mm", "v_ok", "scored", "max_ok", "max_turned", "max_read", "max_diff", "max_p2", "max_p3",
            "scored_t", "arg_ok", "prob_ok", "summed", "o_raw_ok", "sums_turned", "rden_ok", "wide_ok", "spread_ok", "o_t_ok", "projected",
            "resid_ok", "y_ok", "stats_ok", "mv_ok", "eps_ok", "rstd_ok", "yn_ok", "yg_ok", "s_ok")}
        xs_in = sem.pair(tag + "xs_in")
        spilled = [[sem(f"{tag}spilled{u}{f}") for f in range(2)] for u in range(2)]
        stacked = [[sem(f"{tag}stacked{u}{f}") for f in range(2)] for u in range(2)]
        max_in = [[sem(f"{tag}max_in{u}{f}") for f in range(2)] for u in range(2)]
        block = ctx.enter_context(nc.Block())

        def bank_o(u):
            return p_o[u][0:OROWS, :].rearrange("p (f q) -> p f q", f=2)

        def steps(eng, do):
            do(eng, 0, 0)
            do(eng, 0, 1)
            with eng.Fori(1, B // 2 - 1) as j:
                do(eng, j, 0)
                do(eng, j, 1)
            do(eng, 0, B - 2)
            do(eng, 0, B - 1)

        def has(j, c, ahead):
            return not isinstance(j, int) or 0 <= c + ahead < B

        def stage_x(sp, b):
            if not isinstance(b.n, int) or b.n >= 2:
                sp.wait_ge(s["v_mm"], b.n - 1)
            sp.dma_start(xs[b.u][:], R.xt[:, bass.ds(S * b.n, S)]).then_inc(xs_in[b.u], 16)

        def spill(sp, b):
            for name in ("part1", "part2", "part3"):
                sp.wait_ge(s[name], b.n + 1)
            for f in range(2):
                wait_if(sp, stacked[b.u][f], 64 * b.half)
                for k in range(2):
                    dst = bass.AP(tensor=D["parts"].tensor, offset=at_parts(b, k, f),
                                  ap=[[S, P // 2], [P // 2 * S, PARTS], [1, S]])
                    sp.dma_start(dst, part[b.u][P // 2 * f:P // 2 * (f + 1), :, k * S:(k + 1) * S]
                                 ).then_inc(spilled[b.u][f], 16)

        def at_parts(b, k, f):
            return ((b.u * 2 + k) * 2 + f) * PARTS * P // 2 * S

        def stack(sp, b, f):
            wait_if(sp, s["scored_t"], H * (b.n - 2) + HALF * (f + 1))
            sp.wait_ge(spilled[b.u][f], 32 * (b.half + 1))
            heads = slice(HALF * f, HALF * (f + 1))
            src = bass.AP(tensor=D["parts"].tensor, offset=at_parts(b, 1, f),
                          ap=[[0, PARTS], [HALF * S, PARTS * HD], [1, HALF * S]])
            sp.dma_start(kst[b.u][0:KROWS, heads, :], src).then_inc(stacked[b.u][f], 16)
            for i in range(PARTS):
                src = bass.AP(tensor=D["parts"].tensor, offset=at_parts(b, 0, f) + i * P // 2 * S,
                              ap=[[0, PARTS], [HALF * S, HD], [1, HALF * S]])
                sp.dma_start(qst[b.u][PARTS * HD * i:PARTS * HD * (i + 1), heads, :], src
                             ).then_inc(stacked[b.u][f], 16)

        @block.sync
        def _(sp):
            sem.clear_old(sp)
            stage_x(sp, Batch(0, 0))
            stage_x(sp, Batch(0, 1))
            sp.wait_ge(s["rows_ok"], 2)
            for b in (Batch(0, 0), Batch(0, 1)):
                spill(sp, b)
                stack(sp, b, 0)
                stack(sp, b, 1)
            def step(sp, j, c):
                b = Batch(j, c)
                if has(j, c, 2):
                    stage_x(sp, Batch(j, c + 2))
                if has(j, c, 2):
                    spill(sp, Batch(j, c + 2))
                    stack(sp, Batch(j, c + 2), 0)
                if has(j, c, 2):
                    stack(sp, Batch(j, c + 2), 1)
            steps(sp, step)

        def project(pe, b):
            wait_if(pe, s["qk_ok"], 2 * b.n)
            pe.matmul(p_qk[:, 0:S], R.w_qkv[:, 0:P], R.xt[:, bass.ds(S * b.n, S)], start=True, stop=True)
            pe.matmul(p_qk[:, S:2 * S], R.w_qkv[:, P:2 * P], R.xt[:, bass.ds(S * b.n, S)], start=True, stop=True
                      ).then_inc(s["qk_mm"], 1)

        def values(pe, b):
            pe.wait_ge(xs_in[b.u], 16 * (b.half + 1))
            for k in range(2):
                mm = pe.matmul(p_misc[:, k * P:(k + 1) * P], xs[b.u][:, k * P:(k + 1) * P],
                               R.w_qkv[:, 2 * P:3 * P], start=True, stop=True)
            mm.then_inc(s["v_mm"], 1)

        def score(pe, b, h):
            n = H * b.n + h
            if h % HALF == 0:
                pe.wait_ge(stacked[b.u][h // HALF], 64 * (b.half + 1))
            wait_if(pe, s["max_ok"], 2 * (n - 1))
            q, k = qst[b.u][0:KROWS, h, :], kst[b.u][0:KROWS, h, :]
            pe.matmul(p_s[h % 2][:, 0:S], q[:, P:S], k, start=True, stop=True)
            pe.matmul(p_s[h % 2][:, S:S + P], q[:, 0:P], k[:, 0:P], start=True, stop=True).then_inc(s["scored"], 1)

        def turn_max(pe, b, f):
            pe.wait_ge(s["max_ok"], 2 * H * b.n + H * (f + 1))
            flat = neg_max[b.u][:].rearrange("p h t -> p (h t)")
            pe.transpose(p_qk[0:H, 0:P], flat[:, H * f:H * (f + 1)], R.ident[:]).then_inc(s["max_turned"], 1)

        def score_t(pe, b, h):
            n = H * b.n + h
            if h % HALF == 0:
                f = h // HALF
                pe.wait_ge(max_in[b.u][f], 48 * (b.half + 1))
            wait_if(pe, s["arg_ok"], n - 1)
            q, k = qst[b.u][:, h, :], kst[b.u][:, h, :]
            pe.matmul(p_t[h % 2][:, 0:S], k[:, 0:P], q, start=True, stop=True)
            pe.matmul(p_t[h % 2][:, S:S + P], k[:, P:S], q[:, P:S], start=True, stop=True).then_inc(s["scored_t"], 1)

        def weigh(pe, b, h):
            pe.wait_ge(s["prob_ok"], H * b.n + h + 1)
            if h == 0:
                pe.wait_ge(s["v_ok"], b.n + 1)
                if isinstance(b.n, int) and b.n < 2:
                    pe.wait_ge(s["ones_ok"], 2)
                wait_if(pe, s["o_raw_ok"], b.n - 1)
            o, pr, v = bank_o(b.u)[:, h // HALF, :], prob[h % 4], va[b.u]
            first, last = h % HALF == 0, h % HALF == HALF - 1
            if first:
                pe.matmul(o, v[:, 0, h, :], pr[:, 0:S], start=True, stop=False)
            mm = pe.matmul(o[:, P:S], v[:, 1, h, :], pr[:, S:S + P], start=False, stop=False)
            if not first:
                mm = pe.matmul(o, v[:, 0, h, :], pr[:, 0:S], start=False, stop=last)
            mm.then_inc(s["summed"], 1)

        def turn_sums(pe, b):
            pe.wait_ge(s["o_raw_ok"], b.n + 1)
            for n in range(4):
                mm = pe.matmul(p_misc[:, HALF * n:HALF * (n + 1)],
                               o_raw[P // 2:OROWS, n // 2, n % 2 * P:(n % 2 + 1) * P],
                               R.ident[P // 2:OROWS, P // 2:OROWS], start=True, stop=True)
            mm.then_inc(s["sums_turned"], 1)

        def spread(pe, b):
            pe.wait_ge(s["wide_ok"], b.n + 1)
            for n in range(4):
                mm = pe.matmul(p_misc[0:P // 2, n * P:(n + 1) * P], rden_wide[:, n, :], R.ident[:],
                               start=True, stop=True)
            mm.then_inc(s["spread_ok"], 1)

        def project_o(pe, b):
            pe.wait_ge(s["o_t_ok"], b.n + 1)
            for k in range(2):
                for f in range(2):
                    mm = pe.matmul(p_misc[:, k * P:(k + 1) * P], o_t[:, f, k * P:(k + 1) * P], R.w_proj[:, f, :],
                                   start=(f == 0), stop=(f == 1))
            mm.then_inc(s["projected"], 1)

        @block.tensor
        def _(pe):
            b0, b1 = Batch(0, 0), Batch(0, 1)
            project(pe, b0)
            values(pe, b0)
            project(pe, b1)
            for h in range(H):
                score(pe, b0, h)
                if h == HALF:
                    pe.wait_ge(s["qk_ok"], 4)
                    turn_max(pe, b0, 0)
            def step(pe, j, c):
                b, nxt, prev = Batch(j, c), Batch(j, c + 1), Batch(j, c - 1)
                for h in range(H):
                    score_t(pe, b, h)
                    if has(j, c, 1):
                        score(pe, nxt, h)
                    if h >= LAG:
                        weigh(pe, b, h - LAG)
                    elif has(j, c, -1):
                        weigh(pe, prev, H - LAG + h)
                    if h == 0:
                        pe.wait_ge(s["max_read"], 2 * (2 * b.n + 1))
                        turn_max(pe, b, 1)
                    if h == 2 and has(j, c, 2):
                        pe.wait_ge(s["max_read"], 2 * (2 * b.n + 2))
                        project(pe, Batch(j, c + 2))
                    if h == 8 and has(j, c, 1):
                        if has(j, c, 2):
                            pe.wait_ge(s["qk_ok"], 2 * (b.n + 3))
                        else:
                            pe.wait_ge(s["max_read"], 2 * (2 * b.n + 2))
                        turn_max(pe, nxt, 0)
                    if h == 3 and has(j, c, 1):
                        if has(j, c, -2):
                            pe.wait_ge(s["y_ok"], b.n - 1)
                        else:
                            pe.wait_ge(s["v_ok"], b.n + 1)
                        values(pe, nxt)
                    if h == 6 and has(j, c, -1):
                        if has(j, c, 1):
                            pe.wait_ge(s["v_ok"], b.n + 2)
                        else:
                            pe.wait_ge(s["y_ok"], b.n - 1)
                        turn_sums(pe, prev)
                    if h == 9 and has(j, c, -1):
                        spread(pe, prev)
                    if h == 11 and has(j, c, -1):
                        project_o(pe, prev)
            steps(pe, step)
            last = Batch(0, B - 1)
            for h in range(H - LAG, H):
                weigh(pe, last, h)
            pe.wait_ge(s["y_ok"], B - 1)
            turn_sums(pe, last)
            spread(pe, last)
            project_o(pe, last)

        def read_qk(act, b):
            act.wait_ge(s["qk_mm"], b.n + 1)
            wait_if(act, s["part1"], b.n)
            wait_if(act, s["rest_ok"], b.n)
            act.activation(qk[:, 0:S], p_qk[:, 0:S], ACT.Identity, bias=R.bq_neg[:], scale=-SCALE0
                           ).then_inc(s["qk_ok"], 1)
            act.activation(qk[:, S:2 * S], p_qk[:, S:2 * S], ACT.Identity, bias=R.b_qk[:, 1:2]
                           ).then_inc(s["qk_ok"], 1)

        def first_part(act, b):
            act.wait_ge(s["qk_ok"], 2 * (b.n + 1))
            for f in range(2):
                wait_if(act, spilled[b.u][f], 32 * b.half)
            act.activation(part[b.u][:, 0, :], qk[:], ACT.Copy).then_inc(s["part1"], 1)

        def second_part(act, b):
            act.wait_ge(s["rest_ok"], b.n + 1)
            act.activation(part[b.u][:, 1, :], rest[:], ACT.Copy).then_inc(s["part2"], 1)

        def read_max(act, b, f):
            act.wait_ge(s["max_turned"], 2 * b.n + f + 1)
            wait_if(act, s["max_diff"], 2 * b.n + f - 1)
            if not isinstance(b.half, int) or b.half > 0 or b.u > 0:
                pu = 1 - b.u
                prev_half = b.half if b.u else b.half - 1
                act.wait_ge(max_in[pu][f], 48 * (prev_half + 1))
            act.activation(max_f[f][:], p_qk[0:H, 0:P], ACT.Copy).then_inc(s["max_read"], 1)
            act.activation(max_part[f][:, 0, :], p_qk[0:H, 0:P], ACT.Copy).then_inc(s["max_read"], 1)

        def second_max(act, b, f):
            act.wait_ge(s["max_diff"], 2 * b.n + f + 1)
            act.activation(max_part[f][:, 1, :], max_rest[f][:], ACT.Copy).then_inc(s["max_p2"], 1)

        def stack_max(act, b, f):
            act.wait_ge(s["max_p3"], 2 * b.n + f + 1)
            for i in range(3):
                act.dma_start(qst[b.u][KROWS + i:KROWS + i + 1, HALF * f:HALF * (f + 1), :],
                              max_part[f][:, i, :]).then_inc(max_in[b.u][f], 16)

        def exponent(act, b, h):
            n = H * b.n + h
            act.wait_ge(s["arg_ok"], n + 1)
            wait_if(act, s["summed"], n - 3)
            act.activation(prob[h % 4][:], arg[h % 4][:], ACT.Exp, scale=-1.0).then_inc(s["prob_ok"], 1)

        def copy_o(act, b):
            act.wait_ge(s["summed"], H * (b.n + 1))
            wait_if(act, s["o_t_ok"], b.n)
            act.activation(o_raw[:], bank_o(b.u), ACT.Copy).then_inc(s["o_raw_ok"], 1)

        def widen(act, b):
            act.wait_ge(s["rden_ok"], b.n + 1)
            wait_if(act, s["spread_ok"], b.n)
            act.activation(rden_wide[:].rearrange("p n (h d) -> p n h d", d=HD),
                           rden[:].unsqueeze(3).to_broadcast([P, 4, HALF, HD]), ACT.Copy).then_inc(s["wide_ok"], 1)

        @block.scalar
        def _(act):
            b0, b1 = Batch(0, 0), Batch(0, 1)
            for b in (b0, b1):
                read_qk(act, b)
                first_part(act, b)
                second_part(act, b)
            read_max(act, b0, 0)
            second_max(act, b0, 0)
            stack_max(act, b0, 0)

            def step(act, j, c):
                b, nxt, prev = Batch(j, c), Batch(j, c + 1), Batch(j, c - 1)
                for h in range(H):
                    if h == 1:
                        read_max(act, b, 1)
                    if h == 2:
                        second_max(act, b, 1)
                    exponent(act, b, h)
                    if h == 3:
                        stack_max(act, b, 1)
                    if h == 3 and has(j, c, -1):
                        copy_o(act, prev)
                    if h == 3 and has(j, c, 2):
                        read_qk(act, Batch(j, c + 2))
                        first_part(act, Batch(j, c + 2))
                    if h == 7 and has(j, c, -1):
                        widen(act, prev)
                    if h == 5 and has(j, c, 2):
                        second_part(act, Batch(j, c + 2))
                    if h == 9 and has(j, c, 1):
                        read_max(act, nxt, 0)
                    if h == 10 and has(j, c, 1):
                        second_max(act, nxt, 0)
                    if h == 11 and has(j, c, 1):
                        stack_max(act, nxt, 0)
            steps(act, step)
            copy_o(act, Batch(0, B - 1))
            widen(act, Batch(0, B - 1))

        def read_v(dve, b):
            dve.wait_ge(s["v_mm"], b.n + 1)
            wait_if(dve, s["summed"], H * (b.n - 1) if not isinstance(b.n, int) or b.n >= 2 else 0)
            if isinstance(b.n, int) and b.n < 2:
                dve.wait_ge(s["ones_ok"], 2)
            for k in range(2):
                whole = va[b.u][:, k, :, :]
                own = bass.AP(tensor=whole.tensor, offset=whole.offset,
                              ap=[whole.ap[0], [HALF * OROWS, 2], [OROWS + HD, HALF], [1, HD]])
                ins = dve.tensor_tensor(own, p_misc[:, k * P:(k + 1) * P].rearrange("p (f h d) -> p f h d", f=2, d=HD),
                                        R.b_v[:].rearrange("p (f h d) -> p f h d", f=2, d=HD), ALU.add)
            ins.then_inc(s["v_ok"], 1)

        def row_max_waits(dve, b, h):
            n = H * b.n + h
            dve.wait_ge(s["scored"], n + 1)
            if h == 0:
                wait_if(dve, s["max_turned"], 2 * (b.n - 1) if not isinstance(b.n, int) or b.n >= 2 else 0)
            wait_if(dve, s["max_ok"], 2 * n - 2)

        def row_max(dve, b, h):
            for t, cols, at in ((1, slice(0, S), slice(0, S)), (0, slice(S, S + P), slice(P, S))):
                r = (2 * h + 1 - t) % 4
                w = cols.stop - cols.start
                dve.tensor_tensor_reduce(out=sums[r][:, 0:w], in0=p_s[h % 2][:, cols], in1=bias_q[:, h, at],
                                         scale=1.0, scalar=3.0e38, op0=ALU.add, op1=ALU.min,
                                         accum_out=neg_max[b.u][:, h, t:t + 1]).then_inc(s["max_ok"], 1)

        def add_bias(dve, b, h):
            n = H * b.n + h
            dve.wait_ge(s["scored_t"], n + 1)
            wait_if(dve, s["prob_ok"], n - 3)
            dve.tensor_tensor(arg[h % 4][:], p_t[h % 2][:, 0:S + P], bias_k[:, h, :], ALU.add
                              ).then_inc(s["arg_ok"], 1)

        def invert(dve, b):
            dve.wait_ge(s["sums_turned"], b.n + 1)
            wait_if(dve, s["wide_ok"], b.n)
            dve.reciprocal(rden[:].rearrange("p n h -> p (n h)"), p_misc[:, 0:4 * HALF]).then_inc(s["rden_ok"], 1)

        def normalise(dve, b):
            dve.wait_ge(s["spread_ok"], b.n + 1)
            wait_if(dve, s["projected"], b.n)
            dve.tensor_tensor(o_t[:], o_raw[0:P // 2, :, :], p_misc[0:P // 2, :].rearrange("p (f q) -> p f q", f=2),
                              ALU.mult).then_inc(s["o_t_ok"], 1)

        def residual(dve, b):
            dve.wait_ge(s["projected"], b.n + 1)
            dve.wait_ge(s["resid_ok"], b.n + 1)
            wait_if(dve, s["yn_ok"], 2 * b.n)
            dve.tensor_tensor(y[:], p_misc[:, 0:S].rearrange("p (t d) -> p t d", t=2), resid[:], ALU.add
                              ).then_inc(s["y_ok"], 1)
            dve.wait_ge(s["y_ok"], b.n + 1)
            for k in range(2):
                dve.bn_stats(stats[:, k, :], y[:, k, :]).then_inc(s["stats_ok"], 1)

        def aggregate(dve, b):
            for k in range(2):
                dve.bn_aggr(mean_var[:, k, :], stats[:, k, :]).then_inc(s["mv_ok"], 1)

        def centre(dve, b):
            dve.wait_ge(s["rstd_ok"], b.n + 1)
            wait_if(dve, s["yg_ok"], b.n)
            for k in range(2):
                dve.tensor_scalar(yn[:, k, :], y[:, k, :], mean_var[:, k, 0:1], rstd[:, k:k + 1],
                                  ALU.subtract, ALU.mult).then_inc(s["yn_ok"], 1)

        @block.vector
        def _(dve):
            for u in range(2):
                dve.memset(kst[u][64:MROWS, :, :], -1.0).then_inc(s["rows_ok"], 1)
            b0, b1 = Batch(0, 0), Batch(0, 1)
            read_v(dve, b0)
            for h in range(H):
                row_max_waits(dve, b0, h)
                row_max(dve, b0, h)

            def step(dve, j, c):
                b, nxt, prev = Batch(j, c), Batch(j, c + 1), Batch(j, c - 1)
                for h in range(H):
                    if has(j, c, 1):
                        row_max_waits(dve, nxt, h)
                    if h == 13 and has(j, c, -1):
                        dve.wait_ge(s["stats_ok"], 2 * prev.n + 2)
                        wait_if(dve, s["eps_ok"], prev.n)
                    add_bias(dve, b, h)
                    if has(j, c, 1):
                        row_max(dve, nxt, h)
                    if h == 6 and has(j, c, -1):
                        invert(dve, prev)
                    if h == 9 and has(j, c, -1):
                        normalise(dve, prev)
                    if h == 4 and has(j, c, 1):
                        read_v(dve, nxt)
                    if h == 12 and has(j, c, -1):
                        residual(dve, prev)
                    if h == 13 and has(j, c, -1):
                        aggregate(dve, prev)
                    if h == 15 and has(j, c, -1):
                        centre(dve, prev)
            steps(dve, step)
            last = Batch(0, B - 1)
            invert(dve, last)
            normalise(dve, last)
            residual(dve, last)
            dve.wait_ge(s["stats_ok"], 2 * B)
            dve.wait_ge(s["eps_ok"], B - 1)
            aggregate(dve, last)
            centre(dve, last)

        def take_first(pool, b):
            pool.wait_ge(s["part1"], b.n + 1)
            wait_if(pool, s["part3"], b.n)
            wait_if(pool, s["part2"], b.n)
            pool.tensor_tensor(rest[:], qk[:], part[b.u][:, 0, :], ALU.subtract).then_inc(s["rest_ok"], 1)

        def third_part(pool, b):
            pool.wait_ge(s["part2"], b.n + 1)
            pool.tensor_tensor(part[b.u][:, 2, :], rest[:], part[b.u][:, 1, :], ALU.subtract
                               ).then_inc(s["part3"], 1)

        def max_diff(pool, b, f):
            pool.wait_ge(s["max_read"], 2 * (2 * b.n + f + 1))
            wait_if(pool, s["max_p3"], 2 * b.n + f - 1)
            pool.tensor_tensor(max_rest[f][:], max_f[f][:], max_part[f][:, 0, :], ALU.subtract
                               ).then_inc(s["max_diff"], 1)

        def third_max(pool, b, f):
            pool.wait_ge(s["max_p2"], 2 * b.n + f + 1)
            pool.tensor_tensor(max_part[f][:, 2, :], max_rest[f][:], max_part[f][:, 1, :], ALU.subtract
                               ).then_inc(s["max_p3"], 1)

        def prepare_residual(pool, b):
            wait_if(pool, s["y_ok"], b.n)
            pool.tensor_tensor(resid[:], R.xn[:, bass.ds(2 * b.n, 2), :],
                               R.b_proj[:].unsqueeze(1).to_broadcast([P, 2, P]), ALU.add).then_inc(s["resid_ok"], 1)

        def inverse_std(pool, b):
            pool.wait_ge(s["mv_ok"], 2 * (b.n + 1))
            pool.tensor_tensor(var_eps[:], mean_var[:, :, 1], R.eps[:].to_broadcast([P, 2]), ALU.add).then_inc(s["eps_ok"], 1)
            pool.wait_ge(s["eps_ok"], b.n + 1)
            wait_if(pool, s["yn_ok"], 2 * b.n)
            pool.tensor_tensor(rstd[:], var_eps[:], R.neg_half[:].to_broadcast([P, 2]), ALU.pow).then_inc(s["rstd_ok"], 1)

        def affine(pool, b):
            pool.wait_ge(s["yn_ok"], 2 * (b.n + 1))
            wait_if(pool, s["s_ok"], b.n)
            pool.tensor_tensor(yg[:], yn[:], R.ln_g[:].unsqueeze(1).to_broadcast([P, 2, P]), ALU.mult
                               ).then_inc(s["yg_ok"], 1)
            pool.wait_ge(s["yg_ok"], b.n + 1)
            pool.tensor_tensor(R.s[:, bass.ds(2 * b.n, 2), :], yg[:], R.ln_b[:].unsqueeze(1).to_broadcast([P, 2, P]),
                               ALU.add).then_inc(s["s_ok"], 1)

        @block.gpsimd
        def _(pool):
            for u in range(2):
                pool.memset(va[u][:], 0.0).then_inc(s["zeros_ok"], 1)
            for u in range(2):
                by_half = va[u][:].rearrange("p k (f h) c -> p (k f) (h c)", f=2)
                pool.wait_ge(s["zeros_ok"], u + 1)
                pool.memset(by_half[:, :, P // 2:HALF * OROWS:OROWS + 1], 1.0).then_inc(s["ones_ok"], 1)
            b0, b1 = Batch(0, 0), Batch(0, 1)
            for b in (b0, b1):
                take_first(pool, b)
                third_part(pool, b)
            max_diff(pool, b0, 0)
            third_max(pool, b0, 0)

            def step(pool, j, c):
                b, nxt, prev = Batch(j, c), Batch(j, c + 1), Batch(j, c - 1)

                def scatter_some(begin, end):
                    if isinstance(j, int):
                        first = NT // 4 * (c if c < 2 else c - B + 4)
                        scatter(pool, R, D, 0, range(first + begin, first + end))

                max_diff(pool, b, 1)
                third_max(pool, b, 1)
                scatter_some(0, 2)
                if has(j, c, 2):
                    take_first(pool, Batch(j, c + 2))
                    third_part(pool, Batch(j, c + 2))
                scatter_some(2, 4)
                if has(j, c, -1):
                    prepare_residual(pool, prev)
                if has(j, c, 1):
                    max_diff(pool, nxt, 0)
                    third_max(pool, nxt, 0)
                scatter_some(4, NT // 4)
                if has(j, c, -1):
                    inverse_std(pool, prev)
                    affine(pool, prev)
            steps(pool, step)
            last = Batch(0, B - 1)
            prepare_residual(pool, last)
            inverse_std(pool, last)
            affine(pool, last)


def attention1(nc, R, D, f):
    tag = "a1_"
    with ExitStack() as ctx:
        sem = Sems(nc, ctx)
        ctx.callback(sem.done)

        def sb(name, shape, dt=F32):
            return ctx.enter_context(nc.sbuf_tensor(tag + name, shape, dt))

        def ps(name):
            return ctx.enter_context(nc.psum_tensor(tag + name, [P, 512], F32))

        cos_sin = sb("cos_sin", [P, 2, 2 * S])
        decay = sb("decay", [P, 2, S])
        xs = [sb(f"xs{u}", [P, S]) for u in range(2)]
        along = sb("along", [P, 2 * S])
        across = sb("across", [P, 2 * S])
        qk = [sb(f"qk{u}", [P, 2 * S]) for u in range(2)]
        v = [sb(f"v{u}", [P, 2, P]) for u in range(2)]
        neg_max = sb("neg_max", [P, 2])
        total, rden = sb("total", [P, 2]), [sb(f"rden{u}", [P, 2]) for u in range(2)]
        prob, decayed = sb("prob", [P, 2, S]), sb("decayed", [P, 2, S])
        prob_t = [sb(f"prob_t{u}", [P, 2, S]) for u in range(2)]
        p_a, p_b, p_v = ps("p_a"), ps("p_b"), ps("p_v")
        p_s = [ps(f"p_s{u}") for u in range(2)]
        p_p = [ps(f"p_p{u}") for u in range(2)]
        p_o = ps("p_o")
        s = {n: sem(tag + n) for n in (
            "tables_in", "qk_mm", "along_ok", "across_ok", "qk_ok", "v_mm", "v_ok", "scored", "max_ok", "prob_ok",
            "decayed_ok", "turned", "turned_ok", "summed", "rden_ok", "s_ok", "shared_in", "first_ok")}
        xs_in = sem.pair(tag + "xs_in")
        block = ctx.enter_context(nc.Block())

        def steps(eng, do):
            do(eng, 0, 0)
            do(eng, 0, 1)
            with eng.Fori(1, B // 2 - 1) as j:
                do(eng, j, 0)
                do(eng, j, 1)
            do(eng, 0, B - 2)
            do(eng, 0, B - 1)

        def has(j, c, ahead):
            return not isinstance(j, int) or 0 <= c + ahead < B

        @block.sync
        def _(sp):
            sem.clear_old(sp)
            sp.dma_start(cos_sin[:], D["cos_sin"]).then_inc(s["tables_in"], 16)
            sp.dma_start(decay[:], D["decay"].rearrange("(t p) k -> p t k", p=P)).then_inc(s["tables_in"], 16)
            sp.dma_start(f.shared[:], D["slots_out"][1][0:B * S, :].rearrange("(t p) d -> p t d", p=P)
                         ).then_inc(s["shared_in"], 16)

            def step(sp, j, c):
                b = Batch(j, c)
                wait_if(sp, s["v_mm"], b.n - 1)
                sp.dma_start(xs[b.u][:], R.xt[:, bass.ds(S * b.n, S)]).then_inc(xs_in[b.u], 16)
            steps(sp, step)
            sp.wait_ge(s["shared_in"], 16)

        def project(pe, b):
            wait_if(pe, s["along_ok"], b.n)
            wait_if(pe, s["across_ok"], b.n)
            for bank, at in ((p_a, 0), (p_b, 2)):
                for k in range(2):
                    mm = pe.matmul(bank[:, k * S:(k + 1) * S], R.w_x1[:, (at + k) * P:(at + k + 1) * P],
                                   R.xt[:, bass.ds(S * b.n, S)], start=True, stop=True)
            mm.then_inc(s["qk_mm"], 1)

        def values(pe, b):
            pe.wait_ge(xs_in[b.u], 16 * (b.half + 1))
            wait_if(pe, s["v_ok"], b.n)
            for k in range(2):
                mm = pe.matmul(p_v[:, k * P:(k + 1) * P], xs[b.u][:, k * P:(k + 1) * P], R.w_x1[:, 4 * P:5 * P],
                               start=True, stop=True)
            mm.then_inc(s["v_mm"], 1)

        def score(pe, b):
            pe.wait_ge(s["qk_ok"], b.n + 1)
            wait_if(pe, s["prob_ok"], 2 * (b.n - 1))
            for k in range(2):
                mm = pe.matmul(p_s[b.u][:, k * S:(k + 1) * S], qk[b.u][:, k * P:(k + 1) * P], qk[b.u][:, S:2 * S],
                               start=True, stop=True)
            mm.then_inc(s["scored"], 1)

        def turn(pe, b):
            pe.wait_ge(s["decayed_ok"], b.n + 1)
            wait_if(pe, s["turned_ok"], b.n - 1)
            for k in range(2):
                for q in range(2):
                    mm = pe.transpose(p_p[b.u][:, k * S + q * P:k * S + (q + 1) * P],
                                      decayed[:, q, k * P:(k + 1) * P], R.ident[:])
            mm.then_inc(s["turned"], 1)

        def weigh(pe, b):
            pe.wait_ge(s["turned_ok"], b.n + 1)
            pe.wait_ge(s["v_ok"], b.n + 1)
            wait_if(pe, s["s_ok"], 2 * b.n)
            for q in range(2):
                for k in range(2):
                    mm = pe.matmul(p_o[:, q * P:(q + 1) * P], prob_t[b.u][:, k, q * P:(q + 1) * P], v[b.u][:, k, :],
                                   start=(k == 0), stop=(k == 1))
            mm.then_inc(s["summed"], 1)

        @block.tensor
        def _(pe):
            project(pe, Batch(0, 0))
            values(pe, Batch(0, 0))
            project(pe, Batch(0, 1))
            score(pe, Batch(0, 0))

            def step(pe, j, c):
                if has(j, c, 2):
                    project(pe, Batch(j, c + 2))
                if has(j, c, -1):
                    turn(pe, Batch(j, c - 1))
                if has(j, c, 1):
                    score(pe, Batch(j, c + 1))
                    values(pe, Batch(j, c + 1))
                if has(j, c, -1):
                    weigh(pe, Batch(j, c - 1))
            steps(pe, step)
            turn(pe, Batch(0, B - 1))
            weigh(pe, Batch(0, B - 1))

        @block.vector
        def _(dve):
            def rotate(dve, b):
                dve.wait_ge(s["qk_mm"], b.n + 1)
                wait_if(dve, s["qk_ok"], b.n)
                dve.tensor_tensor(along[:], p_a[:], cos_sin[:, 0, :], ALU.mult).then_inc(s["along_ok"], 1)
                dve.tensor_tensor(across[:], p_b[:], cos_sin[:, 1, :], ALU.mult).then_inc(s["across_ok"], 1)

            def add_across(dve, b):
                dve.wait_ge(s["across_ok"], b.n + 1)
                wait_if(dve, s["scored"], b.n - 1)
                dve.tensor_tensor(qk[b.u][:], along[:], across[:], ALU.add).then_inc(s["qk_ok"], 1)

            def row_max(dve, b):
                dve.wait_ge(s["scored"], b.n + 1)
                wait_if(dve, s["prob_ok"], 2 * b.n)
                dve.tensor_reduce(neg_max[:], p_s[b.u][:].rearrange("p (t k) -> p t k", t=2), X, ALU.max,
                                  negate=True).then_inc(s["max_ok"], 1)

            def decay_it(dve, b):
                dve.wait_ge(s["prob_ok"], 2 * (b.n + 1))
                wait_if(dve, s["turned"], b.n)
                dve.tensor_tensor(decayed[:], prob[:], decay[:], ALU.mult).then_inc(s["decayed_ok"], 1)
                wait_if(dve, s["s_ok"], 2 * (b.n - 1))
                dve.reciprocal(rden[b.u][:], total[:]).then_inc(s["rden_ok"], 1)

            dve.wait_ge(s["tables_in"], 32)
            def mix(dve, b):
                tiles = [(k, 2 * b.n - 4 + k) for k in range(2)]
                for k, t in tiles:
                    dve.wait_ge(R.gathered[2 * b.u + k], 32 * b.half)
                    dve.scalar_tensor_tensor(out=f.shared[:, t, :], in0=f.top[0][:, t, :],
                                             scalar=R.weight[0][:, bass.ds(t, 1)], in1=f.shared[:, t, :],
                                             op0=ALU.mult, op1=ALU.add).then_inc(s["first_ok"], 1)
                for k, t in tiles:
                    dve.wait_ge(s["first_ok"], 2 * b.n - 3 + k)
                    dve.scalar_tensor_tensor(out=f.top[0][:, t, :], in0=f.top[1][:, t, :],
                                             scalar=R.weight[1][:, bass.ds(t, 1)], in1=f.shared[:, t, :],
                                             op0=ALU.mult, op1=ALU.add)

            for b in (Batch(0, 0), Batch(0, 1)):
                rotate(dve, b)
                add_across(dve, b)
            row_max(dve, Batch(0, 0))

            def step(dve, j, c):
                if has(j, c, 2):
                    rotate(dve, Batch(j, c + 2))
                decay_it(dve, Batch(j, c))
                if has(j, c, 2):
                    add_across(dve, Batch(j, c + 2))
                if has(j, c, 1):
                    row_max(dve, Batch(j, c + 1))
                if isinstance(j, int) and c == 1:
                    dve.wait_ge(s["shared_in"], 16)
                if has(j, c, -2):
                    mix(dve, Batch(j, c))
            steps(dve, step)
            mix(dve, Batch(0, B))
            mix(dve, Batch(0, B + 1))

        @block.gpsimd
        def _(pool):
            ring = len(R.gathered)
            for t in range(NT):
                if t >= ring:
                    pool.wait_ge(R.gathered[t % ring], 32 * (t // ring))
                for n in range(2):
                    pool.indirect_dma_start(f.top[n][:, t, :], None, D["slots_out"][1],
                                            bass.IndirectOffsetOnAxis(ap=R.pos[n][:, t:t + 1], axis=0)
                                            ).then_inc(R.gathered[t % ring], 16)

        @block.scalar
        def _(act):
            def read_v(act, b):
                act.wait_ge(s["v_mm"], b.n + 1)
                wait_if(act, s["summed"], b.n - 1)
                act.activation(v[b.u][:].rearrange("p t d -> p (t d)"), p_v[:, 0:S], ACT.Copy).then_inc(s["v_ok"], 1)

            def exponent(act, b):
                act.wait_ge(s["max_ok"], b.n + 1)
                wait_if(act, s["decayed_ok"], b.n)
                wait_if(act, s["rden_ok"], b.n)
                for k in range(2):
                    act.activation(prob[:, k, :], p_s[b.u][:, k * S:(k + 1) * S], ACT.Exp, bias=neg_max[:, k:k + 1],
                                   accum_out=total[:, k:k + 1]).then_inc(s["prob_ok"], 1)

            def read_turned(act, b):
                act.wait_ge(s["turned"], b.n + 1)
                wait_if(act, s["summed"], b.n - 1)
                act.activation(prob_t[b.u][:].rearrange("p t k -> p (t k)"), p_p[b.u][:], ACT.Copy
                               ).then_inc(s["turned_ok"], 1)

            def out(act, b):
                act.wait_ge(s["summed"], b.n + 1)
                act.wait_ge(s["rden_ok"], b.n + 1)
                for k in range(2):
                    act.activation(R.s[:, 2 * b.n + k, :], p_o[:, k * P:(k + 1) * P], ACT.Copy,
                                   scale=rden[b.u][:, k:k + 1]).then_inc(s["s_ok"], 1)

            read_v(act, Batch(0, 0))

            def step(act, j, c):
                b = Batch(j, c)
                exponent(act, b)
                if has(j, c, -1):
                    read_turned(act, Batch(j, c - 1))
                if has(j, c, 1):
                    read_v(act, Batch(j, c + 1))
                if has(j, c, -1):
                    out(act, Batch(j, c - 1))
            steps(act, step)
            read_turned(act, Batch(0, B - 1))
            out(act, Batch(0, B - 1))


class Resident:

    def __init__(self, nc, ctx):
        def sem(name):
            return ctx.enter_context(nc.semaphore("k_" + name))

        self.scattered, self.zeroed = sem("scattered"), sem("zeroed")
        self.gathered = [sem(f"gathered{r}") for r in range(4)]
        self.arrived = [sem(f"arrived{r}") for r in range(8)]

        def sb(name, shape, dt=F32):
            return ctx.enter_context(nc.sbuf_tensor("k_" + name, shape, dt))

        self.x, self.xn, self.s = sb("x", [P, NT, P]), sb("xn", [P, NT, P]), sb("s", [P, NT, P])
        self.xt = sb("xt", [P, B * S])
        self.gate_w = [sb(f"gate_w{n}", [P, E]) for n in range(2)]
        self.gb, self.rb = sb("gb", [P, E]), sb("rb", [P, E])
        self.w_qkv, self.b_qk, self.b_v = sb("w_qkv", [P, 3 * P]), sb("b_qk", [P, 2]), sb("b_v", [P, P])
        self.bq_neg = sb("bq_neg", [P, 1])
        self.w_proj, self.b_proj = sb("w_proj", [P // 2, 2, P]), sb("b_proj", [P, P])
        self.ln_g, self.ln_b = sb("ln_g", [P, P]), sb("ln_b", [P, P])
        self.w_x1 = sb("w_x1", [P, 5 * P])
        self.ident, self.reverse = sb("ident", [P, P]), sb("reverse", [P, P])
        self.ones_bf, self.upper_bf = sb("ones_bf", [P, P], BF16), sb("upper_bf", [P, P], BF16)
        self.neg_half, self.eps, self.zero32 = sb("neg_half", [P, 1]), sb("eps", [P, 1]), sb("zero32", [P, NT])
        self.zeros = sb("zeros", [P, P])
        self.mean_var, self.var_eps, self.rstd = sb("mean_var", [P, NT, 2]), sb("var_eps", [P, NT]), sb("rstd", [P, NT])
        self.expert_m8, self.tile_start = sb("expert_m8", [P, E]), sb("tile_start", [P, B * S // SLOTS])
        self.tile_no = sb("tile_no", [P, ROUTED1])
        self.logits = sb("logits", [P, NT, E])
        self.weight = [sb(f"weight{n}", [P, NT]) for n in range(2)]
        self.pos = [sb(f"pos{n}", [P, NT], I32) for n in range(2)]
        self.tile_expert = sb("tile_expert", [1, TILES], I32)


def build(nc, D):
    D["slots_in"] = nc.dram_tensor("slots_in", [TILES * SLOTS, P], F32, kind="Internal").ap()
    D["slots_out"] = [nc.dram_tensor(f"slots_out{n}", [tiles * SLOTS, P], F32, kind="Internal").ap()
                      for n, tiles in enumerate((ROUTED0, TILES))]
    D["parts"] = nc.dram_tensor("parts", [2 * PARTS * 2 * P, S], BF16, kind="Internal").ap()
    Sems.before = None
    with ExitStack() as ctx:
        R = Resident(nc, ctx)
        with ExitStack() as first:
            bias = Bias(nc, first)
            build_constants(nc, R, D, bias)
            layer_norm_gate(nc, R, D, bias)
            route(nc, R, D, 0, bias)
            attention0(nc, R, D, bias)
        experts(nc, R, D, 0)
        combine0(nc, R, D)
        route(nc, R, D, 1, None)
        experts(nc, R, D, 1)
        f = Gathered(nc, ctx)
        attention1(nc, R, D, f)
        combine1(nc, R, D, f)


def xpos_tables():
    f = np.float32
    scale_vec = (np.arange(0, P, 2, dtype=f) + f(0.4 * P)) / f(1.4 * P)
    scale = scale_vec[None, :] ** (np.arange(S, dtype=f) / f(512.0))[:, None]
    inv_freq = f(1.0) / f(10000.0) ** (np.arange(P // 2, dtype=f) / f(P // 2))
    angle = np.arange(S, dtype=f)[:, None] * inv_freq[None, :]
    sign = np.where(np.arange(P) % 2 == 0, f(-1), f(1))
    out = np.zeros((P, 2, 2 * S), f)
    for k, sc in enumerate((scale, f(1.0) / scale)):
        out[:, 0, k * S:(k + 1) * S] = np.repeat(np.cos(angle) * sc, 2, axis=-1).T
        out[:, 1, k * S:(k + 1) * S] = (np.repeat(np.sin(angle) * sc, 2, axis=-1) * sign).T
    return out


def kernel(**inputs):
    import concourse.bacc as _bacc
    from concourse.bass_utils import run_bass_kernel_spmd as _run

    a = {k: np.asarray(v) for k, v in inputs.items()}
    by_part = a["L0_attn_W_w"].reshape(3, 2, HALF, HD, P)
    w_q, w_k = (by_part[n].transpose(3, 0, 2, 1).reshape(P, P) for n in range(2))
    w_v = a["L0_attn_W_w"][2 * P:].T
    b_part = a["L0_attn_W_b"].reshape(3, 2, HALF, HD)
    swap = np.arange(P) ^ 1
    wq1, wk1, wv1 = a["L1_attn_W_Q"], a["L1_attn_W_K"], a["L1_attn_W_V"]
    rpb_t = a["L0_attn_rpb"].T
    step = np.arange(S)

    def chunks(w):
        return w.reshape(w.shape[0], -1, P, P).transpose(0, 2, 1, 3).reshape(w.shape[0], P, -1)

    def with_shared(n):
        return np.concatenate([a["L1_ffn_W" + n], a["L1_ffn_Ws" + n][None]])

    arrays = {
        "x": a["L0_attn_x"].reshape(B * S, P),
        "gate_W": a["L0_ffn_gate_W"], "gate_b": a["L0_ffn_gate_b"], "Wr": a["L1_ffn_Wr"], "rb": a["L1_ffn_rb"],
        "w_qkv": np.concatenate([w_q, w_k, w_v], axis=1),
        "b_qk": np.stack([b_part[n].transpose(0, 2, 1).reshape(P) for n in range(2)], axis=1),
        "b_v": a["L0_attn_W_b"][2 * P:], "w_proj": a["L0_attn_proj_w"].T, "b_proj": a["L0_attn_proj_b"],
        "ln_g": a["L0_attn_ln_g"], "ln_b": a["L0_attn_ln_b"],
        "rpbT": rpb_t, "rpbR": rpb_t[:, ::-1],
        "b2": a["L0_ffn_b2"],
        "W_0": np.concatenate([a["L0_ffn_W1"], chunks(a["L0_ffn_W2"]),
                               a["L0_ffn_b1"].reshape(E, F0 // P, P).transpose(0, 2, 1)], axis=2),
        "W_1": np.concatenate([with_shared("1"), with_shared("3"), chunks(with_shared("2"))], axis=2),
        "w_x1": np.concatenate([wq1, wk1, wq1[:, swap], wk1[:, swap], wv1], axis=1),
        "cos_sin": xpos_tables(),
        "decay": np.float32(0.9) ** np.abs(step[:, None] - step[None, :]).astype(np.float32),
    }
    arrays = {k: np.ascontiguousarray(v) for k, v in arrays.items()}
    nc = _bacc.Bacc("TRN2", target_bir_lowering=False, num_devices=1)
    D = {k: nc.dram_tensor("in_" + k, v.shape, mybir.dt.from_np(v.dtype), kind="ExternalInput").ap()
         for k, v in arrays.items()}
    D["out"] = nc.dram_tensor("out_0", (B * S, P), F32, kind="ExternalOutput").ap()
    D["W"] = [D["W_0"], D["W_1"]]
    build(nc, D)
    r = _run(nc, [{"in_" + k: v for k, v in arrays.items()}], core_ids=[0])
    return r.results[0]["out_0"].reshape(B, S, P)
```
